# Optimizing a Trainium2 kernel written in Bass

```python
import numpy as np
import jax
import jax.numpy as jnp

def _softmax(x, axis=-1):
    return jax.nn.softmax(x, axis=axis)
def _gelu(x):
    return jax.nn.gelu(x, approximate=True)
def _silu(x):
    return jax.nn.silu(x)
def _sigmoid(x):
    return jax.nn.sigmoid(x)
def _layernorm(x, axis=-1, eps=1e-5):
    m = jnp.mean(x, axis=axis, keepdims=True)
    v = jnp.var(x, axis=axis, keepdims=True)
    return (x - m) / jnp.sqrt(v + eps)
def _scatter_add(tgt, idx, src, axis=0):
    return tgt.at[idx].add(src)
def _segment_sum(src, seg, n):
    return jax.ops.segment_sum(src, seg, n)

kernel_name = 'mk_metaformer_d2_conv_nhwc384_d96c4e'

def setup_inputs(seed: int = 0):
    np.random.seed(seed)
    _w = jnp.asarray
    def _rec_inputs():
        import jax
        import jax.numpy as jnp
        _gk = jax.random.key(seed)
        x = -0.0008768 + 1.001 * jax.random.normal(jax.random.fold_in(_gk, 1), (2, 48, 48, 384), jnp.float32)
        return x
    x = _rec_inputs()
    def _L0_conv_setup():
        import jax, jax.numpy as jnp
        import numpy as np
        from jax import lax
        B_SZ, H_SZ, W_SZ = (2, 48, 48)
        D_MODEL = 192
        SSM_RATIO = 2.0
        D_PROJ = int(SSM_RATIO * D_MODEL)
        C_INNER = 2 * D_PROJ
        K_GRP = 4
        D_IN = C_INNER // K_GRP
        N_STATE = 16
        R_RANK = 12

        def _ss2d(x, in_proj_w, conv_w, conv_b, x_proj_weight, dt_projs_weight, dt_projs_bias, A_logs, Ds, out_norm_w, out_norm_b, out_proj_w):
            B, H, W, _ = x.shape
            C = in_proj_w.shape[0]
            K = x_proj_weight.shape[0]
            d = C // K
            N = A_logs.shape[1]
            R = dt_projs_weight.shape[2]
            L = H * W
            xz = jnp.einsum('bhwc,oc->bhwo', x, in_proj_w)
            xc = xz.transpose(0, 3, 1, 2)
            xc = lax.conv_general_dilated(xc, conv_w, (1, 1), 'SAME', feature_group_count=C)
            xc = xc + conv_b[None, :, None, None]
            xc = xc * jax.nn.sigmoid(xc)
            ch = xc.reshape(B, K, d, H, W)
            f0 = ch[:, 0].reshape(B, d, L)
            f1 = ch[:, 1].transpose(0, 1, 3, 2).reshape(B, d, L)
            f2 = jnp.flip(ch[:, 2].reshape(B, d, L), -1)
            f3 = jnp.flip(ch[:, 3].transpose(0, 1, 3, 2).reshape(B, d, L), -1)
            xs = jnp.stack([f0, f1, f2, f3], axis=1)
            x_dbl = jnp.einsum('bkdl,kcd->bkcl', xs, x_proj_weight)
            dts, Bs, Cs = jnp.split(x_dbl, [R, R + N], axis=2)
            dts = jnp.einsum('bkrl,kdr->bkdl', dts, dt_projs_weight) + dt_projs_bias[None, :, :, None]
            u = xs.astype(jnp.float32)
            dts = jax.nn.softplus(dts.astype(jnp.float32))
            Bs = Bs.astype(jnp.float32)
            Cs = Cs.astype(jnp.float32)
            A = -jnp.exp(A_logs.astype(jnp.float32)).reshape(K, d, N)

            def step(h, inp):
                u_t, dt_t, B_t, C_t = inp
                h = h * jnp.exp(dt_t[..., None] * A) + (dt_t * u_t)[..., None] * B_t[:, :, None, :]
                y_t = jnp.einsum('bkdn,bkn->bkd', h, C_t)
                return (h, y_t)
            inps = (u.transpose(3, 0, 1, 2), dts.transpose(3, 0, 1, 2), Bs.transpose(3, 0, 1, 2), Cs.transpose(3, 0, 1, 2))
            h0 = jnp.zeros((B, K, d, N), jnp.float32)
            _, ys = lax.scan(step, h0, inps)
            ys = ys.transpose(1, 2, 3, 0)
            ys = ys + Ds.astype(jnp.float32).reshape(K, d)[None, :, :, None] * u
            y0 = ys[:, 0]
            y1 = ys[:, 1].reshape(B, d, W, H).transpose(0, 1, 3, 2).reshape(B, d, L)
            y2 = jnp.flip(ys[:, 2], -1)
            y3 = jnp.flip(ys[:, 3], -1).reshape(B, d, W, H).transpose(0, 1, 3, 2).reshape(B, d, L)
            y = jnp.concatenate([y0, y1, y2, y3], axis=1).reshape(B, C, H, W).transpose(0, 2, 3, 1)
            mu = jnp.mean(y, -1, keepdims=True)
            var = jnp.mean(jnp.square(y - mu), -1, keepdims=True)
            y = (y - mu) * lax.rsqrt(var + 1e-05) * out_norm_w + out_norm_b
            out = jnp.einsum('bhwc,oc->bhwo', y.astype(x.dtype), out_proj_w)
            return out
        key = jax.random.key(seed)
        ks = jax.random.split(key, 12)
        x = jax.random.normal(ks[0], (B_SZ, H_SZ, W_SZ, 2 * D_MODEL), jnp.float32)
        in_proj_w = jax.random.normal(ks[1], (C_INNER, 2 * D_MODEL), jnp.float32) * 0.02
        conv_w = jax.random.normal(ks[2], (C_INNER, 1, 3, 3), jnp.float32) * 0.1
        conv_b = jnp.zeros((C_INNER,), jnp.float32)
        x_proj_weight = jax.random.normal(ks[3], (K_GRP, R_RANK + 2 * N_STATE, D_IN), jnp.float32) * 0.05
        dt_projs_weight = jax.random.normal(ks[4], (K_GRP, D_IN, R_RANK), jnp.float32) * R_RANK ** (-0.5)
        dt = jnp.exp(jax.random.uniform(ks[5], (K_GRP, D_IN)) * (np.log(0.1) - np.log(0.001)) + np.log(0.001))
        dt = jnp.clip(dt, 0.0001, None)
        dt_projs_bias = dt + jnp.log(-jnp.expm1(-dt))
        A_logs = jnp.log(jnp.tile(jnp.arange(1, N_STATE + 1, dtype=jnp.float32)[None, :], (K_GRP * D_IN, 1)))
        Ds = jnp.ones((K_GRP * D_IN,), jnp.float32)
        out_norm_w = jnp.ones((C_INNER,), jnp.float32)
        out_norm_b = jnp.zeros((C_INNER,), jnp.float32)
        out_proj_w = jax.random.normal(ks[6], (2 * D_MODEL, C_INNER), jnp.float32) * 0.02
        return dict(x=x, in_proj_w=in_proj_w, conv_w=conv_w, conv_b=conv_b, x_proj_weight=x_proj_weight, dt_projs_weight=dt_projs_weight, dt_projs_bias=dt_projs_bias, A_logs=A_logs, Ds=Ds, out_norm_w=out_norm_w, out_norm_b=out_norm_b, out_proj_w=out_proj_w)
    _L0_conv_all = _L0_conv_setup()
    _L0_conv_in = {k: v for k, v in _L0_conv_all.items() if k in ('in_proj_w', 'conv_w', 'conv_b', 'x_proj_weight', 'dt_projs_weight', 'dt_projs_bias', 'A_logs', 'Ds', 'out_norm_w', 'out_norm_b', 'out_proj_w', )}
    del _L0_conv_all

    def _L0_ffn_setup():
        import jax, jax.numpy as jnp
        import numpy as np
        NUM_EXPERTS = 4
        TOP_K = 2
        DIM = 384
        HID = 4 * DIM
        key = jax.random.key(seed)
        ks = jax.random.split(key, 5)
        B, S = (16, 2048)
        scale_in = 1.0 / np.sqrt(DIM)
        scale_hid = 1.0 / np.sqrt(HID)
        return {'x': jax.random.normal(ks[0], (B, S, DIM), dtype=jnp.float32), 'gate_w': jax.random.normal(ks[1], (DIM, NUM_EXPERTS), dtype=jnp.float32) * scale_in, 'gate_b': jnp.zeros((NUM_EXPERTS,), dtype=jnp.float32), 'w1': jax.random.normal(ks[2], (NUM_EXPERTS, DIM, HID), dtype=jnp.float32) * scale_in, 'b1': jnp.zeros((NUM_EXPERTS, HID), dtype=jnp.float32), 'w2': jax.random.normal(ks[3], (NUM_EXPERTS, HID, DIM), dtype=jnp.float32) * scale_hid, 'b2': jnp.zeros((NUM_EXPERTS, DIM), dtype=jnp.float32)}
    _L0_ffn_all = _L0_ffn_setup()
    _L0_ffn_in = {k: v for k, v in _L0_ffn_all.items() if k in ('gate_w', 'gate_b', 'w1', 'b1', 'w2', 'b2', )}
    del _L0_ffn_all

    def _L1_conv_setup():
        import jax, jax.numpy as jnp
        import numpy as np
        D_MODEL = 384
        D_STATE = 16
        D_CONV = 3
        EXPAND = 2
        D_INNER = EXPAND * D_MODEL
        HEADDIM = 64
        NHEADS = D_INNER // HEADDIM
        NGROUPS = 1
        CHUNK = 64
        D_IN_PROJ = 2 * D_INNER + 2 * NGROUPS * D_STATE + NHEADS
        CONV_DIM = D_INNER + 2 * NGROUPS * D_STATE

        def segsum(x):
            T = x.shape[-1]
            xe = jnp.broadcast_to(x[..., None], x.shape + (T,))
            mask_strict = jnp.tril(jnp.ones((T, T), bool), -1)
            xe = jnp.where(mask_strict, xe, 0.0)
            x_segsum = jnp.cumsum(xe, axis=-2)
            mask_incl = jnp.tril(jnp.ones((T, T), bool), 0)
            return jnp.where(mask_incl, x_segsum, -jnp.inf)

        def ssd_minimal_discrete(X, A, Bm, Cm, block_len):
            b, seqlen, h, p = X.shape
            c = seqlen // block_len
            X = X.reshape(b, c, block_len, h, p)
            Bm = Bm.reshape(b, c, block_len, h, -1)
            Cm = Cm.reshape(b, c, block_len, h, -1)
            A = A.reshape(b, c, block_len, h).transpose(0, 3, 1, 2)
            A_cumsum = jnp.cumsum(A, axis=-1)
            L = jnp.exp(segsum(A))
            Y_diag = jnp.einsum('bclhn,bcshn,bhcls,bcshp->bclhp', Cm, Bm, L, X)
            decay_states = jnp.exp(A_cumsum[:, :, :, -1:] - A_cumsum)
            states = jnp.einsum('bclhn,bhcl,bclhp->bchpn', Bm, decay_states, X)
            init = jnp.zeros_like(states[:, :1])
            states = jnp.concatenate([init, states], axis=1)
            A_last = jnp.pad(A_cumsum[:, :, :, -1], ((0, 0), (0, 0), (1, 0)))
            decay_chunk = jnp.exp(segsum(A_last))
            new_states = jnp.einsum('bhzc,bchpn->bzhpn', decay_chunk, states)
            states, final_state = (new_states[:, :-1], new_states[:, -1])
            state_decay_out = jnp.exp(A_cumsum)
            Y_off = jnp.einsum('bclhn,bchpn,bhcl->bclhp', Cm, states, state_decay_out)
            Y = (Y_diag + Y_off).reshape(b, seqlen, h, p)
            return (Y, final_state)
        key = jax.random.key(seed)
        ks = jax.random.split(key, 10)
        x = jax.random.normal(ks[0], (8, 64, 64, D_MODEL), jnp.float32)
        W_in = jax.random.normal(ks[1], (D_MODEL, D_IN_PROJ), jnp.float32) * 0.02
        W_conv = jax.random.normal(ks[2], (D_CONV, D_CONV, 1, CONV_DIM), jnp.float32) * 0.1
        b_conv = jax.random.normal(ks[3], (CONV_DIM,), jnp.float32) * 0.01
        dt = jnp.exp(jax.random.uniform(ks[4], (NHEADS,)) * (np.log(0.1) - np.log(0.001)) + np.log(0.001))
        dt = jnp.clip(dt, 0.0001, None)
        dt_bias = dt + jnp.log(-jnp.expm1(-dt))
        A_log = jnp.log(jax.random.uniform(ks[5], (NHEADS,), minval=1.0, maxval=16.0))
        D_param = jnp.ones((NHEADS,), jnp.float32)
        gamma = jnp.ones((D_INNER,), jnp.float32)
        beta = jnp.zeros((D_INNER,), jnp.float32)
        W_out = jax.random.normal(ks[6], (D_INNER, D_MODEL), jnp.float32) * 0.02
        return {'x': x, 'W_in': W_in, 'W_conv': W_conv, 'b_conv': b_conv, 'dt_bias': dt_bias, 'A_log': A_log, 'D_param': D_param, 'gamma': gamma, 'beta': beta, 'W_out': W_out}
    _L1_conv_all = _L1_conv_setup()
    _L1_conv_in = {k: v for k, v in _L1_conv_all.items() if k in ('W_in', 'W_conv', 'b_conv', 'dt_bias', 'A_log', 'D_param', 'gamma', 'beta', 'W_out', )}
    del _L1_conv_all

    def _L1_ffn_setup():
        import jax, jax.numpy as jnp
        import numpy as np
        D_MODEL = 384
        D_FF = 1536
        key = jax.random.key(seed)
        k_x, k1, k2, k3, k4 = jax.random.split(key, 5)
        std = 0.02
        return {'x': jax.random.normal(k_x, (16, 2048, D_MODEL), dtype=jnp.float32), 'c_fc_1': std * jax.random.normal(k1, (1536, 32), dtype=jnp.float32), 'c_fc_2': std * jax.random.normal(k2, (1, 12), dtype=jnp.float32), 'c_proj_1': std * jax.random.normal(k3, (32, 1536), dtype=jnp.float32), 'c_proj_2': std * jax.random.normal(k4, (12, 1), dtype=jnp.float32)}
    _L1_ffn_all = _L1_ffn_setup()
    _L1_ffn_in = {k: v for k, v in _L1_ffn_all.items() if k in ('c_fc_1', 'c_fc_2', 'c_proj_1', 'c_proj_2', )}
    del _L1_ffn_all

    return {
        "x": x,
        "L0_conv_in_proj_w": _L0_conv_in["in_proj_w"],
        "L0_conv_conv_w": _L0_conv_in["conv_w"],
        "L0_conv_conv_b": _L0_conv_in["conv_b"],
        "L0_conv_x_proj_weight": _L0_conv_in["x_proj_weight"],
        "L0_conv_dt_projs_weight": _L0_conv_in["dt_projs_weight"],
        "L0_conv_dt_projs_bias": _L0_conv_in["dt_projs_bias"],
        "L0_conv_A_logs": _L0_conv_in["A_logs"],
        "L0_conv_Ds": _L0_conv_in["Ds"],
        "L0_conv_out_norm_w": _L0_conv_in["out_norm_w"],
        "L0_conv_out_norm_b": _L0_conv_in["out_norm_b"],
        "L0_conv_out_proj_w": _L0_conv_in["out_proj_w"],
        "L0_ffn_gate_w": _L0_ffn_in["gate_w"],
        "L0_ffn_gate_b": _L0_ffn_in["gate_b"],
        "L0_ffn_w1": _L0_ffn_in["w1"],
        "L0_ffn_b1": _L0_ffn_in["b1"],
        "L0_ffn_w2": _L0_ffn_in["w2"],
        "L0_ffn_b2": _L0_ffn_in["b2"],
        "L1_conv_W_in": _L1_conv_in["W_in"],
        "L1_conv_W_conv": _L1_conv_in["W_conv"],
        "L1_conv_b_conv": _L1_conv_in["b_conv"],
        "L1_conv_dt_bias": _L1_conv_in["dt_bias"],
        "L1_conv_A_log": _L1_conv_in["A_log"],
        "L1_conv_D_param": _L1_conv_in["D_param"],
        "L1_conv_gamma": _L1_conv_in["gamma"],
        "L1_conv_beta": _L1_conv_in["beta"],
        "L1_conv_W_out": _L1_conv_in["W_out"],
        "L1_ffn_c_fc_1": _L1_ffn_in["c_fc_1"],
        "L1_ffn_c_fc_2": _L1_ffn_in["c_fc_2"],
        "L1_ffn_c_proj_1": _L1_ffn_in["c_proj_1"],
        "L1_ffn_c_proj_2": _L1_ffn_in["c_proj_2"],
    }

def reference(x, L0_conv_in_proj_w, L0_conv_conv_w, L0_conv_conv_b, L0_conv_x_proj_weight, L0_conv_dt_projs_weight, L0_conv_dt_projs_bias, L0_conv_A_logs, L0_conv_Ds, L0_conv_out_norm_w, L0_conv_out_norm_b, L0_conv_out_proj_w, L0_ffn_gate_w, L0_ffn_gate_b, L0_ffn_w1, L0_ffn_b1, L0_ffn_w2, L0_ffn_b2, L1_conv_W_in, L1_conv_W_conv, L1_conv_b_conv, L1_conv_dt_bias, L1_conv_A_log, L1_conv_D_param, L1_conv_gamma, L1_conv_beta, L1_conv_W_out, L1_ffn_c_fc_1, L1_ffn_c_fc_2, L1_ffn_c_proj_1, L1_ffn_c_proj_2):
    import jax
    import jax.numpy as jnp
    def _L0_conv_ref(x, in_proj_w, conv_w, conv_b, x_proj_weight, dt_projs_weight, dt_projs_bias, A_logs, Ds, out_norm_w, out_norm_b, out_proj_w):
        import jax, jax.numpy as jnp
        import numpy as np
        from jax import lax
        B_SZ, H_SZ, W_SZ = (2, 48, 48)
        D_MODEL = 192
        SSM_RATIO = 2.0
        D_PROJ = int(SSM_RATIO * D_MODEL)
        C_INNER = 2 * D_PROJ
        K_GRP = 4
        D_IN = C_INNER // K_GRP
        N_STATE = 16
        R_RANK = 12

        def _ss2d(x, in_proj_w, conv_w, conv_b, x_proj_weight, dt_projs_weight, dt_projs_bias, A_logs, Ds, out_norm_w, out_norm_b, out_proj_w):
            B, H, W, _ = x.shape
            C = in_proj_w.shape[0]
            K = x_proj_weight.shape[0]
            d = C // K
            N = A_logs.shape[1]
            R = dt_projs_weight.shape[2]
            L = H * W
            xz = jnp.einsum('bhwc,oc->bhwo', x, in_proj_w)
            xc = xz.transpose(0, 3, 1, 2)
            xc = lax.conv_general_dilated(xc, conv_w, (1, 1), 'SAME', feature_group_count=C)
            xc = xc + conv_b[None, :, None, None]
            xc = xc * jax.nn.sigmoid(xc)
            ch = xc.reshape(B, K, d, H, W)
            f0 = ch[:, 0].reshape(B, d, L)
            f1 = ch[:, 1].transpose(0, 1, 3, 2).reshape(B, d, L)
            f2 = jnp.flip(ch[:, 2].reshape(B, d, L), -1)
            f3 = jnp.flip(ch[:, 3].transpose(0, 1, 3, 2).reshape(B, d, L), -1)
            xs = jnp.stack([f0, f1, f2, f3], axis=1)
            x_dbl = jnp.einsum('bkdl,kcd->bkcl', xs, x_proj_weight)
            dts, Bs, Cs = jnp.split(x_dbl, [R, R + N], axis=2)
            dts = jnp.einsum('bkrl,kdr->bkdl', dts, dt_projs_weight) + dt_projs_bias[None, :, :, None]
            u = xs.astype(jnp.float32)
            dts = jax.nn.softplus(dts.astype(jnp.float32))
            Bs = Bs.astype(jnp.float32)
            Cs = Cs.astype(jnp.float32)
            A = -jnp.exp(A_logs.astype(jnp.float32)).reshape(K, d, N)

            def step(h, inp):
                u_t, dt_t, B_t, C_t = inp
                h = h * jnp.exp(dt_t[..., None] * A) + (dt_t * u_t)[..., None] * B_t[:, :, None, :]
                y_t = jnp.einsum('bkdn,bkn->bkd', h, C_t)
                return (h, y_t)
            inps = (u.transpose(3, 0, 1, 2), dts.transpose(3, 0, 1, 2), Bs.transpose(3, 0, 1, 2), Cs.transpose(3, 0, 1, 2))
            h0 = jnp.zeros((B, K, d, N), jnp.float32)
            _, ys = lax.scan(step, h0, inps)
            ys = ys.transpose(1, 2, 3, 0)
            ys = ys + Ds.astype(jnp.float32).reshape(K, d)[None, :, :, None] * u
            y0 = ys[:, 0]
            y1 = ys[:, 1].reshape(B, d, W, H).transpose(0, 1, 3, 2).reshape(B, d, L)
            y2 = jnp.flip(ys[:, 2], -1)
            y3 = jnp.flip(ys[:, 3], -1).reshape(B, d, W, H).transpose(0, 1, 3, 2).reshape(B, d, L)
            y = jnp.concatenate([y0, y1, y2, y3], axis=1).reshape(B, C, H, W).transpose(0, 2, 3, 1)
            mu = jnp.mean(y, -1, keepdims=True)
            var = jnp.mean(jnp.square(y - mu), -1, keepdims=True)
            y = (y - mu) * lax.rsqrt(var + 1e-05) * out_norm_w + out_norm_b
            out = jnp.einsum('bhwc,oc->bhwo', y.astype(x.dtype), out_proj_w)
            return out
        return _ss2d(x, in_proj_w, conv_w, conv_b, x_proj_weight, dt_projs_weight, dt_projs_bias, A_logs, Ds, out_norm_w, out_norm_b, out_proj_w)

    def _L0_ffn_ref(x, gate_w, gate_b, w1, b1, w2, b2):
        import jax, jax.numpy as jnp
        import numpy as np
        NUM_EXPERTS = 4
        TOP_K = 2
        DIM = 384
        HID = 4 * DIM
        scores = jnp.einsum('bsd,de->bse', x, gate_w) + gate_b
        probs = jax.nn.softmax(scores, axis=-1)
        topk_vals, topk_idx = jax.lax.top_k(probs, TOP_K)
        mask = jnp.sum(jax.nn.one_hot(topk_idx, NUM_EXPERTS, dtype=probs.dtype), axis=-2)
        masked = probs * mask
        masked = masked / (jnp.sum(masked, axis=-1, keepdims=True) + 1e-09)
        h = jax.nn.gelu(jnp.einsum('bsd,edh->ebsh', x, w1) + b1[:, None, None, :], approximate=False)
        y = jnp.einsum('ebsh,ehd->ebsd', h, w2) + b2[:, None, None, :]
        out = jnp.einsum('bse,ebsd->bsd', masked, y)
        return out

    def _L1_conv_ref(x, W_in, W_conv, b_conv, dt_bias, A_log, D_param, gamma, beta, W_out):
        import jax, jax.numpy as jnp
        import numpy as np
        D_MODEL = 384
        D_STATE = 16
        D_CONV = 3
        EXPAND = 2
        D_INNER = EXPAND * D_MODEL
        HEADDIM = 64
        NHEADS = D_INNER // HEADDIM
        NGROUPS = 1
        CHUNK = 64
        D_IN_PROJ = 2 * D_INNER + 2 * NGROUPS * D_STATE + NHEADS
        CONV_DIM = D_INNER + 2 * NGROUPS * D_STATE

        def segsum(x):
            T = x.shape[-1]
            xe = jnp.broadcast_to(x[..., None], x.shape + (T,))
            mask_strict = jnp.tril(jnp.ones((T, T), bool), -1)
            xe = jnp.where(mask_strict, xe, 0.0)
            x_segsum = jnp.cumsum(xe, axis=-2)
            mask_incl = jnp.tril(jnp.ones((T, T), bool), 0)
            return jnp.where(mask_incl, x_segsum, -jnp.inf)

        def ssd_minimal_discrete(X, A, Bm, Cm, block_len):
            b, seqlen, h, p = X.shape
            c = seqlen // block_len
            X = X.reshape(b, c, block_len, h, p)
            Bm = Bm.reshape(b, c, block_len, h, -1)
            Cm = Cm.reshape(b, c, block_len, h, -1)
            A = A.reshape(b, c, block_len, h).transpose(0, 3, 1, 2)
            A_cumsum = jnp.cumsum(A, axis=-1)
            L = jnp.exp(segsum(A))
            Y_diag = jnp.einsum('bclhn,bcshn,bhcls,bcshp->bclhp', Cm, Bm, L, X)
            decay_states = jnp.exp(A_cumsum[:, :, :, -1:] - A_cumsum)
            states = jnp.einsum('bclhn,bhcl,bclhp->bchpn', Bm, decay_states, X)
            init = jnp.zeros_like(states[:, :1])
            states = jnp.concatenate([init, states], axis=1)
            A_last = jnp.pad(A_cumsum[:, :, :, -1], ((0, 0), (0, 0), (1, 0)))
            decay_chunk = jnp.exp(segsum(A_last))
            new_states = jnp.einsum('bhzc,bchpn->bzhpn', decay_chunk, states)
            states, final_state = (new_states[:, :-1], new_states[:, -1])
            state_decay_out = jnp.exp(A_cumsum)
            Y_off = jnp.einsum('bclhn,bchpn,bhcl->bclhp', Cm, states, state_decay_out)
            Y = (Y_diag + Y_off).reshape(b, seqlen, h, p)
            return (Y, final_state)
        Bsz, H, W, C = x.shape
        L = H * W
        xf = x.reshape(Bsz, L, C)
        zxbcdt = xf @ W_in
        z = zxbcdt[..., :D_INNER]
        xBC = zxbcdt[..., D_INNER:D_INNER + CONV_DIM]
        dt = jax.nn.softplus(zxbcdt[..., D_INNER + CONV_DIM:] + dt_bias)
        xBC = xBC.reshape(Bsz, H, W, CONV_DIM)
        xBC = jax.lax.conv_general_dilated(xBC, W_conv, window_strides=(1, 1), padding='SAME', dimension_numbers=('NHWC', 'HWIO', 'NHWC'), feature_group_count=CONV_DIM) + b_conv
        xBC = jax.nn.silu(xBC).reshape(Bsz, L, CONV_DIM)
        x_inner = xBC[..., :D_INNER].reshape(Bsz, L, NHEADS, HEADDIM)
        gn = NGROUPS * D_STATE
        B_state = xBC[..., D_INNER:D_INNER + gn].reshape(Bsz, L, NGROUPS, D_STATE)
        C_state = xBC[..., D_INNER + gn:].reshape(Bsz, L, NGROUPS, D_STATE)
        rep = NHEADS // NGROUPS
        B_state = jnp.broadcast_to(B_state[:, :, :, None, :], (Bsz, L, NGROUPS, rep, D_STATE)).reshape(Bsz, L, NHEADS, D_STATE)
        C_state = jnp.broadcast_to(C_state[:, :, :, None, :], (Bsz, L, NGROUPS, rep, D_STATE)).reshape(Bsz, L, NHEADS, D_STATE)
        A = -jnp.exp(A_log)
        y, _ = ssd_minimal_discrete(x_inner * dt[..., None], A[None, None, :] * dt, B_state, C_state, CHUNK)
        y = y + x_inner * D_param[None, None, :, None]
        y = y.reshape(Bsz, L, D_INNER)
        mu = jnp.mean(y, axis=-1, keepdims=True)
        var = jnp.mean((y - mu) ** 2, axis=-1, keepdims=True)
        y = (y - mu) * jax.lax.rsqrt(var + 1e-05) * gamma + beta
        y = y * jax.nn.silu(z)
        y = y @ W_out
        return y.reshape(Bsz, H, W, D_MODEL)

    def _L1_ffn_ref(x, c_fc_1, c_fc_2, c_proj_1, c_proj_2):
        import jax, jax.numpy as jnp
        import numpy as np
        D_MODEL = 384
        D_FF = 1536
        w_fc = jnp.kron(c_fc_1, c_fc_2)
        w_proj = jnp.kron(c_proj_1, c_proj_2)
        h = x @ w_fc.T
        h = jax.nn.gelu(h, approximate=False)
        out = h @ w_proj.T
        return out

    def _gn(v, G=32, eps=1e-5):
        B_, H_, W_, C_ = v.shape
        g = v.reshape(B_, H_, W_, G, C_ // G)
        m = jnp.mean(g, axis=(1, 2, 4), keepdims=True)
        s = jnp.var(g, axis=(1, 2, 4), keepdims=True)
        return ((g - m) / jnp.sqrt(s + eps)).reshape(v.shape)

    def _ln_c(v, eps=1e-6):
        m = jnp.mean(v, axis=-1, keepdims=True)
        s = jnp.var(v, axis=-1, keepdims=True)
        return (v - m) / jnp.sqrt(s + eps)

    def _ln_t(v, eps=1e-5):
        m = jnp.mean(v, axis=-1, keepdims=True)
        s = jnp.var(v, axis=-1, keepdims=True)
        return (v - m) / jnp.sqrt(s + eps)

    def _to_tokens(v):
        B_, H_, W_, C_ = v.shape
        return v.reshape(B_, H_ * W_, C_)
    def _from_tokens(t, like):
        return t.reshape(like.shape)

    x = x + _L0_conv_ref(_ln_c(x), L0_conv_in_proj_w, L0_conv_conv_w, L0_conv_conv_b, L0_conv_x_proj_weight, L0_conv_dt_projs_weight, L0_conv_dt_projs_bias, L0_conv_A_logs, L0_conv_Ds, L0_conv_out_norm_w, L0_conv_out_norm_b, L0_conv_out_proj_w)
    t = _to_tokens(x)
    t = t + _L0_ffn_ref(_ln_t(t), L0_ffn_gate_w, L0_ffn_gate_b, L0_ffn_w1, L0_ffn_b1, L0_ffn_w2, L0_ffn_b2)
    x = _from_tokens(t, x)
    x = x + _L1_conv_ref(_ln_c(x), L1_conv_W_in, L1_conv_W_conv, L1_conv_b_conv, L1_conv_dt_bias, L1_conv_A_log, L1_conv_D_param, L1_conv_gamma, L1_conv_beta, L1_conv_W_out)
    t = _to_tokens(x)
    t = t + _L1_ffn_ref(_ln_t(t), L1_ffn_c_fc_1, L1_ffn_c_fc_2, L1_ffn_c_proj_1, L1_ffn_c_proj_2)
    x = _from_tokens(t, x)
    return x


_drawn_inputs = setup_inputs


def setup_inputs(seed=0):
    import zlib

    import numpy as np

    out = dict(_drawn_inputs(seed))
    spreads = {'L0_conv_conv_b': (0.0, 0.1),
     'L0_conv_Ds': (1.0, 0.2),
     'L0_conv_out_norm_w': (1.0, 0.2),
     'L0_conv_out_norm_b': (0.0, 0.1),
     'L0_ffn_gate_b': (0.0, 0.1),
     'L0_ffn_b1': (0.0, 0.1),
     'L0_ffn_b2': (0.0, 0.1),
     'L1_conv_D_param': (1.0, 0.6),
     'L1_conv_gamma': (1.0, 0.6),
     'L1_conv_beta': (0.0, 0.8)}
    factors = {'L0_conv_x_proj_weight': 8.0,
     'L0_conv_dt_projs_weight': 8.0,
     'L0_conv_dt_projs_bias': 8.0,
     'L0_conv_A_logs': 8.0,
     'L1_conv_b_conv': 7.228,
     'L1_conv_dt_bias': 8.0,
     'L1_conv_A_log': 8.0,
     'L1_ffn_c_fc_1': 8.0,
     'L1_ffn_c_fc_2': 8.0,
     'L1_ffn_c_proj_1': 8.0,
     'L1_ffn_c_proj_2': 8.0}
    for name, (base, spread) in spreads.items():
        noise = np.random.default_rng([zlib.crc32(name.encode()), seed]).standard_normal(out[name].shape)
        drawn = base * np.exp(spread * noise) if base else spread * noise
        out[name] = jnp.asarray(drawn.astype(out[name].dtype))
    for name, factor in factors.items():
        out[name] = (out[name] * factor).astype(out[name].dtype)
    return out
```

```python
from contextlib import ExitStack

import concourse.bass as bass
from concourse import mybir

F32 = mybir.dt.float32
F16 = mybir.dt.float16
BF16 = mybir.dt.bfloat16
ACT = mybir.ActivationFunctionType
ALU = mybir.AluOpType
AX = mybir.AxisListType

P = 128
IMAGES, SIDE, D = 2, 48, 384
L = SIDE * SIDE
T = IMAGES * L
DC = D // P
G = 384
GT = G // P
NG = T // G
GI = L // G
ROWS = G // SIDE
BANK = 512

KD, DI, NS, RANK = 4, 192, 16, 12
CI = KD * DI
REST = DI - P
BC = 2 * NS
EX, HID = 4, 1536
HEADS, HP = 12, 64
DIN = HEADS * HP
CONV = DIN + 2 * NS
KR, KJ, FF = 32, 12, 1536


class Chain:

    def __init__(self, eng, sem, per):
        self.eng, self.sem, self.per = eng, sem, per
        self.base, self.n = 0, 0

    def start(self, turn):
        assert self.n in (0, self.per), (self.n, self.per)
        self.base, self.n = turn * self.per, 0

    def mark(self, ins):
        ins.then_inc(self.sem, 1)
        self.n += 1

    def wait(self):
        self.eng.wait_ge(self.sem, self.base + self.n)

    def __call__(self, ins):
        self.mark(ins)
        self.wait()


def settle(eng, held):
    eng.sem_inc(held, 1)


class Stage:

    def __init__(self, nc, name):
        self.nc, self.name = nc, name

    def __enter__(self):
        self.ctx, self.sems = ExitStack(), []
        return self

    def sb(self, name, shape, dt=F32):
        return self.ctx.enter_context(self.nc.sbuf_tensor(f"{self.name}_{name}", shape, dt))

    def ps(self, name, shape, dt=F32):
        return self.ctx.enter_context(self.nc.psum_tensor(f"{self.name}_{name}", shape, dt))

    def sem(self, name):
        self.sems.append(self.nc.alloc_semaphore(f"{self.name}_{name}"))
        return self.sems[-1]

    def block(self):
        return self.ctx.enter_context(self.nc.Block())

    def __exit__(self, *a):
        self.ctx.__exit__(*a)
        if self.sems:
            self.nc.clear_and_free_semaphores(self.sems)
            self.nc.all_engine_barrier()


def tok_groups(dram):
    return dram.rearrange("(g t p) d -> g p t d", t=GT, p=P)


def norm_steps(dve, chain, x, stats, mv, std, rstd, out, var_ready, std_ready, turn, held):
    nc = dve.bass
    for t in range(GT):
        chain.mark(nc.vector.bn_stats(stats[:, t, :], x[:, t, :]))
    chain.wait()
    settle(dve, held)
    for t in range(GT):
        chain.mark(nc.vector.bn_aggr(mv[:, t, :], stats[:, t, :]))
    chain.wait()
    nc.vector.tensor_copy(std[:, 0, :], mv[:, :, 1]).then_inc(var_ready, 1)
    dve.wait_ge(std_ready, turn + 1)
    chain(nc.vector.reciprocal(rstd[:, :], std[:, 1, :]))
    for t in range(GT):
        last = nc.vector.tensor_scalar(out[:, t, :], x[:, t, :], mv[:, t, 0:1], rstd[:, t:t + 1],
                                       ALU.subtract, ALU.mult)
    return last


NORM_STEPS = 2 * GT + 1


CREDIT = 2


def free(turn):
    return turn + 1


def ready(turn):
    return turn + CREDIT + 1


def norm_transpose(nc, name, c, src, dst, eps):
    src_g = tok_groups(src)
    with Stage(nc, name) as s:
        ident = s.sb("ident", [P, P])
        epst = s.sb("eps", [P, 1])
        x = [s.sb(f"x{u}", [P, GT, D]) for u in range(2)]
        xn = [s.sb(f"xn{u}", [P, GT, D]) for u in range(2)]
        xt = [s.sb(f"xt{u}", [P, DC, G]) for u in range(2)]
        stats, mv = s.sb("stats", [P, GT, 6]), s.sb("mv", [P, GT, 2])
        std, rstd = s.sb("std", [P, 2, GT]), s.sb("rstd", [P, GT])
        pt = [s.ps(f"pt{u}", [P, DC, BANK]) for u in range(2)]
        held = s.sem("held")
        consts, x_in = s.sem("consts"), [s.sem("x_in0"), s.sem("x_in1")]
        stored = [s.sem("stored0"), s.sem("stored1")]
        eps_set, var_ready, std_ready = s.sem("eps_set"), s.sem("var_ready"), s.sem("std_ready")
        normed, steps, turned, copied = s.sem("normed"), s.sem("steps"), s.sem("turned"), s.sem("copied")
        block = s.block()

        @block.sync
        def _(sp):
            sp.dma_start(ident[:, :], c["ident"]).then_inc(consts, 16)
            with sp.Fori(0, NG // 2) as i:
                for u in range(2):
                    g = i * 2 + u
                    sp.wait_ge(normed, free(g))
                    sp.dma_start(x[u][:, :, :], src_g[g]).then_inc(x_in[u], 16)

        @block.vector
        def _(dve):
            nc.vector.memset(epst[:, :], eps).then_inc(eps_set, 1)
            dve.sem_inc(normed, CREDIT)
            chain = Chain(dve, steps, NORM_STEPS)
            with dve.Fori(0, NG // 2) as i:
                for u in range(2):
                    g = i * 2 + u
                    chain.start(g)
                    dve.wait_ge(x_in[u], i * 16 + 16)
                    dve.wait_ge(turned, free(g))
                    norm_steps(dve, chain, x[u], stats, mv, std, rstd, xn[u], var_ready, std_ready, g,
                               held).then_inc(normed, 1)

        @block.tensor
        def _(pe):
            pe.sem_inc(turned, CREDIT)
            pe.wait_ge(consts, 16)
            with pe.Fori(0, NG // 2) as i:
                for u in range(2):
                    g = i * 2 + u
                    pe.wait_ge(normed, ready(g))
                    pe.wait_ge(copied, free(g))
                    for t in range(GT):
                        for d in range(DC):
                            ins = nc.tensor.transpose(pt[u][:, d, t * P:(t + 1) * P],
                                                      xn[u][:, t, d * P:(d + 1) * P], ident[:, :])
                    ins.then_inc(turned, 1)

        @block.scalar
        def _(act):
            act.sem_inc(copied, CREDIT)
            for u in range(2):
                act.sem_inc(stored[u], 16)
            act.wait_ge(eps_set, 1)
            with act.Fori(0, NG // 2) as i:
                for u in range(2):
                    g = i * 2 + u
                    act.wait_ge(var_ready, g + 1)
                    nc.scalar.activation(std[:, 1, :], std[:, 0, :], ACT.Sqrt, bias=epst[:, :]).then_inc(std_ready, 1)
                    act.wait_ge(turned, ready(g))
                    act.wait_ge(stored[u], i * 16 + 16)
                    nc.scalar.copy(xt[u][:, :, :], pt[u][:, :, 0:G]).then_inc(copied, 1)
                    act.wait_ge(copied, ready(g))
                    act.dma_start(dst[:, :, bass.ds(g * G, G)], xt[u][:, :, :]).then_inc(stored[u], 16)
            for u in range(2):
                act.wait_ge(stored[u], 16 * (NG // 2 + 1))


SEG = 2 * G
SEGS = L // SEG
STEPS_N = 3 * SEGS
PARTS = 3
BROWS = PARTS * BC
XROWS = BROWS + RANK


def in_order(image, k):
    if k >= 2:
        image = image[:, ::-1]
    return image.rearrange("p (h w) -> p h w" if k % 2 == 0 else "p (h w) -> p w h", h=SIDE)


def ss2d_conv(nc, c, w, k, xn, u, aneg, sel):
    with Stage(nc, f"a{k}") as s:
        win = s.sb("win", [P, 3, DC, P])
        taps, bias = s.sb("taps", [P, 3, 9]), s.sb("bias", [P, 3])
        alog = s.sb("alog", [P, 3, NS])
        pad = [s.sb(f"pad{v}", [P, SIDE + 2, SIDE + 2]) for v in range(2)]
        acc = [s.sb(f"acc{v}", [P, SIDE, SIDE]) for v in range(2)]
        pi = [s.ps(f"pi{v}", [P, BANK]) for v in range(2)]
        xn_in = [s.sem(f"xn_in{b}") for b in range(IMAGES)]
        loaded, win_in, zeroed, projected, padded, tapped, convolved, active, a_ready, a_exp, held = (s.sem(x) for x in (
            "loaded win_in zeroed projected padded tapped convolved active a_ready a_exp held".split()))
        block = s.block()

        @block.sync
        def _(sp):
            sp.dma_start(win[:, :, :, :], w["in_proj"][k]).then_inc(win_in, 16)
            sp.dma_start(xn[:, 0, :, :], w["xn"][:, :, 0:L]).then_inc(xn_in[0], 16)
            sp.dma_start(taps[:, :, :], w["conv"][k]).then_inc(loaded, 16)
            sp.dma_start(bias[:, :], w["conv_b"][k]).then_inc(loaded, 16)
            sp.dma_start(alog[:, :, :], w["a_logs"][k]).then_inc(loaded, 16)
            sp.dma_start(xn[:, 1, :, :], w["xn"][:, :, L:T]).then_inc(xn_in[1], 16)
            if sel:
                sp.dma_start(sel[0][:, :, :, :], c["sel"]).then_inc(sel[1], 16)
                sp.wait_ge(sel[1], 16)

        @block.gpsimd
        def _(pool):
            for v in range(2):
                nc.gpsimd.memset(pad[v][:, :, :], 0.0).then_inc(zeroed, 1)

        @block.tensor
        def _(pe):
            pe.sem_inc(projected, CREDIT)
            pe.wait_ge(win_in, 16)
            for ct in range(3):
                images = ((0,), (1,), (0, 1))[ct]
                pe.wait_ge(xn_in[images[0]], 16)
                terms = [(j, b, d) for j, b in enumerate(images) for d in range(DC)]
                with pe.Fori(0, GI // 2) as i:
                    for v in range(2):
                        q = i * 2 + v
                        pe.wait_ge(padded, free(q + ct * GI))
                        for j, b, d in terms:
                            ins = nc.tensor.matmul(pi[v][:, 0:G], win[:, 1 + j if ct == 2 else 0, d, :],
                                                   xn[:, b, d, bass.ds(q * G, G)],
                                                   start=(j, d) == (0, 0), stop=(j, b, d) == terms[-1])
                        ins.then_inc(projected, 1)

        @block.vector
        def _(dve):
            dve.wait_ge(loaded, 48)
            dve.wait_ge(a_exp, 1)
            nc.vector.tensor_scalar(aneg[:, :, :], alog[:, :, :], -1.0, None, ALU.mult).then_inc(a_ready, 1)
            chain = Chain(dve, tapped, None)
            for ct in range(3):
                dve.wait_ge(padded, CREDIT + GI * (ct + 1))
                if ct == 2:
                    dve.wait_ge(active, 1)
                image = acc[ct % 2][:, :, :]
                for t in range(9):
                    rows = pad[ct % 2][:, t // 3:t // 3 + SIDE, t % 3:t % 3 + SIDE]
                    tap = taps[:, ct, t:t + 1]
                    if t == 0:
                        ins = nc.vector.tensor_scalar(image, rows, tap, None, ALU.mult)
                    else:
                        ins = nc.vector.scalar_tensor_tensor(out=image, in0=rows, scalar=tap, in1=image,
                                                             op0=ALU.mult, op1=ALU.add)
                    if t < 8:
                        chain(ins)
                ins.then_inc(convolved, 1)

        @block.scalar
        def _(act):
            act.sem_inc(padded, CREDIT)
            act.wait_ge(loaded, 48)
            nc.scalar.activation(alog[:, :, :], alog[:, :, :], ACT.Exp).then_inc(a_exp, 1)
            act.wait_ge(zeroed, 2)

            def silu(ct):
                act.wait_ge(convolved, ct + 1)
                nc.scalar.activation(in_order(u[:, ct, :], k), acc[ct % 2][:, :, :], ACT.Silu,
                                     bias=bias[:, ct:ct + 1]).then_inc(active, 1)

            for ct in range(3):
                if ct == 2:
                    act.wait_ge(convolved, 1)
                with act.Fori(0, GI // 2) as i:
                    for v in range(2):
                        q = i * 2 + v
                        act.wait_ge(projected, ready(q + ct * GI))
                        settle(act, held)
                        nc.scalar.copy(pad[ct % 2][:, bass.ds(q * ROWS + 1, ROWS), 1:SIDE + 1],
                                       pi[v][:, 0:G].rearrange("p (h w) -> p h w", w=SIDE)).then_inc(padded, 1)
                if ct:
                    silu(ct - 1)
            silu(2)


def ss2d_project(nc, c, w, k, u, dt, y, bc):
    with Stage(nc, f"b{k}") as s:
        wx = s.sb("wx", [P, 3, XROWS])
        wd = s.sb("wd", [XROWS, 3, P])
        dtb, ds = s.sb("dtb", [P, 3]), s.sb("ds", [P, 3])
        xd = [s.sb(f"xd{b}", [XROWS, G]) for b in range(IMAGES)]
        rest = s.sb("rest", [64, G])
        e, one_e, ln, corr = (s.sb(x, [P, 3, G]) for x in ("e", "one_e", "ln", "corr"))
        pos = s.sb("pos", [P, 3, G])
        px = [s.ps(f"px{b}", [P, BANK]) for b in range(IMAGES)]
        pd = s.ps("pd", [P, 3, BANK])
        loaded, projected, xd_ready, split, dt_done = (s.sem(x) for x in (
            "loaded", "projected", "xd_ready", "split", "dt_done"))
        e_ready, one_ready, ln_ready, steps, summed, spread = (s.sem(x) for x in (
            "e_ready", "one_ready", "ln_ready", "steps", "summed", "spread"))
        act_steps, one_set, held = s.sem("act_steps"), s.sem("one_set"), s.sem("held")
        ln_one = s.sb("ln_one", [P, 2])
        block = s.block()

        @block.sync
        def _(sp):
            sp.dma_start(wx[:, :, :], w["x_proj"][k]).then_inc(loaded, 16)
            sp.dma_start(wd[:, :, :], w["dt_proj"][k]).then_inc(loaded, 16)
            sp.dma_start(dtb[:, :], w["dt_b"][k]).then_inc(loaded, 16)
            sp.dma_start(ds[:, :], w["ds"][k]).then_inc(loaded, 16)

        @block.tensor
        def _(pe):
            pe.wait_ge(loaded, 64)
            with pe.Fori(0, GI) as q:
                for b in range(IMAGES):
                    pe.wait_ge(xd_ready, q * 2 + b + 1)
                    nc.tensor.matmul(px[b][0:XROWS, 0:G], wx[:, 0, :], u[:, b, bass.ds(q * G, G)],
                                     start=True, stop=False)
                    nc.tensor.matmul(px[b][0:XROWS, 0:G], wx[:, 1 + b, :], u[:, 2, bass.ds(q * G, G)],
                                     start=False, stop=True).then_inc(projected, 1)
                pe.wait_ge(xd_ready, q * 2 + 4)
                pe.wait_ge(summed, q + 1)
                for b in range(IMAGES):
                    nc.tensor.matmul(pd[:, b, 0:G], wd[:, 0, :], xd[b][:, :], start=True, stop=True)
                nc.tensor.matmul(pd[:, 2, 0:G], wd[:, 1, :], xd[0][:, :], start=True, stop=False)
                nc.tensor.matmul(pd[:, 2, 0:G], wd[:, 2, :], xd[1][:, :], start=False, stop=True).then_inc(dt_done, 1)

        @block.scalar
        def _(act):
            nc.scalar.preload_act_table_set("natural_log_exp_and_others")
            act.sem_inc(xd_ready, 2)
            act.wait_ge(one_set, 1)
            nc.scalar.activation(ln_one[:, 1:2], ln_one[:, 0:1], ACT.Ln).then_inc(one_set, 1)
            chain = Chain(act, act_steps, 1)
            act.wait_ge(loaded, 64)
            with act.Fori(0, GI) as q:
                act.wait_ge(split, q + 1)
                for b in range(IMAGES):
                    act.wait_ge(projected, q * 2 + b + 1)
                    nc.scalar.copy(xd[b][:, :], px[b][0:XROWS, 0:G]).then_inc(xd_ready, 1)
                act.wait_ge(dt_done, q + 1)
                chain.start(q)
                for ct in range(3):
                    ins = nc.scalar.activation(e[:, ct, :], pd[:, ct, 0:G], ACT.Abs, bias=dtb[:, ct:ct + 1])
                chain(ins)
                nc.scalar.activation(e[:, :, :], e[:, :, :], ACT.Exp, scale=-1.0).then_inc(e_ready, 1)
                act.wait_ge(one_ready, q + 1)
                nc.scalar.activation(ln[:, :, :], one_e[:, :, :], ACT.Ln).then_inc(ln_ready, 1)

        @block.vector
        def _(dve):
            dve.sem_inc(split, 1)
            dve.sem_inc(summed, 1)
            nc.vector.memset(ln_one[:, 0:1], 1.0).then_inc(one_set, 1)
            chain = Chain(dve, steps, 7)
            dve.wait_ge(loaded, 64)
            dve.wait_ge(one_set, 2)
            with dve.Fori(0, GI) as q:
                chain.start(q)
                cols = bass.ds(q * G, G)
                for b in range(IMAGES):
                    dve.wait_ge(xd_ready, q * 2 + 3 + b)
                    settle(dve, held)
                    chain(nc.vector.tensor_copy(bc[:, b, cols], xd[b][0:BROWS, :]))
                    chain(nc.vector.tensor_tensor(rest[:, :], xd[b][0:64, :], bc[0:64, b, cols], ALU.subtract))
                    settle(dve, held)
                    chain(nc.vector.tensor_copy(bc[0:64, b, cols], rest[:, :]))
                    last = nc.vector.tensor_tensor(bc[0:32, b, cols], rest[0:32, :], bc[0:32, b, cols], ALU.subtract)
                last.then_inc(split, 1)
                for ct in range(3):
                    nc.vector.tensor_scalar(y[:, ct, cols], u[:, ct, cols], ds[:, ct:ct + 1], None, ALU.mult)
                dve.wait_ge(e_ready, q + 1)
                nc.vector.tensor_scalar(one_e[:, :, :], e[:, :, :], 1.0, None, ALU.add).then_inc(one_ready, 1)
                for ct in range(3):
                    nc.vector.tensor_scalar(pos[:, ct, :], pd[:, ct, 0:G], dtb[:, ct:ct + 1], 0.0, ALU.add, ALU.max)
                dve.wait_ge(one_ready, q + 1)
                chain(nc.vector.scalar_tensor_tensor(out=corr[:, :, :], in0=one_e[:, :, :], scalar=1.0, in1=e[:, :, :],
                                                     op0=ALU.subtract, op1=ALU.subtract))
                dve.wait_ge(ln_ready, q + 1)
                nc.vector.scalar_tensor_tensor(out=corr[:, :, :], in0=ln[:, :, :], scalar=ln_one[:, 1:2], in1=corr[:, :, :],
                                               op0=ALU.subtract, op1=ALU.subtract).then_inc(summed, 1)
                dve.wait_ge(summed, q + 2)
                nc.vector.tensor_tensor(dt[:, :, cols], corr[:, :, :], pos[:, :, :], ALU.add).then_inc(spread, 1)

        @block.gpsimd
        def _(pool):
            with pool.Fori(0, GI) as q:
                cols = bass.ds(q * G, G)
                pool.wait_ge(spread, q + 1)
                nc.gpsimd.tensor_tensor(u[:, :, cols], dt[:, :, cols], u[:, :, cols], ALU.mult)


def ss2d_scan(nc, c, w, k, du, dt, y, bc, aneg, sel, out):
    with Stage(nc, f"c{k}") as s:
        a, h, hc = ([s.sb(f"{x}{v}", [P, SEG]) for v in range(2)] for x in ("a", "h", "hc"))
        pb, pcc = ([s.ps(f"{x}{v}", [P, 2 * BANK]) for v in range(2)] for x in ("pb", "pc"))
        b_ready, c_ready, a_ready = s.sem("b_ready"), s.sem("c_ready"), s.sem("a_ready")
        fed, scanned, weighed, added = s.sem("fed"), s.sem("scanned"), s.sem("weighed"), s.sem("added")
        ordered, stored, held = s.sem("ordered"), s.sem("stored"), s.sem("held")
        block = s.block()
        ITER = 2 * STEPS_N

        def place(m):
            return (m % STEPS_N) // SEGS, m % SEGS, m % 2, m // STEPS_N

        def cols(t, ct, seg):
            return t[:, ct, seg * SEG:(seg + 1) * SEG]

        @block.tensor
        def _(pe):
            with pe.Fori(0, NS // 2) as i:
                def spread(m, first, tiles, gone, signal):
                    ct, seg, v, half = place(m)
                    pe.wait_ge(gone, free(i * ITER + m))
                    terms = (((0, 0),), ((1, 0),), ((0, 1), (1, 2)))[ct]
                    for j, width in ((0, BANK), (BANK, SEG - BANK)):
                        at = seg * SEG + j
                        for b, kind in terms:
                            ins = nc.tensor.matmul(tiles[v][:, j:j + width], sel[:, kind, i * 2 + (half + first), :],
                                                   bc[:, b, at:at + width], start=(b, kind) == terms[0],
                                                   stop=(b, kind) == terms[-1])
                    ins.then_inc(signal, 1)

                spread(0, 0, pb, scanned, b_ready)
                for m in range(ITER):
                    if m + 1 < ITER:
                        spread(m + 1, 0, pb, scanned, b_ready)
                    spread(m, NS, pcc, weighed, c_ready)

        @block.scalar
        def _(act):
            with act.Fori(0, NS // 2) as i:
                for m in range(ITER):
                    ct, seg, v, half = place(m)
                    act.wait_ge(scanned, free(i * ITER + m))
                    settle(act, held)
                    nc.scalar.activation(a[v][:, :], dt[:, ct, seg * SEG:(seg + 1) * SEG], ACT.Exp,
                                         scale=aneg[:, ct, bass.ds(i * 2 + half, 1)]).then_inc(a_ready, 1)

        @block.vector
        def _(dve):
            dve.sem_inc(scanned, CREDIT)
            dve.sem_inc(weighed, CREDIT)
            with dve.Fori(0, NS // 2) as i:
                def feed(m):
                    ct, seg, v, _ = place(m)
                    dve.wait_ge(b_ready, i * ITER + m + 1)
                    nc.vector.tensor_tensor(pb[v][:, 0:SEG], pb[v][:, 0:SEG], cols(du, ct, seg), ALU.mult).then_inc(fed, 1)

                def scan(m):
                    ct, seg, v, _ = place(m)
                    dve.wait_ge(fed, i * ITER + m + 1)
                    dve.wait_ge(a_ready, i * ITER + m + 1)
                    dve.wait_ge(weighed, free(i * ITER + m))
                    if seg:
                        dve.wait_ge(scanned, i * ITER + m + CREDIT)
                    nc.vector.tensor_tensor_scan(h[v][:, :], a[v][:, :], pb[v][:, 0:SEG], h[1 - v][:, SEG - 1:SEG] if seg else 0.0,
                                                 ALU.mult, ALU.add).then_inc(scanned, 1)

                def weigh(m):
                    ct, seg, v, _ = place(m)
                    dve.wait_ge(scanned, i * ITER + m + 1 + CREDIT)
                    dve.wait_ge(c_ready, i * ITER + m + 1)
                    dve.wait_ge(added, i * ITER + (m - 1 + STEPS_N))
                    nc.vector.tensor_tensor(hc[v][:, :], h[v][:, :], pcc[v][:, 0:SEG], ALU.mult).then_inc(weighed, 1)

                feed(0)
                for m in range(ITER):
                    if m + 1 < ITER:
                        feed(m + 1)
                    scan(m)
                    if m:
                        weigh(m - 1)
                weigh(ITER - 1)
            if k:
                for ct in range(3):
                    dve.wait_ge(added, NS * STEPS_N + STEPS_N)
                    nc.vector.tensor_copy(in_order(du[:, ct, :], k), y[:, ct, :].rearrange("p (h w) -> p h w", w=SIDE)).then_inc(ordered, 1)

        @block.gpsimd
        def _(pool):
            pool.sem_inc(added, STEPS_N)
            with pool.Fori(0, NS // 2) as i:
                for m in range(ITER):
                    ct, seg, v, half = place(m)
                    pool.wait_ge(weighed, ready(i * ITER + m))
                    pool.wait_ge(added, i * ITER + m + 1)
                    part = y[:, ct, seg * SEG:(seg + 1) * SEG]
                    nc.gpsimd.tensor_tensor(part, part, hc[v][:, :], ALU.add).then_inc(added, 1)

        @block.sync
        def _(sp):
            sp.wait_ge(added, NS * STEPS_N + STEPS_N)
            src = du if k else y
            if k:
                sp.wait_ge(ordered, 3)
            slot, row = 4 + k // 2, (k % 2) * REST
            sp.dma_start(out[k, :, 0:L], src[:, 0, :]).then_inc(stored, 16)
            sp.dma_start(out[k, :, L:T], src[:, 1, :]).then_inc(stored, 16)
            sp.dma_start(out[slot, row:row + REST, 0:L], src[0:REST, 2, :]).then_inc(stored, 16)
            sp.dma_start(out[slot, row:row + REST, L:T], src[REST:P, 2, :]).then_inc(stored, 16)
            sp.wait_ge(stored, 64)


def ss2d(nc, c, w, out, directions=range(KD)):
    with Stage(nc, "ss2d") as s:
        u = s.sb("u", [P, 3, L])
        bc = s.sb("bc", [BROWS, IMAGES, L], BF16)
        aneg = s.sb("aneg", [P, 3, NS])
        sel = s.sb("sel", [BROWS, 3, BC, P], BF16)
        sel_in = s.sem("sel_in")
        for k in directions:
            with Stage(nc, f"x{k}") as t:
                xn = t.sb("xn", [P, IMAGES, DC, L])
                ss2d_conv(nc, c, w, k, xn, u, aneg, (sel, sel_in) if k == directions[0] else None)
            with Stage(nc, f"y{k}") as t:
                dt, y = t.sb("dt", [P, 3, L]), t.sb("y", [P, 3, L])
                ss2d_project(nc, c, w, k, u, dt, y, bc)
                ss2d_scan(nc, c, w, k, u, dt, y, bc, aneg, sel, out)


SLOTS = CI // P
NT = T // P


def ss2d_out(nc, c, w, y, x, x1, th, tl, scores_out):
    xg, x1g = tok_groups(x), tok_groups(x1)
    with Stage(nc, "o") as s:
        ident, mean_w = s.sb("ident", [P, P]), s.sb("mean_w", [P, P])
        wo, nw, nb = s.sb("wo", [P, SLOTS, D]), s.sb("nw", [P, SLOTS]), s.sb("nb", [P, SLOTS])
        nbb, bias = s.sb("nbb", [P, SLOTS, P]), s.sb("bias", [P, D])
        gw, gb, ones = s.sb("gw", [P, DC, EX]), s.sb("gb", [1, EX]), s.sb("ones", [P, P])
        epst = s.sb("eps", [P, 1])
        yt = [s.sb(f"yt{u}", [P, SLOTS, G]) for u in range(2)]
        sq = s.sb("sq", [P, SLOTS, G])
        xin = [s.sb(f"xin{u}", [P, GT, D]) for u in range(2)]
        xo = [s.sb(f"xo{u}", [P, GT, D]) for u in range(2)]
        xn = s.sb("xn", [P, GT, D])
        xt = s.sb("xt", [P, DC, G])
        hi = [s.sb(f"hi{u}", [P, DC, G], F16) for u in range(2)]
        lo = [s.sb(f"lo{u}", [P, DC, G], F16) for u in range(2)]
        stats, mv = s.sb("stats", [P, GT, 6]), s.sb("mv", [P, GT, 2])
        std, rstd = s.sb("std", [P, 2, GT]), s.sb("rstd", [P, GT])
        ystd, yrstd = s.sb("ystd", [P, GT]), s.sb("yrstd", [P, GT])
        sc = s.sb("sc", [P, NT, EX])
        pm, po, pt, pg = (s.ps("pm", [P, BANK]), s.ps("po", [P, GT, BANK]), s.ps("pt", [P, DC, BANK]),
                          s.ps("pg", [P, BANK]))
        loaded, y_in, x_in, x_out, t_out, sc_out = (s.sem("loaded"), [s.sem(f"y_in{u}") for u in range(2)],
                                                    [s.sem(f"x_in{u}") for u in range(2)], [s.sem(f"x_out{u}") for u in range(2)],
                                                    [s.sem(f"t_out{u}") for u in range(2)], s.sem("sc_out"))
        (eps_set, setup, bias_sum, mean_ready, centred, squared, var_ready, rooted, projected, x1_ready, nvar_ready, nstd_ready,
         normed, turned, copied, scored, taken, hi_ready, lo_ready, steps, held, ydone) = (s.sem(x) for x in (
             "eps_set setup bias_sum mean_ready centred squared var_ready rooted projected x1_ready nvar_ready nstd_ready "
             "normed turned copied scored taken hi_ready lo_ready steps held ydone").split())
        block = s.block()

        @block.sync
        def _(sp):
            for tile, src in ((ident[:, :], c["ident"]), (mean_w[:, :], c["mean768"]), (wo[:, :, :], w["out_proj"]),
                              (nw[:, :], w["out_nw"]), (nb[:, :], w["out_nb"]), (gw[:, :, :], w["gate_w"]), (gb[:, :], w["gate_b"])):
                sp.dma_start(tile, src).then_inc(loaded, 16)
            with sp.Fori(0, NG // 2) as i:
                for v in range(2):
                    g = i * 2 + v
                    sp.wait_ge(projected, free(g))
                    sp.dma_start(yt[v][:, :, :], y.rearrange("s p t -> p s t")[:, :, bass.ds(g * G, G)]).then_inc(y_in[v], 16)
                    sp.wait_ge(x1_ready, free(g))
                    sp.dma_start(xin[v][:, :, :], xg[g]).then_inc(x_in[v], 16)
            sp.wait_ge(taken, NG + 1)
            sp.dma_start(scores_out, sc[:, :, :]).then_inc(sc_out, 16)
            sp.wait_ge(sc_out, 16)

        @block.vector
        def _(dve):
            nc.vector.memset(ones[:, :], 1.0).then_inc(eps_set, 1)
            nc.vector.memset(epst[:, :], 1e-5).then_inc(eps_set, 1)
            dve.sem_inc(x1_ready, CREDIT)
            dve.sem_inc(taken, 1)
            dve.wait_ge(loaded, 112)
            dve.wait_ge(eps_set, 2)
            for j in range(SLOTS):
                ins = nc.vector.tensor_scalar(nbb[:, j, :], ones[:, :], nb[:, j:j + 1], None, ALU.mult)
            ins.then_inc(setup, 1)
            dve.wait_ge(bias_sum, 1)
            nc.vector.tensor_copy(bias[:, :], pm[:, 0:D])
            for j in range(SLOTS):
                ins = nc.vector.tensor_scalar(wo[:, j, :], wo[:, j, :], nw[:, j:j + 1], None, ALU.mult)
            ins.then_inc(setup, 1)
            dve.wait_ge(setup, 2)
            chain = Chain(dve, steps, NORM_STEPS + 2)
            with dve.Fori(0, NG // 2) as i:
                for v in range(2):
                    g = i * 2 + v
                    chain.start(g)
                    dve.wait_ge(mean_ready, g + 1)
                    nc.vector.tensor_tensor(yt[v][:, :, :], yt[v][:, :, :],
                                            pm[:, 0:G].rearrange("p (a g) -> p a g", a=1).to_broadcast([P, SLOTS, G]),
                                            ALU.subtract).then_inc(centred, 1)
                    dve.wait_ge(rooted, g + 2)
                    chain(nc.vector.reciprocal(yrstd[:, :], ystd[:, :]))
                    dve.wait_ge(projected, ready(g))
                    dve.wait_ge(x_in[v], i * 16 + 16)
                    dve.wait_ge(x_out[v], i * 16 + 16)
                    for t in range(GT):
                        ins = nc.vector.scalar_tensor_tensor(out=xo[v][:, t, :], in0=po[:, t, 0:D], scalar=yrstd[:, t:t + 1],
                                                             in1=xin[v][:, t, :], op0=ALU.mult, op1=ALU.add)
                    chain(ins)
                    nc.vector.tensor_tensor(xo[v][:, :, :], xo[v][:, :, :],
                                            bias[:, :].rearrange("p (a g) -> p a g", a=1).to_broadcast([P, GT, D]),
                                            ALU.add).then_inc(x1_ready, 1)
                    dve.wait_ge(x1_ready, ready(g))
                    dve.wait_ge(turned, g + 1)
                    norm_steps(dve, chain, xo[v], stats, mv, std, rstd, xn, nvar_ready, nstd_ready, g, held).then_inc(normed, 1)
                    dve.wait_ge(scored, g + 2)
                    settle(dve, held)
                    nc.vector.tensor_copy(sc[:, bass.ds(g * GT, GT), :],
                                          pg[:, 0:GT * EX].rearrange("p (t e) -> p t e", e=EX)).then_inc(taken, 1)

        @block.gpsimd
        def _(pool):
            pool.sem_inc(lo_ready, 1)
            with pool.Fori(0, NG // 2) as i:
                for v in range(2):
                    g = i * 2 + v
                    pool.wait_ge(hi_ready, g + 1)
                    pool.wait_ge(t_out[v], i * 32 + 32)
                    nc.gpsimd.tensor_tensor(lo[v][:, :, :], xt[:, :, :], hi[v][:, :, :], ALU.subtract).then_inc(lo_ready, 1)

        @block.tensor
        def _(pe):
            pe.sem_inc(projected, CREDIT)
            pe.sem_inc(turned, 1)
            pe.sem_inc(scored, 1)
            pe.wait_ge(loaded, 112)
            pe.wait_ge(setup, 1)
            for j in range(SLOTS):
                ins = nc.tensor.matmul(pm[:, 0:D], nbb[:, j, :], wo[:, j, :], start=j == 0, stop=j == SLOTS - 1)
            ins.then_inc(bias_sum, 1)
            pe.wait_ge(setup, 2)
            with pe.Fori(0, NG // 2) as i:
                for v in range(2):
                    g = i * 2 + v
                    pe.wait_ge(y_in[v], i * 16 + 16)
                    pe.wait_ge(rooted, g + 1)
                    for j in range(SLOTS):
                        ins = nc.tensor.matmul(pm[:, 0:G], mean_w[:, :], yt[v][:, j, :], start=j == 0, stop=j == SLOTS - 1)
                    ins.then_inc(mean_ready, 1)
                    pe.wait_ge(squared, g + 1)
                    for t in range(GT):
                        for j in range(SLOTS):
                            ins = nc.tensor.matmul(pm[:, G + t:G + t + 1], sq[:, j, t * P:(t + 1) * P], mean_w[:, 0:1],
                                                   start=j == 0, stop=j == SLOTS - 1)
                    ins.then_inc(var_ready, 1)
                    pe.wait_ge(x1_ready, g + CREDIT)
                    for t in range(GT):
                        for j in range(SLOTS):
                            ins = nc.tensor.matmul(po[:, t, 0:D], yt[v][:, j, t * P:(t + 1) * P], wo[:, j, :],
                                                   start=j == 0, stop=j == SLOTS - 1)
                    ins.then_inc(projected, 1)
                    pe.wait_ge(normed, g + 1)
                    pe.wait_ge(copied, g + 1)
                    for t in range(GT):
                        for d in range(DC):
                            ins = nc.tensor.transpose(pt[:, d, t * P:(t + 1) * P], xn[:, t, d * P:(d + 1) * P], ident[:, :])
                    ins.then_inc(turned, 1)
                    pe.wait_ge(copied, g + 2)
                    pe.wait_ge(taken, g + 1)
                    for t in range(GT):
                        out = pg[:, t * EX:(t + 1) * EX]
                        for d in range(DC):
                            nc.tensor.matmul(out, xt[:, d, t * P:(t + 1) * P], gw[:, d, :], start=d == 0, stop=False)
                        ins = nc.tensor.matmul(out, ones[0:1, :], gb[:, :], start=False, stop=True)
                    ins.then_inc(scored, 1)

        @block.scalar
        def _(act):
            act.sem_inc(copied, 1)
            act.sem_inc(rooted, 1)
            for v in range(2):
                act.sem_inc(x_out[v], 16)
                act.sem_inc(t_out[v], 32)
            act.wait_ge(eps_set, 2)
            with act.Fori(0, NG // 2) as i:
                for v in range(2):
                    g = i * 2 + v
                    act.wait_ge(centred, g + 1)
                    nc.scalar.activation(sq[:, :, :], yt[v][:, :, :], ACT.Square).then_inc(squared, 1)
                    act.wait_ge(var_ready, g + 1)
                    nc.scalar.activation(ystd[:, :], pm[:, G:G + GT], ACT.Sqrt, bias=epst[:, :]).then_inc(rooted, 1)
                    act.wait_ge(x1_ready, ready(g))
                    act.dma_start(x1g[g], xo[v][:, :, :]).then_inc(x_out[v], 16)
                    act.wait_ge(nvar_ready, g + 1)
                    nc.scalar.activation(std[:, 1, :], std[:, 0, :], ACT.Sqrt, bias=epst[:, :]).then_inc(nstd_ready, 1)
                    act.wait_ge(turned, g + 2)
                    act.wait_ge(lo_ready, g + 1)
                    act.wait_ge(scored, g + 1)
                    nc.scalar.copy(xt[:, :, :], pt[:, :, 0:G]).then_inc(copied, 1)
                    act.wait_ge(copied, g + 2)
                    act.wait_ge(t_out[v], i * 32 + 32)
                    nc.scalar.copy(hi[v][:, :, :], xt[:, :, :]).then_inc(hi_ready, 1)
                    act.wait_ge(hi_ready, g + 1)
                    act.dma_start(th[:, :, bass.ds(g * G, G)], hi[v][:, :, :]).then_inc(t_out[v], 16)
                    act.wait_ge(lo_ready, g + 2)
                    act.dma_start(tl[:, :, bass.ds(g * G, G)], lo[v][:, :, :]).then_inc(t_out[v], 16)
            for v in range(2):
                act.wait_ge(x_out[v], 16 * (NG // 2 + 1))
                act.wait_ge(t_out[v], 32 * (NG // 2 + 1))


HALF = HID // 2
HT = HALF // P
PAIRS = HT // 2
W_SCALE = 64.0


def moe(nc, c, w, x1, th, tl, scores, x2):
    with Stage(nc, "m") as s:
        acc = s.sb("acc", [P, NT, D])
        xh, xl = s.sb("xh", [P, DC, T], F16), s.sb("xl", [P, DC, T], F16)
        w1s, w2s = s.sb("w1s", [P, DC, HALF]), s.sb("w2s", [P, HT, D])
        w1h, w1l, w2h, w2l = ([s.sb(f"{x}{v}", shape, F16) for v in range(2)] for x, shape in (
            ("w1h", [P, DC, HALF]), ("w1l", [P, DC, HALF]), ("w2h", [P, HT, D]), ("w2l", [P, HT, D])))
        b1, b2, ones = s.sb("b1", [P, EX * 2 * HT]), s.sb("b2", [1, EX * D]), s.sb("ones", [1, P])
        act_out = [s.sb(f"act_out{v}", [P, 2, G]) for v in range(2)]
        hh, hl = ([s.sb(f"{x}{v}", [P, HT, G], F16) for v in range(2)] for x in ("hh", "hl"))
        sc, gate, rank = s.sb("sc", [P, NT, EX]), s.sb("gate", [P, NT, EX]), s.sb("rank", [P, NT, EX])
        row, above = s.sb("row", [P, NT]), s.sb("above", [P, NT])
        ph = [s.ps(f"ph{v}", [P, 2, BANK]) for v in range(2)]
        py = s.ps("py", [P, GT, BANK])
        (loaded, x_in, acc_in, w_in, split, h_ready, gelu, parted, y_ready, added, stored, steps, shifted, expd, ones_set,
         held, parts, high, pe_held, pool_held) = (s.sem(x) for x in "loaded x_in acc_in w_in split h_ready gelu parted y_ready added stored steps shifted "
                   "expd ones_set held parts high pe_held pool_held".split())
        block = s.block()
        UNIT = NG * GT
        Y_CREDIT = 2 * UNIT

        @block.sync
        def _(sp):
            for tile, src in ((sc[:, :, :], scores), (b1[:, :], w["b1"]), (b2[:, :], w["b2"])):
                sp.dma_start(tile, src).then_inc(loaded, 16)
            sp.dma_start(w1s[:, :, :], w["w1"][0, 0]).then_inc(w_in, 16)
            sp.dma_start(w2s[:, :, :], w["w2"][0, 0]).then_inc(w_in, 16)
            sp.dma_start(xh[:, :, :], th).then_inc(x_in, 16)
            sp.dma_start(xl[:, :, :], tl).then_inc(x_in, 16)
            sp.dma_start(acc[:, :, :], x1.rearrange("(n p) d -> p n d", p=P)).then_inc(acc_in, 16)
            sp.wait_ge(split, 1)
            sp.dma_start(w1s[:, :, :], w["w1"][0, 1]).then_inc(w_in, 16)
            sp.dma_start(w2s[:, :, :], w["w2"][0, 1]).then_inc(w_in, 16)
            with sp.Fori(1, EX) as e:
                for v in range(2):
                    sp.wait_ge(split, e * 2 + v)
                    sp.dma_start(w1s[:, :, :], w["w1"][e, v]).then_inc(w_in, 16)
                    sp.dma_start(w2s[:, :, :], w["w2"][e, v]).then_inc(w_in, 16)
            sp.wait_ge(added, EX * 2 * UNIT + GT)
            sp.dma_start(x2.rearrange("(n p) d -> p n d", p=P), acc[:, :, :]).then_inc(stored, 16)
            sp.wait_ge(stored, 16)

        @block.gpsimd
        def _(pool):
            with pool.Fori(0, EX) as e:
                for v in range(2):
                    unit = e * 2 + v
                    pool.wait_ge(w_in, unit * 32 + 32)
                    pool.wait_ge(y_ready, unit * UNIT + UNIT)
                    settle(pool, pool_held)
                    for part, whole in ((w1h, w1s), (w2h, w2s)):
                        nc.gpsimd.tensor_scalar(part[v][:, :, :], whole[:, :, :], W_SCALE, 1.0, ALU.mult, ALU.mult)
                        nc.gpsimd.tensor_scalar(whole[:, :, :], whole[:, :, :], W_SCALE, 1.0, ALU.mult, ALU.mult).then_inc(parts, 1)
                    pool.wait_ge(parts, unit * 2 + 2)
                    nc.gpsimd.tensor_tensor(w1l[v][:, :, :], w1s[:, :, :], w1h[v][:, :, :], ALU.subtract)
                    nc.gpsimd.tensor_tensor(w2l[v][:, :, :], w2s[:, :, :], w2h[v][:, :, :], ALU.subtract).then_inc(split, 1)

        @block.tensor
        def _(pe):
            pe.sem_inc(y_ready, Y_CREDIT)
            pe.wait_ge(loaded, 48)
            pe.wait_ge(ones_set, 2)
            pe.wait_ge(x_in, 32)
            with pe.Fori(0, EX) as e:
                for half in range(2):
                    pe.wait_ge(split, e * 2 + half + 1)
                    settle(pe, pe_held)
                    with pe.Fori(0, NG // 2) as i:
                        turn0 = (e * 2 + half) * NG + i * 2

                        def hidden(v):
                            cols = bass.ds((i * 2 + v) * G, G)
                            for jj in range(PAIRS):
                                pe.wait_ge(gelu, (turn0 + v) * PAIRS + jj + 1)
                                for j in (2 * jj, 2 * jj + 1):
                                    terms = [(a, b, d) for a, b in ((w1h, xh), (w1h, xl), (w1l, xh)) for d in range(DC)]
                                    for n, (a, b, d) in enumerate(terms):
                                        ins = nc.tensor.matmul(ph[(v * PAIRS + jj) % 2][:, j % 2, 0:G],
                                                               a[half][:, d, j * P:(j + 1) * P], b[:, d, cols],
                                                               start=n == 0, stop=n == len(terms) - 1)
                                ins.then_inc(h_ready, 1)

                        def outputs(v):
                            pe.wait_ge(parted, (turn0 + v) * PAIRS + PAIRS + CREDIT)
                            for t in range(GT):
                                pe.wait_ge(added, (turn0 + v) * GT + t + 1)
                                if half == 0:
                                    settle(pe, pe_held)
                                    nc.tensor.matmul(py[:, t, 0:D], ones[:, :], b2[:, bass.ds(e * D, D)], start=True, stop=False)
                                terms = [(a, b, j) for a, b in ((hh, w2h), (hl, w2h), (hh, w2l)) for j in range(HT)]
                                for n, (a, b, j) in enumerate(terms):
                                    ins = nc.tensor.matmul(py[:, t, 0:D], a[v][:, j, t * P:(t + 1) * P], b[half][:, j, :],
                                                           start=n == 0 and half == 1, stop=n == len(terms) - 1)
                                ins.then_inc(y_ready, 1)

                        hidden(0)
                        hidden(1)
                        outputs(0)
                        outputs(1)

        @block.scalar
        def _(act):
            act.sem_inc(gelu, CREDIT)
            act.wait_ge(loaded, 48)
            act.wait_ge(shifted, 1)
            nc.scalar.activation(sc[:, :, :], sc[:, :, :], ACT.Exp).then_inc(expd, 1)
            with act.Fori(0, EX) as e:
                for half in range(2):
                    with act.Fori(0, NG // 2) as i:
                        for v in range(2):
                            for jj in range(PAIRS):
                                n = ((e * 2 + half) * NG + i * 2 + v) * PAIRS + jj
                                b = (v * PAIRS + jj) % 2
                                act.wait_ge(parted, n + 1)
                                act.wait_ge(h_ready, n + 1)
                                settle(act, held)
                                for j in range(2):
                                    ins = nc.scalar.activation(act_out[b][:, j, :], ph[b][:, j, 0:G], ACT.Gelu, scale=1.0 / W_SCALE,
                                                               bias=b1[:, bass.ds(e * (2 * HT) + (half * HT + 2 * jj + j), 1)])
                                ins.then_inc(gelu, 1)

        @block.vector
        def _(dve):
            dve.sem_inc(parted, CREDIT)
            dve.sem_inc(added, GT)
            dve.wait_ge(loaded, 48)
            nc.vector.memset(ones[:, :], 1.0).then_inc(ones_set, 1)
            nc.vector.tensor_scalar(b2[:, :], b2[:, :], W_SCALE, None, ALU.mult).then_inc(ones_set, 1)
            chain = Chain(dve, steps, None)
            chain(nc.vector.tensor_reduce(row[:, :], sc[:, :, :], AX.X, ALU.max))

            def by_expert(t):
                return t[:, :].rearrange("p (n a) -> p n a", a=1).to_broadcast([P, NT, EX])

            nc.vector.tensor_tensor(sc[:, :, :], sc[:, :, :], by_expert(row), ALU.subtract).then_inc(shifted, 1)
            dve.wait_ge(expd, 1)
            chain(nc.vector.tensor_reduce(row[:, :], sc[:, :, :], AX.X, ALU.add))
            chain(nc.vector.reciprocal(row[:, :], row[:, :]))
            chain(nc.vector.tensor_tensor(sc[:, :, :], sc[:, :, :], by_expert(row), ALU.mult))
            for j in range(EX):
                ins = nc.vector.memset(rank[:, :, j], float(j))
            chain(ins)
            for i in range(EX):
                for j in range(i + 1, EX):
                    chain(nc.vector.tensor_tensor(above[:, :], sc[:, :, j], sc[:, :, i], ALU.is_gt))
                    chain(nc.vector.tensor_tensor(rank[:, :, i], rank[:, :, i], above[:, :], ALU.add))
                    chain(nc.vector.tensor_tensor(rank[:, :, j], rank[:, :, j], above[:, :], ALU.subtract))
            chain(nc.vector.tensor_scalar(rank[:, :, :], rank[:, :, :], 2.0, None, ALU.is_lt))
            chain(nc.vector.tensor_tensor(sc[:, :, :], sc[:, :, :], rank[:, :, :], ALU.mult))
            chain(nc.vector.tensor_reduce(row[:, :], sc[:, :, :], AX.X, ALU.add))
            chain(nc.vector.tensor_scalar(row[:, :], row[:, :], 1e-9, None, ALU.add))
            chain(nc.vector.reciprocal(row[:, :], row[:, :]))
            chain(nc.vector.tensor_tensor(gate[:, :, :], sc[:, :, :], by_expert(row), ALU.mult))
            chain(nc.vector.tensor_scalar(gate[:, :, :], gate[:, :, :], 1.0 / W_SCALE, None, ALU.mult))
            dve.wait_ge(acc_in, 16)
            with dve.Fori(0, EX) as e:
                for half in range(2):
                    with dve.Fori(0, NG // 2) as i:
                        turn0 = (e * 2 + half) * NG + i * 2

                        def part(v):
                            dve.wait_ge(y_ready, (turn0 + v) * GT + (Y_CREDIT - GT))
                            for jj in range(PAIRS):
                                n, b = (turn0 + v) * PAIRS + jj, (v * PAIRS + jj) % 2
                                at = slice(2 * jj, 2 * jj + 2)
                                dve.wait_ge(gelu, n + 1 + CREDIT)
                                nc.vector.tensor_copy(hh[v][:, at, :], act_out[b][:, :, :]).then_inc(high, 1)
                                dve.wait_ge(high, n + 1)
                                nc.vector.tensor_tensor(hl[v][:, at, :], act_out[b][:, :, :], hh[v][:, at, :],
                                                        ALU.subtract).then_inc(parted, 1)

                        def add(v):
                            for t in range(GT):
                                n = (turn0 + v) * GT + t
                                tile = (i * 2 + v) * GT + t
                                dve.wait_ge(y_ready, n + 1 + Y_CREDIT)
                                into = acc[:, bass.ds(tile, 1), :].rearrange("p a d -> p (a d)")
                                nc.vector.scalar_tensor_tensor(out=into, in0=py[:, t, 0:D],
                                                               scalar=gate[:, bass.ds(tile, 1), bass.ds(e, 1)].rearrange("p a b -> p (a b)"), in1=into,
                                                               op0=ALU.mult, op1=ALU.add).then_inc(added, 1)

                        part(0)
                        part(1)
                        add(0)
                        add(1)


def mamba_gate(nc, c, w, x, xn_ch, sz, dt_raw):
    src_g, sz_g = tok_groups(x), tok_groups(sz)
    with Stage(nc, "g") as s:
        ident, epst = s.sb("ident", [P, P]), s.sb("eps", [P, 1])
        wz, wdt = s.sb("wz", [P, DC, DIN]), s.sb("wdt", [P, DC, HEADS])
        xin = [s.sb(f"x{u}", [P, GT, D]) for u in range(2)]
        xn = [s.sb(f"xn{u}", [P, GT, D]) for u in range(2)]
        xt = [s.sb(f"xt{u}", [P, DC, G]) for u in range(2)]
        szt = [s.sb(f"szt{u}", [P, GT, DIN]) for u in range(2)]
        raw = s.sb("raw", [P, NT, HEADS])
        stats, mv = s.sb("stats", [P, GT, 6]), s.sb("mv", [P, GT, 2])
        std, rstd = s.sb("std", [P, 2, GT]), s.sb("rstd", [P, GT])
        pt = s.ps("pt", [P, DC, BANK])
        pz = [s.ps(f"pz{v}", [P, 2, BANK]) for v in range(2)]
        pdt = s.ps("pdt", [P, BANK])
        x_in, xt_out, sz_out = ([s.sem(f"{x}{u}") for u in range(2)] for x in ("x_in", "xt_out", "sz_out"))
        (loaded, eps_set, var_ready, std_ready, normed, steps, turned, copied, z_ready, gated, dt_ready, dt_taken, held,
         dt_out) = (s.sem(x) for x in "loaded eps_set var_ready std_ready normed steps turned copied z_ready gated dt_ready "
                    "dt_taken held dt_out".split())
        block = s.block()

        @block.sync
        def _(sp):
            for tile, src in ((ident[:, :], c["ident"]), (wz[:, :, :], w["w_z"]), (wdt[:, :, :], w["w_dt"])):
                sp.dma_start(tile, src).then_inc(loaded, 16)
            with sp.Fori(0, NG // 2) as i:
                for u in range(2):
                    g = i * 2 + u
                    sp.wait_ge(normed, free(g))
                    sp.dma_start(xin[u][:, :, :], src_g[g]).then_inc(x_in[u], 16)
            sp.wait_ge(dt_taken, NG + 1)
            sp.dma_start(dt_raw, raw[:, :, :]).then_inc(dt_out, 16)
            sp.wait_ge(dt_out, 16)

        @block.vector
        def _(dve):
            nc.vector.memset(epst[:, :], 1e-6).then_inc(eps_set, 1)
            dve.sem_inc(normed, CREDIT)
            dve.sem_inc(dt_taken, 1)
            chain = Chain(dve, steps, NORM_STEPS)
            with dve.Fori(0, NG // 2) as i:
                for u in range(2):
                    g = i * 2 + u
                    chain.start(g)
                    dve.wait_ge(x_in[u], i * 16 + 16)
                    dve.wait_ge(turned, free(g))
                    norm_steps(dve, chain, xin[u], stats, mv, std, rstd, xn[u], var_ready, std_ready, g,
                               held).then_inc(normed, 1)
                    dve.wait_ge(dt_ready, g + 1)
                    settle(dve, held)
                    nc.vector.tensor_copy(raw[:, bass.ds(g * GT, GT), :],
                                          pdt[:, 0:GT * HEADS].rearrange("p (t h) -> p t h", h=HEADS)).then_inc(dt_taken, 1)

        @block.tensor
        def _(pe):
            pe.sem_inc(turned, CREDIT)
            pe.wait_ge(loaded, 48)
            with pe.Fori(0, NG // 2) as i:
                for u in range(2):
                    g = i * 2 + u
                    pe.wait_ge(normed, ready(g))
                    for t in range(GT):
                        for d in range(DC):
                            ins = nc.tensor.transpose(pt[:, d, t * P:(t + 1) * P], xn[u][:, t, d * P:(d + 1) * P],
                                                      ident[:, :])
                    ins.then_inc(turned, 1)
                    pe.wait_ge(copied, ready(g))
                    pe.wait_ge(dt_taken, g + 1)
                    for t in range(GT):
                        for d in range(DC):
                            ins = nc.tensor.matmul(pdt[:, t * HEADS:(t + 1) * HEADS], xt[u][:, d, t * P:(t + 1) * P],
                                                   wdt[:, d, :], start=d == 0, stop=d == DC - 1)
                    ins.then_inc(dt_ready, 1)
                    for t in range(GT):
                        v = (u * GT + t) % 2
                        pe.wait_ge(gated, free(g * GT + t))
                        for half in range(2):
                            for d in range(DC):
                                ins = nc.tensor.matmul(pz[v][:, half, 0:D], xt[u][:, d, t * P:(t + 1) * P],
                                                       wz[:, d, half * D:(half + 1) * D], start=d == 0, stop=d == DC - 1)
                        ins.then_inc(z_ready, 1)

        @block.scalar
        def _(act):
            act.sem_inc(copied, CREDIT)
            act.sem_inc(gated, CREDIT)
            for u in range(2):
                act.sem_inc(xt_out[u], 16)
                act.sem_inc(sz_out[u], 16)
            act.wait_ge(eps_set, 1)
            with act.Fori(0, NG // 2) as i:
                for u in range(2):
                    g = i * 2 + u
                    act.wait_ge(var_ready, g + 1)
                    nc.scalar.activation(std[:, 1, :], std[:, 0, :], ACT.Sqrt, bias=epst[:, :]).then_inc(std_ready, 1)
                    act.wait_ge(turned, ready(g))
                    act.wait_ge(xt_out[u], i * 16 + 16)
                    nc.scalar.copy(xt[u][:, :, :], pt[:, :, 0:G]).then_inc(copied, 1)
                    act.wait_ge(copied, ready(g))
                    act.dma_start(xn_ch[:, :, bass.ds(g * G, G)], xt[u][:, :, :]).then_inc(xt_out[u], 16)
                    act.wait_ge(sz_out[u], i * 16 + 16)
                    for t in range(GT):
                        v = (u * GT + t) % 2
                        act.wait_ge(z_ready, g * GT + t + 1)
                        nc.scalar.activation(szt[u][:, t, :].rearrange("p (a d) -> p a d", a=2), pz[v][:, :, 0:D],
                                             ACT.Silu).then_inc(gated, 1)
                    act.wait_ge(gated, g * GT + GT + CREDIT)
                    act.dma_start(sz_g[g], szt[u][:, :, :]).then_inc(sz_out[u], 16)
            for u in range(2):
                act.wait_ge(xt_out[u], 16 * (NG // 2 + 1))
                act.wait_ge(sz_out[u], 16 * (NG // 2 + 1))


CT = -(-CONV // P)


def mamba_conv(nc, w, xn_ch, xbc):
    with Stage(nc, "v") as s:
        xn = s.sb("xn", [P, IMAGES, DC, L])
        wct = [s.sb(f"wct{b}", [P, DC, P]) for b in range(IMAGES)]
        taps, bias = s.sb("taps", [P, CT, 9]), s.sb("bias", [P, CT])
        pad = [s.sb(f"pad{b}", [P, SIDE + 2, SIDE + 2]) for b in range(IMAGES)]
        acc = [s.sb(f"acc{b}", [P, L]) for b in range(IMAGES)]
        out = [s.sb(f"out{b}", [P, L]) for b in range(IMAGES)]
        pi = [s.ps(f"pi{v}", [P, BANK]) for v in range(2)]
        w_in, stored = ([s.sem(f"{x}{b}") for b in range(IMAGES)] for x in ("w_in", "stored"))
        loaded, xn_in, zeroed, projected, padded, tapped, convolved, active, held, pe_held = (s.sem(x) for x in (
            "loaded xn_in zeroed projected padded tapped convolved active held pe_held".split()))
        block = s.block()

        @block.sync
        def _(sp):
            for b in range(IMAGES):
                sp.sem_inc(stored[b], 16)
            sp.dma_start(taps[:, :, :], w["conv1"]).then_inc(loaded, 16)
            sp.dma_start(bias[:, :], w["conv1_b"]).then_inc(loaded, 16)
            for b in range(IMAGES):
                sp.dma_start(wct[b][:, :, :], w["w_x"][0]).then_inc(w_in[b], 16)
                sp.dma_start(xn[:, b, :, :], xn_ch[:, :, b * L:(b + 1) * L]).then_inc(xn_in, 16)
            with sp.Fori(1, CT) as ct:
                for b in range(IMAGES):
                    turn = ct * 2 + b
                    sp.wait_ge(projected, (turn - 1) * GI + CREDIT)
                    sp.dma_start(wct[b][:, :, :], w["w_x"][ct]).then_inc(w_in[b], 16)
                    sp.wait_ge(active, turn - 2 + CREDIT + 1)
                    sp.dma_start(xbc[ct - 1, :, b * L:(b + 1) * L], out[b][:, :]).then_inc(stored[b], 16)
            for b in range(IMAGES):
                sp.wait_ge(active, ready(2 * (CT - 1) + b))
                sp.dma_start(xbc[CT - 1, :, b * L:(b + 1) * L], out[b][:, :]).then_inc(stored[b], 16)
            for b in range(IMAGES):
                sp.wait_ge(stored[b], 16 * (CT + 1))

        @block.gpsimd
        def _(pool):
            for b in range(IMAGES):
                nc.gpsimd.memset(pad[b][:, :, :], 0.0).then_inc(zeroed, 1)

        @block.tensor
        def _(pe):
            pe.sem_inc(projected, CREDIT)
            with pe.Fori(0, CT) as ct:
                for b in range(IMAGES):
                    pe.wait_ge(w_in[b], ct * 16 + 16)
                    pe.wait_ge(xn_in, 32)
                    settle(pe, pe_held)
                    with pe.Fori(0, GI // 2) as i:
                        for v in range(2):
                            q = i * 2 + v
                            pe.wait_ge(padded, free((ct * 2 + b) * GI + q))
                            for d in range(DC):
                                ins = nc.tensor.matmul(pi[v][:, 0:G], wct[b][:, d, :], xn[:, b, d, bass.ds(q * G, G)],
                                                       start=d == 0, stop=d == DC - 1)
                            ins.then_inc(projected, 1)

        @block.vector
        def _(dve):
            dve.sem_inc(convolved, CREDIT)
            dve.wait_ge(loaded, 32)
            chain = Chain(dve, tapped, 8)
            with dve.Fori(0, CT) as ct:
                for b in range(IMAGES):
                    turn = ct * 2 + b
                    chain.start(turn)
                    dve.wait_ge(padded, (turn + 1) * GI + CREDIT)
                    dve.wait_ge(active, turn + 1)
                    view = acc[b][:, :].rearrange("p (h w) -> p h w", w=SIDE)
                    for t in range(9):
                        tap = taps[:, bass.ds(ct, 1), t:t + 1].rearrange("p a b -> p (a b)")
                        rows = pad[b][:, t // 3:t // 3 + SIDE, t % 3:t % 3 + SIDE]
                        if t == 0:
                            ins = nc.vector.tensor_scalar(view, rows, tap, None, ALU.mult)
                        else:
                            ins = nc.vector.scalar_tensor_tensor(out=view, in0=rows, scalar=tap, in1=view,
                                                                 op0=ALU.mult, op1=ALU.add)
                        if t < 8:
                            chain(ins)
                    ins.then_inc(convolved, 1)

        @block.scalar
        def _(act):
            act.sem_inc(padded, CREDIT)
            act.sem_inc(active, 2)
            act.wait_ge(loaded, 32)
            act.wait_ge(zeroed, 2)

            def copies(ct, b):
                turn = ct * 2 + b
                act.wait_ge(convolved, free(turn))
                settle(act, held)
                with act.Fori(0, GI // 2) as i:
                    for v in range(2):
                        q = i * 2 + v
                        act.wait_ge(projected, ready(turn * GI + q))
                        settle(act, held)
                        nc.scalar.copy(pad[b][:, bass.ds(q * ROWS + 1, ROWS), 1:SIDE + 1],
                                       pi[v][:, 0:G].rearrange("p (h w) -> p h w", w=SIDE)).then_inc(padded, 1)

            def silu(ct, b):
                act.wait_ge(convolved, ready(ct * 2 + b))
                act.wait_ge(stored[b], ct * 16 + 16)
                settle(act, held)
                nc.scalar.activation(out[b][:, :], acc[b][:, :], ACT.Silu, bias=bias[:, bass.ds(ct, 1)]).then_inc(active, 1)

            copies(0, 0)
            copies(0, 1)
            silu(0, 0)
            with act.Fori(1, CT) as ct:
                copies(ct, 0)
                silu(ct - 1, 1)
                copies(ct, 1)
                silu(ct, 0)
            silu(CT - 1, 1)


NQ = L // P
HH = HEADS // 2
B_AT, CUM, SUF, TOT, SMALL = P, P + NS, P + NS + HEADS, P + NS + 2 * HEADS, P + NS + 3 * HEADS


def mamba_scan(nc, c, w, x, sz, dt_raw, xbc, out):
    with Stage(nc, "s") as s:
        ident, upto, beyond = s.sb("ident", [P, P]), s.sb("upto", [P, P]), s.sb("beyond", [P, P])
        ones = s.sb("ones", [P, P])
        wo = s.sb("wo", [P, SLOTS, D])
        d1, gamma, beta = s.sb("d1", [P, DIN]), s.sb("gamma", [P, DIN]), s.sb("beta", [P, DIN])
        dtb, alog, epst = s.sb("dtb", [P, HEADS]), s.sb("alog", [P, HEADS]), s.sb("eps", [P, 1])
        ln_one = s.sb("ln_one", [P, 2])
        raw, e, one_e, ln, corr = (s.sb(x, [P, NT, HEADS]) for x in ("raw", "e", "one_e", "ln", "corr"))
        da = s.sb("da", [P, NT, 2 * HEADS])

        def both(name, shape):
            return [s.sb(f"{name}{b}", shape) for b in range(IMAGES)]

        xc, bt, ctr = both("xc", [P, SLOTS, P]), both("bt", [NS, P]), both("ct", [NS, P])
        szt, xin, xo = both("szt", [P, DIN]), both("xin", [P, D]), both("xo", [P, D])
        dab, r = both("dab", [P, 2 * HEADS]), both("r", [P, HEADS, P])
        xs, xdt, xde, xd1 = both("xs", [P, DIN]), both("xdt", [P, DIN]), both("xde", [P, DIN]), both("xd1", [P, DIN])
        gs, es = both("gs", [P, SMALL]), both("es", [P, 3 * HEADS])
        y, state, yts = both("y", [P, DIN]), both("state", [NS, DIN]), both("yts", [P, SLOTS, P])
        gm, ex, m = s.sb("gm", [P, P]), s.sb("ex", [P, HEADS, P]), s.sb("m", [P, HEADS, P])
        stats, mv, lnv, rstd = s.sb("stats", [P, 2, 6]), s.sb("mv", [P, 2]), s.sb("lnv", [P, 2]), s.sb("rstd", [P, 1])
        px, psm, pd, py = (s.ps("px", [P, 2, BANK]), s.ps("psm", [P, BANK]), s.ps("pd", [P, 3, BANK]),
                           s.ps("py", [P, 2, BANK]))
        xc_in, tok_in, xo_out = ([s.sem(f"{x}{b}") for b in range(IMAGES)] for x in ("xc_in", "tok_in", "xo_out"))
        (loaded, set_up, a_exp, e_ready, one_ready, ln_ready, steps0, prepared, x_turned, x_copied, sums_ready, gs_ready,
         es_ready, d_ready, ex_ready, dab_ready, r_ready, xd_ready, xde_ready, xdt_ready, m_ready, ydiag, yoff, ds_ready,
         weighed, updated, steps, var_ready, rstd_ready, gated, yt_ready, yt_copied, out_ready, added, held, act_steps,
         pool_held, pe_held, one_set, gm_ready) = (s.sem(x) for x in (
             "loaded set_up a_exp e_ready one_ready ln_ready steps0 prepared x_turned x_copied sums_ready gs_ready "
             "es_ready d_ready ex_ready dab_ready r_ready xd_ready xde_ready xdt_ready m_ready ydiag yoff ds_ready "
             "weighed updated steps var_ready rstd_ready gated yt_ready yt_copied out_ready added held act_steps "
             "pool_held pe_held one_set gm_ready").split())
        block = s.block()

        def heads(t):
            return t.rearrange("p (h a) -> p h a", a=1).to_broadcast([P, HEADS, HP])

        def by_head(t):
            return t[:, :].rearrange("p (h c) -> p h c", h=HEADS)

        def banks(t):
            return t.rearrange("p (a d) -> p a d", a=2)

        @block.sync
        def _(sp):
            for tile, src in ((raw[:, :, :], dt_raw), (dtb[:, :], w["dt1_b"]), (alog[:, :], w["a1_log"]),
                              (ident[:, :], c["ident"]), (upto[:, :], c["upto"]), (beyond[:, :], c["beyond"]),
                              (d1[:, :], w["d1"]), (gamma[:, :], w["gamma"]), (beta[:, :], w["beta"]), (wo[:, :, :], w["w_out1"])):
                sp.dma_start(tile, src).then_inc(loaded, 16)
            xt, szg, xg, og = (a.rearrange("(b q p) d -> b q p d", b=IMAGES, p=P) for a in (x, sz, x, out))
            bc_rows = xbc[SLOTS]

            def load(q, b):
                at = bass.ds(q * P + b * L, P)
                sp.wait_ge(x_turned, free(q * 2 + b))
                sp.wait_ge(yoff, q * 2 + b + CREDIT - 1)
                sp.dma_start(xc[b][:, :, :], xbc[0:SLOTS].rearrange("s p t -> p s t")[:, :, at]).then_inc(xc_in[b], 16)
                sp.dma_start(bt[b][:, :], bc_rows[0:NS, at]).then_inc(xc_in[b], 16)
                sp.dma_start(ctr[b][:, :], bc_rows[NS:2 * NS, at]).then_inc(xc_in[b], 16)

            def load_tok(q, b):
                sp.wait_ge(added, free(q * 2 + b))
                sp.dma_start(szt[b][:, :], szg[b, q]).then_inc(tok_in[b], 16)
                sp.dma_start(xin[b][:, :], xg[b, q]).then_inc(tok_in[b], 16)

            for b in range(IMAGES):
                sp.sem_inc(xo_out[b], 16)
                load(0, b)
                load_tok(0, b)
            with sp.Fori(1, NQ) as q:
                for b in range(IMAGES):
                    load(q, b)
                    load_tok(q, b)
                    sp.dma_start(og[b, q - 1], xo[b][:, :]).then_inc(xo_out[b], 16)
            for b in range(IMAGES):
                sp.wait_ge(added, free(NQ * 2 + b))
                sp.dma_start(og[b, NQ - 1], xo[b][:, :]).then_inc(xo_out[b], 16)
            for b in range(IMAGES):
                sp.wait_ge(xo_out[b], 16 * (NQ + 1))

        @block.tensor
        def _(pe):
            pe.sem_inc(x_turned, CREDIT)
            pe.sem_inc(d_ready, CREDIT)
            pe.sem_inc(yoff, CREDIT)
            pe.wait_ge(loaded, 160)
            pe.wait_ge(set_up, 4)

            def front(q, b):
                turn = q * 2 + b
                pe.wait_ge(xc_in[b], q * 48 + 48)
                pe.wait_ge(weighed, turn + 1)
                for j in range(SLOTS):
                    ins = nc.tensor.transpose(px[:, j // DC, (j % DC) * P:(j % DC + 1) * P], xc[b][:, j, :], ident[:, :])
                ins.then_inc(x_turned, 1)
                pe.wait_ge(gs_ready, turn + 1)
                pe.wait_ge(dab_ready, turn + CREDIT + 1)
                settle(pe, pe_held)
                a = dab[b][:, HEADS:2 * HEADS]
                nc.tensor.matmul(psm[:, 0:P], bt[b][:, :], ctr[b][:, :], start=True, stop=True)
                nc.tensor.transpose(psm[:, B_AT:CUM], bt[b][:, :], ident[0:NS, 0:NS])
                nc.tensor.matmul(psm[:, CUM:SUF], upto[:, :], a, start=True, stop=True)
                nc.tensor.matmul(psm[:, SUF:TOT], beyond[:, :], a, start=True, stop=True)
                nc.tensor.matmul(psm[:, TOT:SMALL], ones[:, :], a, start=True, stop=True).then_inc(sums_ready, 1)
                pe.wait_ge(r_ready, turn + 1)
                pe.wait_ge(updated, turn + 1)
                for j in range(3):
                    ins = nc.tensor.matmul(pd[:, j, :], beyond[:, :], r[b][:, 4 * j:4 * j + 4, :], start=True, stop=True)
                ins.then_inc(d_ready, 1)

            def middle(q, b):
                turn = q * 2 + b
                pe.wait_ge(m_ready, ready(turn))
                pe.wait_ge(added, turn + CREDIT)
                for h in range(HEADS):
                    at = (h % HH) * HP
                    ins = nc.tensor.matmul(py[:, h // HH, at:at + HP], m[:, h, :], xdt[b][:, h * HP:(h + 1) * HP],
                                           start=True, stop=True)
                ins.then_inc(ydiag, 1)
                for half in range(2):
                    ins = nc.tensor.matmul(px[:, half, 0:D], ctr[b][:, :], state[b][:, half * D:(half + 1) * D], start=True, stop=True)
                ins.then_inc(yoff, 1)
                pe.wait_ge(xde_ready, turn + 1)
                for half in range(2):
                    ins = nc.tensor.matmul(pd[0:NS, half, 0:D], gs[b][:, B_AT:CUM], xde[b][:, half * D:(half + 1) * D],
                                           start=True, stop=True)
                ins.then_inc(ds_ready, 1)

            def tail(q, b):
                turn = q * 2 + b
                pe.wait_ge(gated, turn + 1)
                for j in range(SLOTS):
                    ins = nc.tensor.transpose(py[:, j // DC, (j % DC) * P:(j % DC + 1) * P], y[b][:, j * P:(j + 1) * P], ident[:, :])
                ins.then_inc(yt_ready, 1)
                pe.wait_ge(yt_copied, turn + 1)
                for j in range(SLOTS):
                    ins = nc.tensor.matmul(py[:, 0, 0:D], yts[b][:, j, :], wo[:, j, :], start=j == 0, stop=j == SLOTS - 1)
                ins.then_inc(out_ready, 1)

            front(0, 0)
            with pe.Fori(0, NQ - 1) as q:
                for b in range(IMAGES):
                    middle(q, b)
                    front(q + b, 1 - b)
                    tail(q, b)
            middle(NQ - 1, 0)
            front(NQ - 1, 1)
            tail(NQ - 1, 0)
            middle(NQ - 1, 1)
            tail(NQ - 1, 1)

        @block.scalar
        def _(act):
            nc.scalar.preload_act_table_set("natural_log_exp_and_others")
            act.sem_inc(gs_ready, 1)
            act.wait_ge(set_up, 4)
            act.wait_ge(one_set, 1)
            nc.scalar.activation(ln_one[:, 1:2], ln_one[:, 0:1], ACT.Ln)
            act.wait_ge(loaded, 160)
            nc.scalar.activation(alog[:, :], alog[:, :], ACT.Exp).then_inc(a_exp, 1)
            act.wait_ge(steps0, 2)
            nc.scalar.activation(e[:, :, :], e[:, :, :], ACT.Exp, scale=-1.0).then_inc(e_ready, 1)
            act.wait_ge(one_ready, 1)
            nc.scalar.activation(ln[:, :, :], one_e[:, :, :], ACT.Ln).then_inc(ln_ready, 1)
            chain = Chain(act, act_steps, 1)

            def turn_x(q, b):
                act.wait_ge(x_turned, ready(q * 2 + b))
                nc.scalar.copy(banks(xs[b][:, :]), px[:, :, 0:D]).then_inc(x_copied, 1)

            def root(q, b):
                turn = q * 2 + b
                act.wait_ge(var_ready, turn + 1)
                chain.start(turn)
                chain(nc.scalar.activation(lnv[:, 1:2], lnv[:, 0:1], ACT.Ln, bias=epst[:, :]))
                nc.scalar.activation(rstd[:, :], lnv[:, 1:2], ACT.Exp, scale=-0.5).then_inc(rstd_ready, 1)

            def decays(q, b):
                turn = q * 2 + b
                act.wait_ge(sums_ready, turn + 1)
                nc.scalar.copy(gs[b][:, :], psm[:, 0:SMALL]).then_inc(gs_ready, 1)
                act.wait_ge(gs_ready, turn + 2)
                nc.scalar.activation(es[b][:, :], gs[b][:, CUM:SMALL], ACT.Exp).then_inc(es_ready, 1)
                act.wait_ge(d_ready, ready(turn))
                act.wait_ge(m_ready, turn + CREDIT)
                nc.scalar.activation(ex[:, :, :].rearrange("p (j h) l -> p j (h l)", j=3), pd[:, :, :], ACT.Exp).then_inc(ex_ready, 1)

            def turn_y(q, b):
                turn = q * 2 + b
                act.wait_ge(yt_ready, turn + 1)
                nc.scalar.copy(yts[b][:, :, :].rearrange("p (a j) l -> p a (j l)", a=2), py[:, :, 0:D]).then_inc(yt_copied, 1)

            turn_x(0, 0)
            act.wait_ge(sums_ready, 1)
            nc.scalar.copy(gs[0][:, :], psm[:, 0:SMALL]).then_inc(gs_ready, 1)
            act.wait_ge(gs_ready, 2)
            nc.scalar.activation(es[0][:, :], gs[0][:, CUM:SMALL], ACT.Exp).then_inc(es_ready, 1)
            act.wait_ge(d_ready, ready(0))
            nc.scalar.activation(ex[:, :, :].rearrange("p (j h) l -> p j (h l)", j=3), pd[:, :, :], ACT.Exp).then_inc(ex_ready, 1)
            with act.Fori(0, NQ - 1) as q:
                for b in range(IMAGES):
                    turn_x(q + b, 1 - b)
                    root(q, b)
                    decays(q + b, 1 - b)
                    turn_y(q, b)
            turn_x(NQ - 1, 1)
            root(NQ - 1, 0)
            decays(NQ - 1, 1)
            turn_y(NQ - 1, 0)
            root(NQ - 1, 1)
            turn_y(NQ - 1, 1)

        @block.gpsimd
        def _(pool):
            nc.gpsimd.memset(ones[:, :], 1.0).then_inc(set_up, 1)
            nc.gpsimd.memset(epst[:, :], 1e-5).then_inc(set_up, 1)
            nc.gpsimd.memset(state[0][:, :], 0.0).then_inc(set_up, 1)
            nc.gpsimd.memset(state[1][:, :], 0.0).then_inc(set_up, 1)
            pool.sem_inc(dab_ready, CREDIT)
            pool.wait_ge(set_up, 4)
            pool.wait_ge(loaded, 160)
            pool.wait_ge(prepared, 2)
            with pool.Fori(0, NQ) as q:
                for b in range(IMAGES):
                    turn = q * 2 + b
                    pool.wait_ge(m_ready, free(turn))
                    pool.wait_ge(d_ready, free(turn))
                    settle(pool, pool_held)
                    nc.gpsimd.tensor_tensor(dab[b][:, :], da[:, bass.ds(b * NQ + q, 1), :].rearrange("p a h -> p (a h)"),
                                            ones[:, 0:2 * HEADS], ALU.mult).then_inc(dab_ready, 1)
                    pool.wait_ge(dab_ready, ready(turn))
                    nc.gpsimd.tensor_tensor(r[b][:, :, :],
                                            dab[b][:, HEADS:].rearrange("p (h a) -> p h a", a=1).to_broadcast([P, HEADS, P]),
                                            upto[:, :].rearrange("p (a l) -> p a l", a=1).to_broadcast([P, HEADS, P]),
                                            ALU.mult).then_inc(r_ready, 1)
                    pool.wait_ge(x_copied, turn + 1)
                    nc.gpsimd.tensor_tensor(xd1[b][:, :], xs[b][:, :], d1[:, :], ALU.mult).then_inc(xd_ready, 1)
                    pool.wait_ge(xdt_ready, turn + 1)
                    pool.wait_ge(es_ready, turn + 1)
                    nc.gpsimd.tensor_tensor(by_head(xde[b]), by_head(xdt[b]), heads(es[b][:, HEADS:2 * HEADS]),
                                            ALU.mult).then_inc(xde_ready, 1)

        @block.vector
        def _(dve):
            dve.sem_inc(weighed, 1)
            dve.sem_inc(updated, 1)
            dve.sem_inc(added, CREDIT)
            dve.sem_inc(m_ready, CREDIT)
            nc.vector.memset(ln_one[:, 0:1], 1.0).then_inc(one_set, 1)
            dve.wait_ge(loaded, 160)
            once = Chain(dve, steps0, None)

            def tiles(t):
                return t[:, :].rearrange("p (a h) -> p a h", a=1).to_broadcast([P, NT, HEADS])

            once(nc.vector.tensor_tensor(raw[:, :, :], raw[:, :, :], tiles(dtb), ALU.add))
            once(nc.vector.scalar_tensor_tensor(out=e[:, :, :], in0=raw[:, :, :], scalar=-1.0, in1=raw[:, :, :],
                                                op0=ALU.mult, op1=ALU.max))
            dve.wait_ge(e_ready, 1)
            nc.vector.tensor_scalar(one_e[:, :, :], e[:, :, :], 1.0, None, ALU.add).then_inc(one_ready, 1)
            dve.wait_ge(one_ready, 1)
            once(nc.vector.scalar_tensor_tensor(out=corr[:, :, :], in0=one_e[:, :, :], scalar=1.0, in1=e[:, :, :],
                                                op0=ALU.subtract, op1=ALU.subtract))
            dve.wait_ge(ln_ready, 1)
            once(nc.vector.scalar_tensor_tensor(out=corr[:, :, :], in0=ln[:, :, :], scalar=ln_one[:, 1:2], in1=corr[:, :, :],
                                                op0=ALU.subtract, op1=ALU.subtract))
            nc.vector.scalar_tensor_tensor(out=da[:, :, 0:HEADS], in0=raw[:, :, :], scalar=0.0, in1=corr[:, :, :],
                                           op0=ALU.max, op1=ALU.add).then_inc(prepared, 1)
            dve.wait_ge(prepared, 1)
            dve.wait_ge(a_exp, 1)
            nc.vector.scalar_tensor_tensor(out=da[:, :, HEADS:], in0=da[:, :, 0:HEADS], scalar=-1.0, in1=tiles(alog),
                                           op0=ALU.mult, op1=ALU.mult).then_inc(prepared, 1)
            chain = Chain(dve, steps, 9)

            def weights(q, b):
                turn = q * 2 + b
                dve.wait_ge(x_copied, turn + 1)
                dve.wait_ge(dab_ready, ready(turn))
                nc.vector.tensor_tensor(by_head(xdt[b]), by_head(xs[b]), heads(dab[b][:, 0:HEADS]), ALU.mult).then_inc(xdt_ready, 1)
                dve.wait_ge(gs_ready, turn + 2)
                nc.vector.tensor_tensor(gm[:, :], gs[b][:, 0:P], upto[:, :], ALU.mult).then_inc(gm_ready, 1)
                dve.wait_ge(gm_ready, turn + 1)
                dve.wait_ge(ex_ready, turn + 1)
                nc.vector.tensor_tensor(m[:, :, :], ex[:, :, :],
                                        gm[:, :].rearrange("p (a l) -> p a l", a=1).to_broadcast([P, HEADS, P]),
                                        ALU.mult).then_inc(m_ready, 1)

            def outputs(q, b):
                turn = q * 2 + b
                chain.start(turn)
                yv = banks(y[b][:, :])
                dve.wait_ge(yoff, ready(turn))
                dve.wait_ge(es_ready, turn + 1)
                nc.vector.tensor_tensor(y[b][:, :].rearrange("p (a h c) -> p a h c", a=2, h=HH),
                                        px[:, :, 0:D].rearrange("p a (h c) -> p a h c", h=HH),
                                        es[b][:, 0:HEADS].rearrange("p (a h c) -> p a h c", a=2, c=1).to_broadcast([P, 2, HH, HP]),
                                        ALU.mult).then_inc(weighed, 1)
                chain.mark(nc.vector.tensor_tensor(by_head(state[b]), by_head(state[b]),
                                                   es[b][0:NS, 2 * HEADS:].rearrange("p (h a) -> p h a", a=1).to_broadcast([NS, HEADS, HP]),
                                                   ALU.mult))
                dve.wait_ge(weighed, turn + 2)
                dve.wait_ge(ydiag, turn + 1)
                chain(nc.vector.tensor_tensor(yv, yv, py[:, :, 0:D], ALU.add))
                dve.wait_ge(ds_ready, turn + 1)
                sv = banks(state[b][:, :])
                nc.vector.tensor_tensor(sv, sv, pd[0:NS, 0:2, 0:D], ALU.add).then_inc(updated, 1)
                dve.wait_ge(xd_ready, turn + 1)
                chain(nc.vector.tensor_tensor(y[b][:, :], y[b][:, :], xd1[b][:, :], ALU.add))
                for half in range(2):
                    chain.mark(nc.vector.bn_stats(stats[:, half, :], y[b][:, half * D:(half + 1) * D]))
                chain.wait()
                settle(dve, held)
                chain(nc.vector.bn_aggr(mv[:, :], stats[:, :, :]))
                nc.vector.tensor_copy(lnv[:, 0:1], mv[:, 1:2]).then_inc(var_ready, 1)
                dve.wait_ge(rstd_ready, turn + 1)
                chain(nc.vector.tensor_scalar(y[b][:, :], y[b][:, :], mv[:, 0:1], rstd[:, :], ALU.subtract, ALU.mult))
                chain(nc.vector.tensor_tensor(y[b][:, :], y[b][:, :], gamma[:, :], ALU.mult))
                chain(nc.vector.tensor_tensor(y[b][:, :], y[b][:, :], beta[:, :], ALU.add))
                dve.wait_ge(tok_in[b], q * 32 + 32)
                nc.vector.tensor_tensor(y[b][:, :], y[b][:, :], szt[b][:, :], ALU.mult).then_inc(gated, 1)

            def add(q, b):
                dve.wait_ge(out_ready, q * 2 + b + 1)
                dve.wait_ge(xo_out[b], q * 16 + 16)
                nc.vector.tensor_tensor(xo[b][:, :], py[:, 0, 0:D], xin[b][:, :], ALU.add).then_inc(added, 1)

            weights(0, 0)
            with dve.Fori(0, NQ - 1) as q:
                for b in range(IMAGES):
                    outputs(q, b)
                    weights(q + b, 1 - b)
                    add(q, b)
            outputs(NQ - 1, 0)
            weights(NQ - 1, 1)
            add(NQ - 1, 0)
            outputs(NQ - 1, 1)
            add(NQ - 1, 1)



FT = FF // P
HPAIRS = FT // 2


def kron_ffn(nc, c, w, x, out):
    x_g, out_g = tok_groups(x), tok_groups(out)
    with Stage(nc, "f") as s:
        ident, epst = s.sb("ident", [P, P]), s.sb("eps", [P, 1])
        fc1, pj1 = s.sb("fc1", [KR, FF]), s.sb("pj1", [P, FT, KR])
        fc2, pj2 = s.sb("fc2", [P, KJ]), s.sb("pj2", [P, KJ])
        xin = [s.sb(f"x{u}", [P, GT, D]) for u in range(2)]
        xo = [s.sb(f"xo{u}", [P, GT, D]) for u in range(2)]
        xn, prod = s.sb("xn", [P, GT, D]), s.sb("prod", [P, GT, D])
        xr = [s.sb(f"xr{u}", [P, GT, KR]) for u in range(2)]
        xrt = [s.sb(f"xrt{u}", [KR, G]) for u in range(2)]
        h = [s.sb(f"h{u}", [P, FT, G]) for u in range(2)]
        o = s.sb("o", [P, GT, KR])
        stats, mv = s.sb("stats", [P, GT, 6]), s.sb("mv", [P, GT, 2])
        std, rstd = s.sb("std", [P, 2, GT]), s.sb("rstd", [P, GT])
        pt, po = s.ps("pt", [KR, BANK]), s.ps("po", [P, BANK])
        ph = [s.ps(f"ph{v}", [P, 2, BANK]) for v in range(2)]
        x_in, x_out = ([s.sem(f"{x}{u}") for u in range(2)] for x in ("x_in", "x_out"))
        (loaded, eps_set, var_ready, std_ready, steps, osteps, reduced, turned, copied, h_ready, gelu, o_ready, o_taken, added, held) = (
            s.sem(x) for x in "loaded eps_set var_ready std_ready steps osteps reduced turned copied h_ready gelu o_ready "
            "o_taken added held".split())
        block = s.block()

        @block.sync
        def _(sp):
            for u in range(2):
                sp.sem_inc(x_out[u], 16)
            for tile, src in ((ident[:, :], c["ident"]), (fc1[:, :], w["fc1"]), (pj1[:, :, :], w["pj1"]), (fc2[:, :], w["fc2"]),
                              (pj2[:, :], w["pj2"])):
                sp.dma_start(tile, src).then_inc(loaded, 16)
            for u in range(2):
                sp.dma_start(xin[u][:, :, :], x_g[u]).then_inc(x_in[u], 16)
            with sp.Fori(0, NG // 2 - 1) as i:
                for u in range(2):
                    g = i * 2 + u
                    sp.wait_ge(added, g + 1)
                    sp.dma_start(out_g[g], xo[u][:, :, :]).then_inc(x_out[u], 16)
                    sp.dma_start(xin[u][:, :, :], x_g[g + 2]).then_inc(x_in[u], 16)
            for u in range(2):
                sp.wait_ge(added, NG - 1 + u)
                sp.dma_start(out_g[NG - 2 + u], xo[u][:, :, :]).then_inc(x_out[u], 16)
            for u in range(2):
                sp.wait_ge(x_out[u], 16 * (NG // 2 + 1))

        @block.vector
        def _(dve):
            nc.vector.memset(epst[:, :], 1e-5).then_inc(eps_set, 1)
            dve.sem_inc(o_taken, 1)
            dve.wait_ge(loaded, 80)
            chain = Chain(dve, steps, NORM_STEPS + 2)
            ochain = Chain(dve, osteps, 1)

            def reduce(i, u):
                g = i * 2 + u
                chain.start(g)
                dve.wait_ge(x_in[u], i * 16 + 16)
                chain(norm_steps(dve, chain, xin[u], stats, mv, std, rstd, xn, var_ready, std_ready, g, held))
                chain(nc.vector.tensor_tensor(prod[:, :, :].rearrange("p t (i j) -> p (t i) j", j=KJ),
                                              xn[:, :, :].rearrange("p t (i j) -> p (t i) j", j=KJ),
                                              fc2[:, :].rearrange("p (a j) -> p a j", a=1).to_broadcast([P, GT * KR, KJ]), ALU.mult))
                nc.vector.tensor_reduce(xr[u][:, :, :].rearrange("p t i -> p (t i)"),
                                        prod[:, :, :].rearrange("p t (i j) -> p (t i) j", j=KJ), AX.X, ALU.add).then_inc(reduced, 1)

            def spread(i, u):
                g = i * 2 + u
                ochain.start(g)
                dve.wait_ge(o_ready, g + 1)
                nc.vector.tensor_copy(o[:, :, :].rearrange("p t i -> p (t i)"), po[:, 0:GT * KR]).then_inc(o_taken, 1)
                dve.wait_ge(o_taken, g + 2)
                dve.wait_ge(x_out[u], i * 16 + 16)
                view = xo[u][:, :, :].rearrange("p t (i j) -> p (t i) j", j=KJ)
                ochain(nc.vector.tensor_tensor(view,
                                               o[:, :, :].rearrange("p t (i a) -> p (t i) a", a=1).to_broadcast([P, GT * KR, KJ]),
                                               pj2[:, :].rearrange("p (a j) -> p a j", a=1).to_broadcast([P, GT * KR, KJ]), ALU.mult))
                nc.vector.tensor_tensor(xo[u][:, :, :], xo[u][:, :, :], xin[u][:, :, :], ALU.add).then_inc(added, 1)

            reduce(0, 0)
            with dve.Fori(0, NG // 2 - 1) as i:
                for u in range(2):
                    reduce(i + u, 1 - u)
                    spread(i, u)
            reduce(NG // 2 - 1, 1)
            spread(NG // 2 - 1, 0)
            spread(NG // 2 - 1, 1)

        @block.tensor
        def _(pe):
            pe.wait_ge(loaded, 80)

            def hidden(i, u):
                g = i * 2 + u
                pe.wait_ge(reduced, g + 1)
                for t in range(GT):
                    ins = nc.tensor.transpose(pt[:, t * P:(t + 1) * P], xr[u][:, t, :], ident[:, :])
                ins.then_inc(turned, 1)
                pe.wait_ge(copied, g + 1)
                for jj in range(HPAIRS):
                    pe.wait_ge(gelu, g * HPAIRS + jj + 1)
                    for j in range(2):
                        at = (2 * jj + j) * P
                        ins = nc.tensor.matmul(ph[jj % 2][:, j, 0:G], fc1[:, at:at + P], xrt[u][:, :], start=True, stop=True)
                    ins.then_inc(h_ready, 1)

            def outputs(i, u):
                g = i * 2 + u
                pe.wait_ge(gelu, g * HPAIRS + HPAIRS + CREDIT)
                pe.wait_ge(o_taken, g + 1)
                for t in range(GT):
                    for j in range(FT):
                        ins = nc.tensor.matmul(po[:, t * KR:(t + 1) * KR], h[u][:, j, t * P:(t + 1) * P], pj1[:, j, :],
                                               start=j == 0, stop=j == FT - 1)
                ins.then_inc(o_ready, 1)

            hidden(0, 0)
            with pe.Fori(0, NG // 2 - 1) as i:
                for u in range(2):
                    hidden(i + u, 1 - u)
                    outputs(i, u)
            hidden(NG // 2 - 1, 1)
            outputs(NG // 2 - 1, 0)
            outputs(NG // 2 - 1, 1)

        @block.scalar
        def _(act):
            act.sem_inc(gelu, CREDIT)
            act.wait_ge(eps_set, 1)
            with act.Fori(0, NG // 2) as i:
                for u in range(2):
                    g = i * 2 + u
                    act.wait_ge(var_ready, g + 1)
                    nc.scalar.activation(std[:, 1, :], std[:, 0, :], ACT.Sqrt, bias=epst[:, :]).then_inc(std_ready, 1)
                    act.wait_ge(turned, g + 1)
                    nc.scalar.copy(xrt[u][:, :], pt[:, 0:G]).then_inc(copied, 1)
                    for jj in range(HPAIRS):
                        act.wait_ge(h_ready, g * HPAIRS + jj + 1)
                        nc.scalar.activation(h[u][:, 2 * jj:2 * jj + 2, :], ph[jj % 2][:, :, 0:G], ACT.Gelu).then_inc(gelu, 1)


def program(nc, c, w, out):
    def dram(name, *shape, dt=F32):
        return nc.dram_tensor(name, list(shape), dt).ap()

    x = w["x"].rearrange("b h w d -> (b h w) d")
    xn, y = dram("xn", P, DC, T), dram("y", SLOTS, P, T)
    norm_transpose(nc, "n", c, x, xn, 1e-6)
    ss2d(nc, c, dict(w, xn=xn), y)
    x1, th, tl, scores = dram("x1", T, D), dram("th", P, DC, T, dt=F16), dram("tl", P, DC, T, dt=F16), dram("scores", P, NT, EX)
    ss2d_out(nc, c, w, y, x, x1, th, tl, scores)
    x2 = dram("x2", T, D)
    moe(nc, c, w, x1, th, tl, scores, x2)
    xn1, sz, dt_raw = dram("xn1", P, DC, T), dram("sz", T, DIN), dram("dt_raw", P, NT, HEADS)
    mamba_gate(nc, c, w, x2, xn1, sz, dt_raw)
    xbc, x3 = dram("xbc", CT, P, T), dram("x3", T, D)
    mamba_conv(nc, w, xn1, xbc)
    mamba_scan(nc, c, w, x2, sz, dt_raw, xbc, x3)
    kron_ffn(nc, c, w, x3, out.rearrange("b h w d -> (b h w) d"))


def constants(np, bf16):
    i = np.arange(P)
    sel = np.zeros((BROWS, 3, BC, P), bf16)
    for p in range(BROWS):
        sel[p, 0, p % BC] = 1
        sel[p, 1, p % BC, :REST] = 1
        sel[p, 2, p % BC, REST:] = 1
    return dict(ident=np.eye(P, dtype=np.float32), mean768=np.full((P, P), 1.0 / CI, np.float32),
                upto=(i[:, None] <= i[None]).astype(np.float32), beyond=(i[:, None] > i[None]).astype(np.float32), sel=sel)


def layouts(np, I):
    def zeros(*shape):
        return np.zeros(shape, np.float32)

    def rows(a):
        return a.reshape((-1, P) + a.shape[1:]).swapaxes(0, 1)

    def spread(a):
        return np.broadcast_to(a.reshape(1, -1), (P, a.size))

    w = dict(x=I["x"])
    proj = I["L0_conv_in_proj_w"].reshape(KD, DI, DC, P).transpose(0, 3, 2, 1)
    w["in_proj"] = zeros(KD, P, 3, DC, P)
    w["in_proj"][:, :, 0] = proj[..., :P]
    w["in_proj"][:, :, 1, :, :REST] = proj[..., P:]
    w["in_proj"][:, :, 2, :, REST:] = proj[..., P:]

    def tiles(a):
        a = a.reshape((KD, DI) + a.shape[1:] if a.shape[0] == CI else a.shape)
        r = zeros(KD, P, 3, *a.shape[2:])
        r[:, :, 0], r[:, :, 1] = a[:, :P], a[:, :P]
        r[:, :REST, 2], r[:, REST:, 2] = a[:, P:], a[:, P:]
        return r

    w["conv"] = tiles(I["L0_conv_conv_w"].reshape(KD, DI, 9))
    w["conv_b"], w["ds"] = tiles(I["L0_conv_conv_b"]), tiles(I["L0_conv_Ds"])
    w["a_logs"], w["dt_b"] = tiles(I["L0_conv_A_logs"]), tiles(I["L0_conv_dt_projs_bias"])
    xp = I["L0_conv_x_proj_weight"]
    xp = np.concatenate([xp[:, RANK:]] * PARTS + [xp[:, :RANK]], 1).transpose(0, 2, 1)
    w["x_proj"] = zeros(KD, P, 3, XROWS)
    w["x_proj"][:, :, 0], w["x_proj"][:, :REST, 1], w["x_proj"][:, REST:, 2] = xp[:, :P], xp[:, P:], xp[:, P:]
    dp = I["L0_conv_dt_projs_weight"].transpose(0, 2, 1)
    w["dt_proj"] = zeros(KD, XROWS, 3, P)
    w["dt_proj"][:, BROWS:, 0] = dp[:, :, :P]
    w["dt_proj"][:, BROWS:, 1, :REST], w["dt_proj"][:, BROWS:, 2, REST:] = dp[:, :, P:], dp[:, :, P:]

    def slots(a):
        a = a.reshape((KD, DI) + a.shape[1:])
        r = zeros(P, SLOTS, *a.shape[2:])
        for k in range(KD):
            r[:, k] = a[k, :P]
            r[k % 2 * REST:k % 2 * REST + REST, KD + k // 2] = a[k, P:]
        return r

    w["out_proj"] = slots(I["L0_conv_out_proj_w"].T)
    w["out_nw"], w["out_nb"] = slots(I["L0_conv_out_norm_w"]), slots(I["L0_conv_out_norm_b"])
    w["gate_w"], w["gate_b"] = rows(I["L0_ffn_gate_w"]), I["L0_ffn_gate_b"].reshape(1, EX)
    w["w1"] = I["L0_ffn_w1"].reshape(EX, DC, P, 2, HALF).transpose(0, 3, 2, 1, 4)
    w["w2"] = I["L0_ffn_w2"].reshape(EX, 2, HT, P, D).transpose(0, 1, 3, 2, 4)
    w["b1"] = I["L0_ffn_b1"].reshape(EX, HID // P, P).transpose(2, 0, 1).reshape(P, -1)
    w["b2"] = I["L0_ffn_b2"].reshape(1, -1)
    win = I["L1_conv_W_in"]
    w["w_z"], w["w_dt"] = rows(win[:, :DIN]), rows(win[:, DIN + CONV:])
    xbc, conv = zeros(D, CT * P), zeros(CT * P, 10)
    xbc[:, :CONV] = win[:, DIN:DIN + CONV]
    w["w_x"] = xbc.reshape(DC, P, CT, P).transpose(2, 1, 0, 3)
    conv[:CONV, :9], conv[:CONV, 9] = I["L1_conv_W_conv"].reshape(9, CONV).T, I["L1_conv_b_conv"]
    conv = rows(conv)
    w["conv1"], w["conv1_b"] = conv[:, :, :9], conv[:, :, 9]
    w["dt1_b"], w["a1_log"] = spread(I["L1_conv_dt_bias"]), spread(I["L1_conv_A_log"])
    w["d1"] = spread(np.repeat(I["L1_conv_D_param"], HP))
    w["gamma"], w["beta"], w["w_out1"] = spread(I["L1_conv_gamma"]), spread(I["L1_conv_beta"]), rows(I["L1_conv_W_out"])
    w["fc1"], w["fc2"] = I["L1_ffn_c_fc_1"].T, spread(I["L1_ffn_c_fc_2"])
    w["pj1"], w["pj2"] = rows(I["L1_ffn_c_proj_1"].T), spread(I["L1_ffn_c_proj_2"])
    return w


def kernel(**inputs):
    import numpy as np
    import concourse.bacc as bacc
    from concourse.bass_utils import run_bass_kernel_spmd

    nc = bacc.Bacc("TRN2", target_bir_lowering=False, num_devices=1)
    arrays, c, w = {}, {}, {}
    for into, source in ((c, constants(np, mybir.dt.np(BF16))), (w, layouts(np, {k: np.asarray(v) for k, v in inputs.items()}))):
        for name, a in source.items():
            a = np.ascontiguousarray(a)
            arrays[f"in_{name}"] = a
            into[name] = nc.dram_tensor(f"in_{name}", a.shape, mybir.dt.from_np(a.dtype), kind="ExternalInput").ap()
    out = nc.dram_tensor("out", [IMAGES, SIDE, SIDE, D], F32, kind="ExternalOutput").ap()
    program(nc, c, w, out)
    return run_bass_kernel_spmd(nc, [arrays], core_ids=[0]).results[0]["out"]
```

```python
from contextlib import ExitStack

import concourse.bass as bass
from concourse import mybir

F32 = mybir.dt.float32
F16 = mybir.dt.float16
BF16 = mybir.dt.bfloat16
ACT = mybir.ActivationFunctionType
ALU = mybir.AluOpType
AX = mybir.AxisListType

P = 128
IMAGES, SIDE, D = 2, 48, 384
L = SIDE * SIDE
T = IMAGES * L
DC = D // P
G = 384
GT = G // P
NG = T // G
GI = L // G
ROWS = G // SIDE
BANK = 512

KD, DI, NS, RANK = 4, 192, 16, 12
CI = KD * DI
REST = DI - P
BC = 2 * NS
EX, HID = 4, 1536
HEADS, HP = 12, 64
DIN = HEADS * HP
CONV = DIN + 2 * NS
KR, KJ, FF = 32, 12, 1536


class Chain:

    def __init__(self, eng, sem, per):
        self.eng, self.sem, self.per = eng, sem, per
        self.base, self.n = 0, 0

    def start(self, turn):
        assert self.n in (0, self.per), (self.n, self.per)
        self.base, self.n = turn * self.per, 0

    def mark(self, ins):
        ins.then_inc(self.sem, 1)
        self.n += 1

    def wait(self):
        self.eng.wait_ge(self.sem, self.base + self.n)

    def __call__(self, ins):
        self.mark(ins)
        self.wait()


def settle(eng, held):
    eng.sem_inc(held, 1)


class Stage:

    def __init__(self, nc, name):
        self.nc, self.name = nc, name

    def __enter__(self):
        self.ctx, self.sems = ExitStack(), []
        return self

    def sb(self, name, shape, dt=F32):
        return self.ctx.enter_context(self.nc.sbuf_tensor(f"{self.name}_{name}", shape, dt))

    def ps(self, name, shape, dt=F32):
        return self.ctx.enter_context(self.nc.psum_tensor(f"{self.name}_{name}", shape, dt))

    def sem(self, name):
        self.sems.append(self.nc.alloc_semaphore(f"{self.name}_{name}"))
        return self.sems[-1]

    def block(self):
        return self.ctx.enter_context(self.nc.Block())

    def __exit__(self, *a):
        self.ctx.__exit__(*a)
        if self.sems:
            self.nc.clear_and_free_semaphores(self.sems)
            self.nc.all_engine_barrier()


def tok_groups(dram):
    return dram.rearrange("(g t p) d -> g p t d", t=GT, p=P)


def norm_steps(dve, chain, x, stats, mv, std, rstd, out, var_ready, std_ready, turn, held):
    nc = dve.bass
    for t in range(GT):
        chain.mark(nc.vector.bn_stats(stats[:, t, :], x[:, t, :]))
    chain.wait()
    settle(dve, held)
    for t in range(GT):
        chain.mark(nc.vector.bn_aggr(mv[:, t, :], stats[:, t, :]))
    chain.wait()
    nc.vector.tensor_copy(std[:, 0, :], mv[:, :, 1]).then_inc(var_ready, 1)
    dve.wait_ge(std_ready, turn + 1)
    chain(nc.vector.reciprocal(rstd[:, :], std[:, 1, :]))
    for t in range(GT):
        last = nc.vector.tensor_scalar(out[:, t, :], x[:, t, :], mv[:, t, 0:1], rstd[:, t:t + 1],
                                       ALU.subtract, ALU.mult)
    return last


NORM_STEPS = 2 * GT + 1


CREDIT = 2


def free(turn):
    return turn + 1


def ready(turn):
    return turn + CREDIT + 1


def norm_transpose(nc, name, c, src, dst, eps):
    src_g = tok_groups(src)
    with Stage(nc, name) as s:
        ident = s.sb("ident", [P, P])
        epst = s.sb("eps", [P, 1])
        x = [s.sb(f"x{u}", [P, GT, D]) for u in range(2)]
        xn = [s.sb(f"xn{u}", [P, GT, D]) for u in range(2)]
        xt = [s.sb(f"xt{u}", [P, DC, G]) for u in range(2)]
        stats, mv = s.sb("stats", [P, GT, 6]), s.sb("mv", [P, GT, 2])
        std, rstd = s.sb("std", [P, 2, GT]), s.sb("rstd", [P, GT])
        pt = [s.ps(f"pt{u}", [P, DC, BANK]) for u in range(2)]
        held = s.sem("held")
        consts, x_in = s.sem("consts"), [s.sem("x_in0"), s.sem("x_in1")]
        stored = [s.sem("stored0"), s.sem("stored1")]
        eps_set, var_ready, std_ready = s.sem("eps_set"), s.sem("var_ready"), s.sem("std_ready")
        normed, steps, turned, copied = s.sem("normed"), s.sem("steps"), s.sem("turned"), s.sem("copied")
        block = s.block()

        @block.sync
        def _(sp):
            sp.dma_start(ident[:, :], c["ident"]).then_inc(consts, 16)
            with sp.Fori(0, NG // 2) as i:
                for u in range(2):
                    g = i * 2 + u
                    sp.wait_ge(normed, free(g))
                    sp.dma_start(x[u][:, :, :], src_g[g]).then_inc(x_in[u], 16)

        @block.vector
        def _(dve):
            nc.vector.memset(epst[:, :], eps).then_inc(eps_set, 1)
            dve.sem_inc(normed, CREDIT)
            chain = Chain(dve, steps, NORM_STEPS)
            with dve.Fori(0, NG // 2) as i:
                for u in range(2):
                    g = i * 2 + u
                    chain.start(g)
                    dve.wait_ge(x_in[u], i * 16 + 16)
                    dve.wait_ge(turned, free(g))
                    norm_steps(dve, chain, x[u], stats, mv, std, rstd, xn[u], var_ready, std_ready, g,
                               held).then_inc(normed, 1)

        @block.tensor
        def _(pe):
            pe.sem_inc(turned, CREDIT)
            pe.wait_ge(consts, 16)
            with pe.Fori(0, NG // 2) as i:
                for u in range(2):
                    g = i * 2 + u
                    pe.wait_ge(normed, ready(g))
                    pe.wait_ge(copied, free(g))
                    for t in range(GT):
                        for d in range(DC):
                            ins = nc.tensor.transpose(pt[u][:, d, t * P:(t + 1) * P],
                                                      xn[u][:, t, d * P:(d + 1) * P], ident[:, :])
                    ins.then_inc(turned, 1)

        @block.scalar
        def _(act):
            act.sem_inc(copied, CREDIT)
            for u in range(2):
                act.sem_inc(stored[u], 16)
            act.wait_ge(eps_set, 1)
            with act.Fori(0, NG // 2) as i:
                for u in range(2):
                    g = i * 2 + u
                    act.wait_ge(var_ready, g + 1)
                    nc.scalar.activation(std[:, 1, :], std[:, 0, :], ACT.Sqrt, bias=epst[:, :]).then_inc(std_ready, 1)
                    act.wait_ge(turned, ready(g))
                    act.wait_ge(stored[u], i * 16 + 16)
                    nc.scalar.copy(xt[u][:, :, :], pt[u][:, :, 0:G]).then_inc(copied, 1)
                    act.wait_ge(copied, ready(g))
                    act.dma_start(dst[:, :, bass.ds(g * G, G)], xt[u][:, :, :]).then_inc(stored[u], 16)
            for u in range(2):
                act.wait_ge(stored[u], 16 * (NG // 2 + 1))


SEG = 2 * G
SEGS = L // SEG
STEPS_N = 3 * SEGS
PARTS = 3
BROWS = PARTS * BC
XROWS = BROWS + RANK


def in_order(image, k):
    if k >= 2:
        image = image[:, ::-1]
    return image.rearrange("p (h w) -> p h w" if k % 2 == 0 else "p (h w) -> p w h", h=SIDE)


def ss2d_conv(nc, c, w, k, xn, u, aneg, sel):
    with Stage(nc, f"a{k}") as s:
        win = s.sb("win", [P, 3, DC, P])
        taps, bias = s.sb("taps", [P, 3, 9]), s.sb("bias", [P, 3])
        alog = s.sb("alog", [P, 3, NS])
        pad = [s.sb(f"pad{v}", [P, SIDE + 2, SIDE + 2]) for v in range(2)]
        acc = [s.sb(f"acc{v}", [P, SIDE, SIDE]) for v in range(2)]
        pi = [s.ps(f"pi{v}", [P, BANK]) for v in range(2)]
        xn_in = [s.sem(f"xn_in{b}") for b in range(IMAGES)]
        loaded, win_in, zeroed, projected, padded, tapped, convolved, active, a_ready, a_exp, held = (s.sem(x) for x in (
            "loaded win_in zeroed projected padded tapped convolved active a_ready a_exp held".split()))
        block = s.block()

        @block.sync
        def _(sp):
            sp.dma_start(win[:, :, :, :], w["in_proj"][k]).then_inc(win_in, 16)
            sp.dma_start(xn[:, 0, :, :], w["xn"][:, :, 0:L]).then_inc(xn_in[0], 16)
            sp.dma_start(taps[:, :, :], w["conv"][k]).then_inc(loaded, 16)
            sp.dma_start(bias[:, :], w["conv_b"][k]).then_inc(loaded, 16)
            sp.dma_start(alog[:, :, :], w["a_logs"][k]).then_inc(loaded, 16)
            sp.dma_start(xn[:, 1, :, :], w["xn"][:, :, L:T]).then_inc(xn_in[1], 16)
            if sel:
                sp.dma_start(sel[0][:, :, :, :], c["sel"]).then_inc(sel[1], 16)
                sp.wait_ge(sel[1], 16)

        @block.gpsimd
        def _(pool):
            for v in range(2):
                nc.gpsimd.memset(pad[v][:, :, :], 0.0).then_inc(zeroed, 1)

        @block.tensor
        def _(pe):
            pe.sem_inc(projected, CREDIT)
            pe.wait_ge(win_in, 16)
            for ct in range(3):
                images = ((0,), (1,), (0, 1))[ct]
                pe.wait_ge(xn_in[images[0]], 16)
                terms = [(j, b, d) for j, b in enumerate(images) for d in range(DC)]
                with pe.Fori(0, GI // 2) as i:
                    for v in range(2):
                        q = i * 2 + v
                        pe.wait_ge(padded, free(q + ct * GI))
                        for j, b, d in terms:
                            ins = nc.tensor.matmul(pi[v][:, 0:G], win[:, 1 + j if ct == 2 else 0, d, :],
                                                   xn[:, b, d, bass.ds(q * G, G)],
                                                   start=(j, d) == (0, 0), stop=(j, b, d) == terms[-1])
                        ins.then_inc(projected, 1)

        @block.vector
        def _(dve):
            dve.wait_ge(loaded, 48)
            dve.wait_ge(a_exp, 1)
            nc.vector.tensor_scalar(aneg[:, :, :], alog[:, :, :], -1.0, None, ALU.mult).then_inc(a_ready, 1)
            chain = Chain(dve, tapped, None)
            for ct in range(3):
                dve.wait_ge(padded, CREDIT + GI * (ct + 1))
                if ct == 2:
                    dve.wait_ge(active, 1)
                image = acc[ct % 2][:, :, :]
                for t in range(9):
                    rows = pad[ct % 2][:, t // 3:t // 3 + SIDE, t % 3:t % 3 + SIDE]
                    tap = taps[:, ct, t:t + 1]
                    if t == 0:
                        ins = nc.vector.tensor_scalar(image, rows, tap, None, ALU.mult)
                    else:
                        ins = nc.vector.scalar_tensor_tensor(out=image, in0=rows, scalar=tap, in1=image,
                                                             op0=ALU.mult, op1=ALU.add)
                    if t < 8:
                        chain(ins)
                ins.then_inc(convolved, 1)

        @block.scalar
        def _(act):
            act.sem_inc(padded, CREDIT)
            act.wait_ge(loaded, 48)
            nc.scalar.activation(alog[:, :, :], alog[:, :, :], ACT.Exp).then_inc(a_exp, 1)
            act.wait_ge(zeroed, 2)

            def silu(ct):
                act.wait_ge(convolved, ct + 1)
                nc.scalar.activation(in_order(u[:, ct, :], k), acc[ct % 2][:, :, :], ACT.Silu,
                                     bias=bias[:, ct:ct + 1]).then_inc(active, 1)

            for ct in range(3):
                if ct == 2:
                    act.wait_ge(convolved, 1)
                with act.Fori(0, GI // 2) as i:
                    for v in range(2):
                        q = i * 2 + v
                        act.wait_ge(projected, ready(q + ct * GI))
                        settle(act, held)
                        nc.scalar.copy(pad[ct % 2][:, bass.ds(q * ROWS + 1, ROWS), 1:SIDE + 1],
                                       pi[v][:, 0:G].rearrange("p (h w) -> p h w", w=SIDE)).then_inc(padded, 1)
                if ct:
                    silu(ct - 1)
            silu(2)


def ss2d_project(nc, c, w, k, u, dt, y, bc):
    with Stage(nc, f"b{k}") as s:
        wx = s.sb("wx", [P, 3, XROWS])
        wd = s.sb("wd", [XROWS, 3, P])
        dtb, ds = s.sb("dtb", [P, 3]), s.sb("ds", [P, 3])
        xd = [s.sb(f"xd{b}", [XROWS, G]) for b in range(IMAGES)]
        rest = s.sb("rest", [64, G])
        e, one_e, ln, corr = (s.sb(x, [P, 3, G]) for x in ("e", "one_e", "ln", "corr"))
        pos = s.sb("pos", [P, 3, G])
        px = [s.ps(f"px{b}", [P, BANK]) for b in range(IMAGES)]
        pd = s.ps("pd", [P, 3, BANK])
        loaded, projected, xd_ready, split, dt_done = (s.sem(x) for x in (
            "loaded", "projected", "xd_ready", "split", "dt_done"))
        e_ready, one_ready, ln_ready, steps, summed, spread = (s.sem(x) for x in (
            "e_ready", "one_ready", "ln_ready", "steps", "summed", "spread"))
        act_steps, one_set, held = s.sem("act_steps"), s.sem("one_set"), s.sem("held")
        ln_one = s.sb("ln_one", [P, 2])
        block = s.block()

        @block.sync
        def _(sp):
            sp.dma_start(wx[:, :, :], w["x_proj"][k]).then_inc(loaded, 16)
            sp.dma_start(wd[:, :, :], w["dt_proj"][k]).then_inc(loaded, 16)
            sp.dma_start(dtb[:, :], w["dt_b"][k]).then_inc(loaded, 16)
            sp.dma_start(ds[:, :], w["ds"][k]).then_inc(loaded, 16)

        @block.tensor
        def _(pe):
            pe.wait_ge(loaded, 64)
            with pe.Fori(0, GI) as q:
                for b in range(IMAGES):
                    pe.wait_ge(xd_ready, q * 2 + b + 1)
                    nc.tensor.matmul(px[b][0:XROWS, 0:G], wx[:, 0, :], u[:, b, bass.ds(q * G, G)],
                                     start=True, stop=False)
                    nc.tensor.matmul(px[b][0:XROWS, 0:G], wx[:, 1 + b, :], u[:, 2, bass.ds(q * G, G)],
                                     start=False, stop=True).then_inc(projected, 1)
                pe.wait_ge(xd_ready, q * 2 + 4)
                pe.wait_ge(summed, q + 1)
                for b in range(IMAGES):
                    nc.tensor.matmul(pd[:, b, 0:G], wd[:, 0, :], xd[b][:, :], start=True, stop=True)
                nc.tensor.matmul(pd[:, 2, 0:G], wd[:, 1, :], xd[0][:, :], start=True, stop=False)
                nc.tensor.matmul(pd[:, 2, 0:G], wd[:, 2, :], xd[1][:, :], start=False, stop=True).then_inc(dt_done, 1)

        @block.scalar
        def _(act):
            nc.scalar.preload_act_table_set("natural_log_exp_and_others")
            act.sem_inc(xd_ready, 2)
            act.wait_ge(one_set, 1)
            nc.scalar.activation(ln_one[:, 1:2], ln_one[:, 0:1], ACT.Ln).then_inc(one_set, 1)
            chain = Chain(act, act_steps, 1)
            act.wait_ge(loaded, 64)
            with act.Fori(0, GI) as q:
                act.wait_ge(split, q + 1)
                for b in range(IMAGES):
                    act.wait_ge(projected, q * 2 + b + 1)
                    nc.scalar.copy(xd[b][:, :], px[b][0:XROWS, 0:G]).then_inc(xd_ready, 1)
                act.wait_ge(dt_done, q + 1)
                chain.start(q)
                for ct in range(3):
                    ins = nc.scalar.activation(e[:, ct, :], pd[:, ct, 0:G], ACT.Abs, bias=dtb[:, ct:ct + 1])
                chain(ins)
                nc.scalar.activation(e[:, :, :], e[:, :, :], ACT.Exp, scale=-1.0).then_inc(e_ready, 1)
                act.wait_ge(one_ready, q + 1)
                nc.scalar.activation(ln[:, :, :], one_e[:, :, :], ACT.Ln).then_inc(ln_ready, 1)

        @block.vector
        def _(dve):
            dve.sem_inc(split, 1)
            dve.sem_inc(summed, 1)
            nc.vector.memset(ln_one[:, 0:1], 1.0).then_inc(one_set, 1)
            chain = Chain(dve, steps, 7)
            dve.wait_ge(loaded, 64)
            dve.wait_ge(one_set, 2)
            with dve.Fori(0, GI) as q:
                chain.start(q)
                cols = bass.ds(q * G, G)
                for b in range(IMAGES):
                    dve.wait_ge(xd_ready, q * 2 + 3 + b)
                    settle(dve, held)
                    chain(nc.vector.tensor_copy(bc[:, b, cols], xd[b][0:BROWS, :]))
                    chain(nc.vector.tensor_tensor(rest[:, :], xd[b][0:64, :], bc[0:64, b, cols], ALU.subtract))
                    settle(dve, held)
                    chain(nc.vector.tensor_copy(bc[0:64, b, cols], rest[:, :]))
                    last = nc.vector.tensor_tensor(bc[0:32, b, cols], rest[0:32, :], bc[0:32, b, cols], ALU.subtract)
                last.then_inc(split, 1)
                for ct in range(3):
                    nc.vector.tensor_scalar(y[:, ct, cols], u[:, ct, cols], ds[:, ct:ct + 1], None, ALU.mult)
                dve.wait_ge(e_ready, q + 1)
                nc.vector.tensor_scalar(one_e[:, :, :], e[:, :, :], 1.0, None, ALU.add).then_inc(one_ready, 1)
                for ct in range(3):
                    nc.vector.tensor_scalar(pos[:, ct, :], pd[:, ct, 0:G], dtb[:, ct:ct + 1], 0.0, ALU.add, ALU.max)
                dve.wait_ge(one_ready, q + 1)
                chain(nc.vector.scalar_tensor_tensor(out=corr[:, :, :], in0=one_e[:, :, :], scalar=1.0, in1=e[:, :, :],
                                                     op0=ALU.subtract, op1=ALU.subtract))
                dve.wait_ge(ln_ready, q + 1)
                nc.vector.scalar_tensor_tensor(out=corr[:, :, :], in0=ln[:, :, :], scalar=ln_one[:, 1:2], in1=corr[:, :, :],
                                               op0=ALU.subtract, op1=ALU.subtract).then_inc(summed, 1)
                dve.wait_ge(summed, q + 2)
                nc.vector.tensor_tensor(dt[:, :, cols], corr[:, :, :], pos[:, :, :], ALU.add).then_inc(spread, 1)

        @block.gpsimd
        def _(pool):
            with pool.Fori(0, GI) as q:
                cols = bass.ds(q * G, G)
                pool.wait_ge(spread, q + 1)
                nc.gpsimd.tensor_tensor(u[:, :, cols], dt[:, :, cols], u[:, :, cols], ALU.mult)


def ss2d_scan(nc, c, w, k, du, dt, y, bc, aneg, sel, out):
    with Stage(nc, f"c{k}") as s:
        a, h, hc = ([s.sb(f"{x}{v}", [P, SEG]) for v in range(2)] for x in ("a", "h", "hc"))
        pb, pcc = ([s.ps(f"{x}{v}", [P, 2 * BANK]) for v in range(2)] for x in ("pb", "pc"))
        b_ready, c_ready, a_ready = s.sem("b_ready"), s.sem("c_ready"), s.sem("a_ready")
        fed, scanned, weighed, added = s.sem("fed"), s.sem("scanned"), s.sem("weighed"), s.sem("added")
        ordered, stored, held = s.sem("ordered"), s.sem("stored"), s.sem("held")
        block = s.block()
        ITER = 2 * STEPS_N

        def place(m):
            return (m % STEPS_N) // SEGS, m % SEGS, m % 2, m // STEPS_N

        def cols(t, ct, seg):
            return t[:, ct, seg * SEG:(seg + 1) * SEG]

        @block.tensor
        def _(pe):
            with pe.Fori(0, NS // 2) as i:
                def spread(m, first, tiles, gone, signal):
                    ct, seg, v, half = place(m)
                    pe.wait_ge(gone, free(i * ITER + m))
                    terms = (((0, 0),), ((1, 0),), ((0, 1), (1, 2)))[ct]
                    for j, width in ((0, BANK), (BANK, SEG - BANK)):
                        at = seg * SEG + j
                        for b, kind in terms:
                            ins = nc.tensor.matmul(tiles[v][:, j:j + width], sel[:, kind, i * 2 + (half + first), :],
                                                   bc[:, b, at:at + width], start=(b, kind) == terms[0],
                                                   stop=(b, kind) == terms[-1])
                    ins.then_inc(signal, 1)

                spread(0, 0, pb, scanned, b_ready)
                for m in range(ITER):
                    if m + 1 < ITER:
                        spread(m + 1, 0, pb, scanned, b_ready)
                    spread(m, NS, pcc, weighed, c_ready)

        @block.scalar
        def _(act):
            with act.Fori(0, NS // 2) as i:
                for m in range(ITER):
                    ct, seg, v, half = place(m)
                    act.wait_ge(scanned, free(i * ITER + m))
                    settle(act, held)
                    nc.scalar.activation(a[v][:, :], dt[:, ct, seg * SEG:(seg + 1) * SEG], ACT.Exp,
                                         scale=aneg[:, ct, bass.ds(i * 2 + half, 1)]).then_inc(a_ready, 1)

        @block.vector
        def _(dve):
            dve.sem_inc(scanned, CREDIT)
            dve.sem_inc(weighed, CREDIT)
            with dve.Fori(0, NS // 2) as i:
                def feed(m):
                    ct, seg, v, _ = place(m)
                    dve.wait_ge(b_ready, i * ITER + m + 1)
                    nc.vector.tensor_tensor(pb[v][:, 0:SEG], pb[v][:, 0:SEG], cols(du, ct, seg), ALU.mult).then_inc(fed, 1)

                def scan(m):
                    ct, seg, v, _ = place(m)
                    dve.wait_ge(fed, i * ITER + m + 1)
                    dve.wait_ge(a_ready, i * ITER + m + 1)
                    dve.wait_ge(weighed, free(i * ITER + m))
                    if seg:
                        dve.wait_ge(scanned, i * ITER + m + CREDIT)
                    nc.vector.tensor_tensor_scan(h[v][:, :], a[v][:, :], pb[v][:, 0:SEG], h[1 - v][:, SEG - 1:SEG] if seg else 0.0,
                                                 ALU.mult, ALU.add).then_inc(scanned, 1)

                def weigh(m):
                    ct, seg, v, _ = place(m)
                    dve.wait_ge(scanned, i * ITER + m + 1 + CREDIT)
                    dve.wait_ge(c_ready, i * ITER + m + 1)
                    dve.wait_ge(added, i * ITER + (m - 1 + STEPS_N))
                    nc.vector.tensor_tensor(hc[v][:, :], h[v][:, :], pcc[v][:, 0:SEG], ALU.mult).then_inc(weighed, 1)

                feed(0)
                for m in range(ITER):
                    if m + 1 < ITER:
                        feed(m + 1)
                    scan(m)
                    if m:
                        weigh(m - 1)
                weigh(ITER - 1)
            if k:
                for ct in range(3):
                    dve.wait_ge(added, NS * STEPS_N + STEPS_N)
                    nc.vector.tensor_copy(in_order(du[:, ct, :], k), y[:, ct, :].rearrange("p (h w) -> p h w", w=SIDE)).then_inc(ordered, 1)

        @block.gpsimd
        def _(pool):
            pool.sem_inc(added, STEPS_N)
            with pool.Fori(0, NS // 2) as i:
                for m in range(ITER):
                    ct, seg, v, half = place(m)
                    pool.wait_ge(weighed, ready(i * ITER + m))
                    pool.wait_ge(added, i * ITER + m + 1)
                    part = y[:, ct, seg * SEG:(seg + 1) * SEG]
                    nc.gpsimd.tensor_tensor(part, part, hc[v][:, :], ALU.add).then_inc(added, 1)

        @block.sync
        def _(sp):
            sp.wait_ge(added, NS * STEPS_N + STEPS_N)
            src = du if k else y
            if k:
                sp.wait_ge(ordered, 3)
            slot, row = 4 + k // 2, (k % 2) * REST
            sp.dma_start(out[k, :, 0:L], src[:, 0, :]).then_inc(stored, 16)
            sp.dma_start(out[k, :, L:T], src[:, 1, :]).then_inc(stored, 16)
            sp.dma_start(out[slot, row:row + REST, 0:L], src[0:REST, 2, :]).then_inc(stored, 16)
            sp.dma_start(out[slot, row:row + REST, L:T], src[REST:P, 2, :]).then_inc(stored, 16)
            sp.wait_ge(stored, 64)


def ss2d(nc, c, w, out, directions=range(KD)):
    with Stage(nc, "ss2d") as s:
        u = s.sb("u", [P, 3, L])
        bc = s.sb("bc", [BROWS, IMAGES, L], BF16)
        aneg = s.sb("aneg", [P, 3, NS])
        sel = s.sb("sel", [BROWS, 3, BC, P], BF16)
        sel_in = s.sem("sel_in")
        for k in directions:
            with Stage(nc, f"x{k}") as t:
                xn = t.sb("xn", [P, IMAGES, DC, L])
                ss2d_conv(nc, c, w, k, xn, u, aneg, (sel, sel_in) if k == directions[0] else None)
            with Stage(nc, f"y{k}") as t:
                dt, y = t.sb("dt", [P, 3, L]), t.sb("y", [P, 3, L])
                ss2d_project(nc, c, w, k, u, dt, y, bc)
                ss2d_scan(nc, c, w, k, u, dt, y, bc, aneg, sel, out)


SLOTS = CI // P
NT = T // P


def ss2d_out(nc, c, w, y, x, x1, th, tl, scores_out):
    xg, x1g = tok_groups(x), tok_groups(x1)
    with Stage(nc, "o") as s:
        ident, mean_w = s.sb("ident", [P, P]), s.sb("mean_w", [P, P])
        wo, nw, nb = s.sb("wo", [P, SLOTS, D]), s.sb("nw", [P, SLOTS]), s.sb("nb", [P, SLOTS])
        nbb, bias = s.sb("nbb", [P, SLOTS, P]), s.sb("bias", [P, D])
        gw, gb, ones = s.sb("gw", [P, DC, EX]), s.sb("gb", [1, EX]), s.sb("ones", [P, P])
        epst = s.sb("eps", [P, 1])
        yt = [s.sb(f"yt{u}", [P, SLOTS, G]) for u in range(2)]
        sq = s.sb("sq", [P, SLOTS, G])
        xin = [s.sb(f"xin{u}", [P, GT, D]) for u in range(2)]
        xo = [s.sb(f"xo{u}", [P, GT, D]) for u in range(2)]
        xn = [s.sb(f"xn{u}", [P, GT, D]) for u in range(2)]
        xt = s.sb("xt", [P, DC, G])
        hi = [s.sb(f"hi{u}", [P, DC, G], F16) for u in range(2)]
        lo = [s.sb(f"lo{u}", [P, DC, G], F16) for u in range(2)]
        stats, mv = s.sb("stats", [P, GT, 6]), s.sb("mv", [P, GT, 2])
        std, rstd = s.sb("std", [P, 2, GT]), s.sb("rstd", [P, GT])
        ystd, yrstd = s.sb("ystd", [P, GT]), s.sb("yrstd", [P, GT])
        sc = s.sb("sc", [P, NT, EX])
        pm, po, pt, pg = (s.ps("pm", [P, BANK]), s.ps("po", [P, GT, BANK]), s.ps("pt", [P, DC, BANK]),
                          s.ps("pg", [P, BANK]))
        loaded, y_in, x_in, x_out, t_out, sc_out = (s.sem("loaded"), [s.sem(f"y_in{u}") for u in range(2)],
                                                    [s.sem(f"x_in{u}") for u in range(2)], [s.sem(f"x_out{u}") for u in range(2)],
                                                    [s.sem(f"t_out{u}") for u in range(2)], s.sem("sc_out"))
        (eps_set, setup, bias_sum, mean_ready, centred, squared, var_ready, rooted, projected, x1_ready, nvar_ready, nstd_ready,
         normed, turned, copied, scored, taken, hi_ready, lo_ready, steps, held, x1_steps) = (s.sem(x) for x in (
             "eps_set setup bias_sum mean_ready centred squared var_ready rooted projected x1_ready nvar_ready nstd_ready "
             "normed turned copied scored taken hi_ready lo_ready steps held x1_steps").split())
        block = s.block()

        @block.sync
        def _(sp):
            for tile, src in ((ident[:, :], c["ident"]), (mean_w[:, :], c["mean768"]), (wo[:, :, :], w["out_proj"]),
                              (nw[:, :], w["out_nw"]), (nb[:, :], w["out_nb"]), (gw[:, :, :], w["gate_w"]), (gb[:, :], w["gate_b"])):
                sp.dma_start(tile, src).then_inc(loaded, 16)
            with sp.Fori(0, NG // 2) as i:
                for v in range(2):
                    g = i * 2 + v
                    sp.wait_ge(projected, free(g))
                    sp.wait_ge(squared, free(g))
                    sp.dma_start(yt[v][:, :, :], y.rearrange("s p t -> p s t")[:, :, bass.ds(g * G, G)]).then_inc(y_in[v], 16)
                    sp.wait_ge(x1_ready, free(g))
                    sp.dma_start(xin[v][:, :, :], xg[g]).then_inc(x_in[v], 16)
            sp.wait_ge(taken, NG + 1)
            sp.dma_start(scores_out, sc[:, :, :]).then_inc(sc_out, 16)
            sp.wait_ge(sc_out, 16)

        @block.vector
        def _(dve):
            nc.vector.memset(ones[:, :], 1.0).then_inc(eps_set, 1)
            nc.vector.memset(epst[:, :], 1e-5).then_inc(eps_set, 1)
            dve.sem_inc(x1_ready, CREDIT)
            dve.sem_inc(taken, 1)
            dve.wait_ge(loaded, 112)
            dve.wait_ge(eps_set, 2)
            for j in range(SLOTS):
                ins = nc.vector.tensor_scalar(nbb[:, j, :], ones[:, :], nb[:, j:j + 1], None, ALU.mult)
            ins.then_inc(setup, 1)
            dve.wait_ge(bias_sum, 1)
            nc.vector.tensor_copy(bias[:, :], pm[:, 0:D])
            for j in range(SLOTS):
                ins = nc.vector.tensor_scalar(wo[:, j, :], wo[:, j, :], nw[:, j:j + 1], None, ALU.mult)
            ins.then_inc(setup, 1)
            dve.wait_ge(setup, 2)
            x1_chain, chain = Chain(dve, x1_steps, 2), Chain(dve, steps, NORM_STEPS)

            def centre(g, v):
                dve.wait_ge(mean_ready, g + 1)
                nc.vector.tensor_tensor(yt[v][:, :, :], yt[v][:, :, :],
                                        pm[:, 0:G].rearrange("p (a g) -> p a g", a=1).to_broadcast([P, SLOTS, G]),
                                        ALU.subtract).then_inc(centred, 1)

            def residual(g, i, v):
                x1_chain.start(g)
                dve.wait_ge(rooted, g + 2)
                x1_chain(nc.vector.reciprocal(yrstd[:, :], ystd[:, :]))
                dve.wait_ge(projected, ready(g))
                dve.wait_ge(x_in[v], i * 16 + 16)
                dve.wait_ge(x_out[v], i * 16 + 16)
                for t in range(GT):
                    ins = nc.vector.scalar_tensor_tensor(out=xo[v][:, t, :], in0=po[:, t, 0:D], scalar=yrstd[:, t:t + 1],
                                                         in1=xin[v][:, t, :], op0=ALU.mult, op1=ALU.add)
                x1_chain(ins)
                nc.vector.tensor_tensor(xo[v][:, :, :], xo[v][:, :, :],
                                        bias[:, :].rearrange("p (a g) -> p a g", a=1).to_broadcast([P, GT, D]),
                                        ALU.add).then_inc(x1_ready, 1)

            def norm(g, v):
                chain.start(g)
                dve.wait_ge(x1_ready, ready(g))
                dve.wait_ge(turned, free(g))
                norm_steps(dve, chain, xo[v], stats, mv, std, rstd, xn[v], nvar_ready, nstd_ready, g, held).then_inc(normed, 1)

            def take(g):
                dve.wait_ge(scored, g + 2)
                settle(dve, held)
                nc.vector.tensor_copy(sc[:, bass.ds(g * GT, GT), :],
                                      pg[:, 0:GT * EX].rearrange("p (t e) -> p t e", e=EX)).then_inc(taken, 1)

            centre(0, 0)
            residual(0, 0, 0)
            centre(1, 1)
            norm(0, 0)
            with dve.Fori(0, NG // 2 - 1) as i:
                for v in range(2):
                    g = i * 2 + v
                    residual(g + 1, i + v, 1 - v)
                    centre(g + 2, v)
                    norm(g + 1, 1 - v)
                    take(g)
            residual(NG - 1, NG // 2 - 1, 1)
            norm(NG - 1, 1)
            take(NG - 2)
            take(NG - 1)

        @block.gpsimd
        def _(pool):
            pool.sem_inc(lo_ready, 1)
            with pool.Fori(0, NG // 2) as i:
                for v in range(2):
                    g = i * 2 + v
                    pool.wait_ge(hi_ready, g + 1)
                    pool.wait_ge(t_out[v], i * 32 + 32)
                    nc.gpsimd.tensor_tensor(lo[v][:, :, :], xt[:, :, :], hi[v][:, :, :], ALU.subtract).then_inc(lo_ready, 1)

        @block.tensor
        def _(pe):
            pe.sem_inc(projected, CREDIT)
            pe.sem_inc(turned, CREDIT)
            pe.sem_inc(scored, 1)
            pe.wait_ge(loaded, 112)
            pe.wait_ge(setup, 1)
            for j in range(SLOTS):
                ins = nc.tensor.matmul(pm[:, 0:D], nbb[:, j, :], wo[:, j, :], start=j == 0, stop=j == SLOTS - 1)
            ins.then_inc(bias_sum, 1)
            pe.wait_ge(setup, 2)

            def mean(g, i, v):
                pe.wait_ge(y_in[v], i * 16 + 16)
                pe.wait_ge(rooted, g + 1)
                for j in range(SLOTS):
                    ins = nc.tensor.matmul(pm[:, 0:G], mean_w[:, :], yt[v][:, j, :], start=j == 0, stop=j == SLOTS - 1)
                ins.then_inc(mean_ready, 1)

            def project(g, v):
                pe.wait_ge(centred, g + 1)
                pe.wait_ge(x1_ready, g + CREDIT)
                for t in range(GT):
                    for j in range(SLOTS):
                        ins = nc.tensor.matmul(po[:, t, 0:D], yt[v][:, j, t * P:(t + 1) * P], wo[:, j, :],
                                               start=j == 0, stop=j == SLOTS - 1)
                ins.then_inc(projected, 1)
                pe.wait_ge(squared, ready(g))
                for t in range(GT):
                    for j in range(SLOTS):
                        ins = nc.tensor.matmul(pm[:, G + t:G + t + 1], sq[:, j, t * P:(t + 1) * P], mean_w[:, 0:1],
                                               start=j == 0, stop=j == SLOTS - 1)
                ins.then_inc(var_ready, 1)

            def turn(g, v):
                pe.wait_ge(normed, g + 1)
                pe.wait_ge(copied, g + 1)
                for t in range(GT):
                    for d in range(DC):
                        ins = nc.tensor.transpose(pt[:, d, t * P:(t + 1) * P], xn[v][:, t, d * P:(d + 1) * P], ident[:, :])
                ins.then_inc(turned, 1)

            def score(g):
                pe.wait_ge(copied, g + 2)
                pe.wait_ge(taken, g + 1)
                for t in range(GT):
                    out = pg[:, t * EX:(t + 1) * EX]
                    for d in range(DC):
                        nc.tensor.matmul(out, xt[:, d, t * P:(t + 1) * P], gw[:, d, :], start=d == 0, stop=False)
                    ins = nc.tensor.matmul(out, ones[0:1, :], gb[:, :], start=False, stop=True)
                ins.then_inc(scored, 1)

            for g in range(2):
                mean(g, 0, g)
                project(g, g)
            with pe.Fori(0, NG // 2 - 1) as i:
                for v in range(2):
                    g = i * 2 + v
                    mean(g + 2, i + 1, v)
                    turn(g, v)
                    project(g + 2, v)
                    score(g)
            for g in range(NG - 2, NG):
                turn(g, g % 2)
                score(g)

        @block.scalar
        def _(act):
            act.sem_inc(copied, 1)
            act.sem_inc(rooted, 1)
            act.sem_inc(squared, CREDIT)
            for v in range(2):
                act.sem_inc(x_out[v], 16)
                act.sem_inc(t_out[v], 32)
            act.wait_ge(eps_set, 2)

            def square(g, v):
                act.wait_ge(centred, g + 1)
                nc.scalar.activation(sq[:, :, :], yt[v][:, :, :], ACT.Square).then_inc(squared, 1)

            def root_y(g, v):
                act.wait_ge(var_ready, g + 1)
                nc.scalar.activation(ystd[:, :], pm[:, G:G + GT], ACT.Sqrt, bias=epst[:, :]).then_inc(rooted, 1)

            def store_x1(g, v):
                act.wait_ge(x1_ready, ready(g))
                act.dma_start(x1g[g], xo[v][:, :, :]).then_inc(x_out[v], 16)

            def root(g):
                act.wait_ge(nvar_ready, g + 1)
                nc.scalar.activation(std[:, 1, :], std[:, 0, :], ACT.Sqrt, bias=epst[:, :]).then_inc(nstd_ready, 1)

            def store_t(g, i, v):
                act.wait_ge(turned, ready(g))
                act.wait_ge(lo_ready, g + 1)
                act.wait_ge(scored, g + 1)
                nc.scalar.copy(xt[:, :, :], pt[:, :, 0:G]).then_inc(copied, 1)
                act.wait_ge(copied, g + 2)
                act.wait_ge(t_out[v], i * 32 + 32)
                nc.scalar.copy(hi[v][:, :, :], xt[:, :, :]).then_inc(hi_ready, 1)
                act.wait_ge(hi_ready, g + 1)
                act.dma_start(th[:, :, bass.ds(g * G, G)], hi[v][:, :, :]).then_inc(t_out[v], 16)

            def store_lo(g, v):
                act.wait_ge(lo_ready, g + 2)
                act.dma_start(tl[:, :, bass.ds(g * G, G)], lo[v][:, :, :]).then_inc(t_out[v], 16)

            for g in range(2):
                square(g, g)
                if g:
                    root(0)
                root_y(g, g)
                store_x1(g, g)
            with act.Fori(0, NG // 2 - 1) as i:
                for v in range(2):
                    g = i * 2 + v
                    square(g + 2, v)
                    root(g + 1)
                    store_t(g, i, v)
                    root_y(g + 2, v)
                    store_lo(g, v)
                    store_x1(g + 2, v)
            root(NG - 1)
            for g in range(NG - 2, NG):
                store_t(g, NG // 2 - 1, g % 2)
                store_lo(g, g % 2)
            for v in range(2):
                act.wait_ge(x_out[v], 16 * (NG // 2 + 1))
                act.wait_ge(t_out[v], 32 * (NG // 2 + 1))


HALF = HID // 2
HT = HALF // P
PAIRS = HT // 2
W_SCALE = 64.0


def moe(nc, c, w, x1, th, tl, scores, x2):
    with Stage(nc, "m") as s:
        acc = s.sb("acc", [P, NT, D])
        xh, xl = s.sb("xh", [P, DC, T], F16), s.sb("xl", [P, DC, T], F16)
        w1s, w2s = s.sb("w1s", [P, DC, HALF]), s.sb("w2s", [P, HT, D])
        w1h, w1l, w2h, w2l = ([s.sb(f"{x}{v}", shape, F16) for v in range(2)] for x, shape in (
            ("w1h", [P, DC, HALF]), ("w1l", [P, DC, HALF]), ("w2h", [P, HT, D]), ("w2l", [P, HT, D])))
        b1, b2, ones = s.sb("b1", [P, EX * 2 * HT]), s.sb("b2", [1, EX * D]), s.sb("ones", [1, P])
        act_out = [s.sb(f"act_out{v}", [P, 2, G]) for v in range(2)]
        hh, hl = ([s.sb(f"{x}{v}", [P, HT, G], F16) for v in range(2)] for x in ("hh", "hl"))
        sc, gate, rank = s.sb("sc", [P, NT, EX]), s.sb("gate", [P, NT, EX]), s.sb("rank", [P, NT, EX])
        row, above = s.sb("row", [P, NT]), s.sb("above", [P, NT])
        ph = [s.ps(f"ph{v}", [P, 2, BANK]) for v in range(2)]
        py = s.ps("py", [P, GT, BANK])
        (loaded, x_in, acc_in, w_in, split, h_ready, gelu, parted, y_ready, added, stored, steps, shifted, expd, ones_set,
         held, parts, high, pe_held, pool_held) = (s.sem(x) for x in "loaded x_in acc_in w_in split h_ready gelu parted y_ready added stored steps shifted "
                   "expd ones_set held parts high pe_held pool_held".split())
        block = s.block()
        UNIT = NG * GT
        Y_CREDIT = 2 * UNIT

        @block.sync
        def _(sp):
            for tile, src in ((sc[:, :, :], scores), (b1[:, :], w["b1"]), (b2[:, :], w["b2"])):
                sp.dma_start(tile, src).then_inc(loaded, 16)
            sp.dma_start(w1s[:, :, :], w["w1"][0, 0]).then_inc(w_in, 16)
            sp.dma_start(w2s[:, :, :], w["w2"][0, 0]).then_inc(w_in, 16)
            sp.dma_start(xh[:, :, :], th).then_inc(x_in, 16)
            sp.dma_start(xl[:, :, :], tl).then_inc(x_in, 16)
            sp.dma_start(acc[:, :, :], x1.rearrange("(n p) d -> p n d", p=P)).then_inc(acc_in, 16)
            sp.wait_ge(split, 1)
            sp.dma_start(w1s[:, :, :], w["w1"][0, 1]).then_inc(w_in, 16)
            sp.dma_start(w2s[:, :, :], w["w2"][0, 1]).then_inc(w_in, 16)
            with sp.Fori(1, EX) as e:
                for v in range(2):
                    sp.wait_ge(split, e * 2 + v)
                    sp.dma_start(w1s[:, :, :], w["w1"][e, v]).then_inc(w_in, 16)
                    sp.dma_start(w2s[:, :, :], w["w2"][e, v]).then_inc(w_in, 16)
            sp.wait_ge(added, EX * 2 * UNIT + GT)
            sp.dma_start(x2.rearrange("(n p) d -> p n d", p=P), acc[:, :, :]).then_inc(stored, 16)
            sp.wait_ge(stored, 16)

        @block.gpsimd
        def _(pool):
            with pool.Fori(0, EX) as e:
                for v in range(2):
                    unit = e * 2 + v
                    pool.wait_ge(w_in, unit * 32 + 32)
                    pool.wait_ge(y_ready, unit * UNIT + UNIT)
                    settle(pool, pool_held)
                    for part, whole in ((w1h, w1s), (w2h, w2s)):
                        nc.gpsimd.tensor_scalar(part[v][:, :, :], whole[:, :, :], W_SCALE, 1.0, ALU.mult, ALU.mult)
                        nc.gpsimd.tensor_scalar(whole[:, :, :], whole[:, :, :], W_SCALE, 1.0, ALU.mult, ALU.mult).then_inc(parts, 1)
                    pool.wait_ge(parts, unit * 2 + 2)
                    nc.gpsimd.tensor_tensor(w1l[v][:, :, :], w1s[:, :, :], w1h[v][:, :, :], ALU.subtract)
                    nc.gpsimd.tensor_tensor(w2l[v][:, :, :], w2s[:, :, :], w2h[v][:, :, :], ALU.subtract).then_inc(split, 1)

        @block.tensor
        def _(pe):
            pe.sem_inc(y_ready, Y_CREDIT)
            pe.wait_ge(loaded, 48)
            pe.wait_ge(ones_set, 2)
            pe.wait_ge(x_in, 32)
            with pe.Fori(0, EX) as e:
                for half in range(2):
                    pe.wait_ge(split, e * 2 + half + 1)
                    settle(pe, pe_held)
                    with pe.Fori(0, NG // 2) as i:
                        turn0 = (e * 2 + half) * NG + i * 2

                        def hidden(v):
                            cols = bass.ds((i * 2 + v) * G, G)
                            for jj in range(PAIRS):
                                pe.wait_ge(gelu, (turn0 + v) * PAIRS + jj + 1)
                                for j in (2 * jj, 2 * jj + 1):
                                    terms = [(a, b, d) for a, b in ((w1h, xh), (w1h, xl), (w1l, xh)) for d in range(DC)]
                                    for n, (a, b, d) in enumerate(terms):
                                        ins = nc.tensor.matmul(ph[(v * PAIRS + jj) % 2][:, j % 2, 0:G],
                                                               a[half][:, d, j * P:(j + 1) * P], b[:, d, cols],
                                                               start=n == 0, stop=n == len(terms) - 1)
                                ins.then_inc(h_ready, 1)

                        def outputs(v):
                            pe.wait_ge(parted, (turn0 + v) * PAIRS + PAIRS + CREDIT)
                            for t in range(GT):
                                pe.wait_ge(added, (turn0 + v) * GT + t + 1)
                                if half == 0:
                                    settle(pe, pe_held)
                                    nc.tensor.matmul(py[:, t, 0:D], ones[:, :], b2[:, bass.ds(e * D, D)], start=True, stop=False)
                                terms = [(a, b, j) for a, b in ((hh, w2h), (hl, w2h), (hh, w2l)) for j in range(HT)]
                                for n, (a, b, j) in enumerate(terms):
                                    ins = nc.tensor.matmul(py[:, t, 0:D], a[v][:, j, t * P:(t + 1) * P], b[half][:, j, :],
                                                           start=n == 0 and half == 1, stop=n == len(terms) - 1)
                                ins.then_inc(y_ready, 1)

                        hidden(0)
                        hidden(1)
                        outputs(0)
                        outputs(1)

        @block.scalar
        def _(act):
            act.sem_inc(gelu, CREDIT)
            act.wait_ge(loaded, 48)
            act.wait_ge(shifted, 1)
            nc.scalar.activation(sc[:, :, :], sc[:, :, :], ACT.Exp).then_inc(expd, 1)
            with act.Fori(0, EX) as e:
                for half in range(2):
                    with act.Fori(0, NG // 2) as i:
                        for v in range(2):
                            for jj in range(PAIRS):
                                n = ((e * 2 + half) * NG + i * 2 + v) * PAIRS + jj
                                b = (v * PAIRS + jj) % 2
                                act.wait_ge(parted, n + 1)
                                act.wait_ge(h_ready, n + 1)
                                settle(act, held)
                                for j in range(2):
                                    ins = nc.scalar.activation(act_out[b][:, j, :], ph[b][:, j, 0:G], ACT.Gelu, scale=1.0 / W_SCALE,
                                                               bias=b1[:, bass.ds(e * (2 * HT) + (half * HT + 2 * jj + j), 1)])
                                ins.then_inc(gelu, 1)

        @block.vector
        def _(dve):
            dve.sem_inc(parted, CREDIT)
            dve.sem_inc(added, GT)
            dve.wait_ge(loaded, 48)
            nc.vector.memset(ones[:, :], 1.0).then_inc(ones_set, 1)
            nc.vector.tensor_scalar(b2[:, :], b2[:, :], W_SCALE, None, ALU.mult).then_inc(ones_set, 1)
            chain = Chain(dve, steps, None)
            chain(nc.vector.tensor_reduce(row[:, :], sc[:, :, :], AX.X, ALU.max))

            def by_expert(t):
                return t[:, :].rearrange("p (n a) -> p n a", a=1).to_broadcast([P, NT, EX])

            nc.vector.tensor_tensor(sc[:, :, :], sc[:, :, :], by_expert(row), ALU.subtract).then_inc(shifted, 1)
            dve.wait_ge(expd, 1)
            chain(nc.vector.tensor_reduce(row[:, :], sc[:, :, :], AX.X, ALU.add))
            chain(nc.vector.reciprocal(row[:, :], row[:, :]))
            chain(nc.vector.tensor_tensor(sc[:, :, :], sc[:, :, :], by_expert(row), ALU.mult))
            for j in range(EX):
                ins = nc.vector.memset(rank[:, :, j], float(j))
            chain(ins)
            for i in range(EX):
                for j in range(i + 1, EX):
                    chain(nc.vector.tensor_tensor(above[:, :], sc[:, :, j], sc[:, :, i], ALU.is_gt))
                    chain(nc.vector.tensor_tensor(rank[:, :, i], rank[:, :, i], above[:, :], ALU.add))
                    chain(nc.vector.tensor_tensor(rank[:, :, j], rank[:, :, j], above[:, :], ALU.subtract))
            chain(nc.vector.tensor_scalar(rank[:, :, :], rank[:, :, :], 2.0, None, ALU.is_lt))
            chain(nc.vector.tensor_tensor(sc[:, :, :], sc[:, :, :], rank[:, :, :], ALU.mult))
            chain(nc.vector.tensor_reduce(row[:, :], sc[:, :, :], AX.X, ALU.add))
            chain(nc.vector.tensor_scalar(row[:, :], row[:, :], 1e-9, None, ALU.add))
            chain(nc.vector.reciprocal(row[:, :], row[:, :]))
            chain(nc.vector.tensor_tensor(gate[:, :, :], sc[:, :, :], by_expert(row), ALU.mult))
            chain(nc.vector.tensor_scalar(gate[:, :, :], gate[:, :, :], 1.0 / W_SCALE, None, ALU.mult))
            dve.wait_ge(acc_in, 16)
            with dve.Fori(0, EX) as e:
                for half in range(2):
                    with dve.Fori(0, NG // 2) as i:
                        turn0 = (e * 2 + half) * NG + i * 2

                        def part(v):
                            dve.wait_ge(y_ready, (turn0 + v) * GT + (Y_CREDIT - GT))
                            for jj in range(PAIRS):
                                n, b = (turn0 + v) * PAIRS + jj, (v * PAIRS + jj) % 2
                                at = slice(2 * jj, 2 * jj + 2)
                                dve.wait_ge(gelu, n + 1 + CREDIT)
                                nc.vector.tensor_copy(hh[v][:, at, :], act_out[b][:, :, :]).then_inc(high, 1)
                                dve.wait_ge(high, n + 1)
                                nc.vector.tensor_tensor(hl[v][:, at, :], act_out[b][:, :, :], hh[v][:, at, :],
                                                        ALU.subtract).then_inc(parted, 1)

                        def add(v):
                            for t in range(GT):
                                n = (turn0 + v) * GT + t
                                tile = (i * 2 + v) * GT + t
                                dve.wait_ge(y_ready, n + 1 + Y_CREDIT)
                                into = acc[:, bass.ds(tile, 1), :].rearrange("p a d -> p (a d)")
                                nc.vector.scalar_tensor_tensor(out=into, in0=py[:, t, 0:D],
                                                               scalar=gate[:, bass.ds(tile, 1), bass.ds(e, 1)].rearrange("p a b -> p (a b)"), in1=into,
                                                               op0=ALU.mult, op1=ALU.add).then_inc(added, 1)

                        part(0)
                        part(1)
                        add(0)
                        add(1)


def mamba_gate(nc, c, w, x, xn_ch, sz, dt_raw):
    src_g, sz_g = tok_groups(x), tok_groups(sz)
    with Stage(nc, "g") as s:
        ident, epst = s.sb("ident", [P, P]), s.sb("eps", [P, 1])
        wz, wdt = s.sb("wz", [P, DC, DIN]), s.sb("wdt", [P, DC, HEADS])
        xin = [s.sb(f"x{u}", [P, GT, D]) for u in range(2)]
        xn = [s.sb(f"xn{u}", [P, GT, D]) for u in range(2)]
        xt = [s.sb(f"xt{u}", [P, DC, G]) for u in range(2)]
        szt = [s.sb(f"szt{u}", [P, GT, DIN]) for u in range(2)]
        raw = s.sb("raw", [P, NT, HEADS])
        stats, mv = s.sb("stats", [P, GT, 6]), s.sb("mv", [P, GT, 2])
        std, rstd = s.sb("std", [P, 2, GT]), s.sb("rstd", [P, GT])
        pt = s.ps("pt", [P, DC, BANK])
        pz = [s.ps(f"pz{v}", [P, 2, BANK]) for v in range(2)]
        pdt = s.ps("pdt", [P, BANK])
        x_in, xt_out, sz_out = ([s.sem(f"{x}{u}") for u in range(2)] for x in ("x_in", "xt_out", "sz_out"))
        (loaded, eps_set, var_ready, std_ready, normed, steps, turned, copied, z_ready, gated, dt_ready, dt_taken, held,
         dt_out) = (s.sem(x) for x in "loaded eps_set var_ready std_ready normed steps turned copied z_ready gated dt_ready "
                    "dt_taken held dt_out".split())
        block = s.block()

        @block.sync
        def _(sp):
            for tile, src in ((ident[:, :], c["ident"]), (wz[:, :, :], w["w_z"]), (wdt[:, :, :], w["w_dt"])):
                sp.dma_start(tile, src).then_inc(loaded, 16)
            with sp.Fori(0, NG // 2) as i:
                for u in range(2):
                    g = i * 2 + u
                    sp.wait_ge(normed, free(g))
                    sp.dma_start(xin[u][:, :, :], src_g[g]).then_inc(x_in[u], 16)
            sp.wait_ge(dt_taken, NG + 1)
            sp.dma_start(dt_raw, raw[:, :, :]).then_inc(dt_out, 16)
            sp.wait_ge(dt_out, 16)

        @block.vector
        def _(dve):
            nc.vector.memset(epst[:, :], 1e-6).then_inc(eps_set, 1)
            dve.sem_inc(normed, CREDIT)
            dve.sem_inc(dt_taken, 1)
            chain = Chain(dve, steps, NORM_STEPS)

            def norm(g, i, u):
                chain.start(g)
                dve.wait_ge(x_in[u], i * 16 + 16)
                dve.wait_ge(turned, free(g))
                norm_steps(dve, chain, xin[u], stats, mv, std, rstd, xn[u], var_ready, std_ready, g,
                           held).then_inc(normed, 1)

            def take(g):
                dve.wait_ge(dt_ready, g + 1)
                settle(dve, held)
                nc.vector.tensor_copy(raw[:, bass.ds(g * GT, GT), :],
                                      pdt[:, 0:GT * HEADS].rearrange("p (t h) -> p t h", h=HEADS)).then_inc(dt_taken, 1)

            norm(0, 0, 0)
            norm(1, 0, 1)
            with dve.Fori(0, NG // 2 - 1) as i:
                for u in range(2):
                    norm(i * 2 + u + 2, i + 1, u)
                    take(i * 2 + u)
            take(NG - 2)
            take(NG - 1)

        @block.tensor
        def _(pe):
            pe.sem_inc(turned, CREDIT)
            pe.wait_ge(loaded, 48)

            def turn(g, u):
                pe.wait_ge(normed, ready(g))
                pe.wait_ge(copied, g + CREDIT)
                for t in range(GT):
                    for d in range(DC):
                        ins = nc.tensor.transpose(pt[:, d, t * P:(t + 1) * P], xn[u][:, t, d * P:(d + 1) * P],
                                                  ident[:, :])
                ins.then_inc(turned, 1)

            def products(g, u):
                pe.wait_ge(copied, ready(g))
                pe.wait_ge(dt_taken, g + 1)
                for t in range(GT):
                    for d in range(DC):
                        ins = nc.tensor.matmul(pdt[:, t * HEADS:(t + 1) * HEADS], xt[u][:, d, t * P:(t + 1) * P],
                                               wdt[:, d, :], start=d == 0, stop=d == DC - 1)
                ins.then_inc(dt_ready, 1)
                for t in range(GT):
                    v = (u * GT + t) % 2
                    pe.wait_ge(gated, free(g * GT + t))
                    for half in range(2):
                        for d in range(DC):
                            ins = nc.tensor.matmul(pz[v][:, half, 0:D], xt[u][:, d, t * P:(t + 1) * P],
                                                   wz[:, d, half * D:(half + 1) * D], start=d == 0, stop=d == DC - 1)
                    ins.then_inc(z_ready, 1)

            turn(0, 0)
            turn(1, 1)
            with pe.Fori(0, NG // 2 - 1) as i:
                for u in range(2):
                    products(i * 2 + u, u)
                    turn(i * 2 + u + 2, u)
            products(NG - 2, 0)
            products(NG - 1, 1)

        @block.scalar
        def _(act):
            act.sem_inc(copied, CREDIT)
            act.sem_inc(gated, CREDIT)
            for u in range(2):
                act.sem_inc(xt_out[u], 16)
                act.sem_inc(sz_out[u], 16)
            act.wait_ge(eps_set, 1)

            def root(g):
                act.wait_ge(var_ready, g + 1)
                nc.scalar.activation(std[:, 1, :], std[:, 0, :], ACT.Sqrt, bias=epst[:, :]).then_inc(std_ready, 1)

            def copy(g, i, u):
                act.wait_ge(turned, ready(g))
                act.wait_ge(xt_out[u], i * 16 + 16)
                nc.scalar.copy(xt[u][:, :, :], pt[:, :, 0:G]).then_inc(copied, 1)
                act.wait_ge(copied, ready(g))
                act.dma_start(xn_ch[:, :, bass.ds(g * G, G)], xt[u][:, :, :]).then_inc(xt_out[u], 16)

            def gates(g, i, u):
                act.wait_ge(sz_out[u], i * 16 + 16)
                for t in range(GT):
                    v = (u * GT + t) % 2
                    act.wait_ge(z_ready, g * GT + t + 1)
                    nc.scalar.activation(szt[u][:, t, :].rearrange("p (a d) -> p a d", a=2), pz[v][:, :, 0:D],
                                         ACT.Silu).then_inc(gated, 1)

            def store(g, u):
                act.wait_ge(gated, g * GT + GT + CREDIT)
                act.dma_start(sz_g[g], szt[u][:, :, :]).then_inc(sz_out[u], 16)

            for u in range(2):
                root(u)
                copy(u, 0, u)
            with act.Fori(0, NG // 2 - 1) as i:
                for u in range(2):
                    g = i * 2 + u
                    root(g + 2)
                    gates(g, i, u)
                    copy(g + 2, i + 1, u)
                    store(g, u)
            for u in range(2):
                gates(NG - 2 + u, NG // 2 - 1, u)
                store(NG - 2 + u, u)
            for u in range(2):
                act.wait_ge(xt_out[u], 16 * (NG // 2 + 1))
                act.wait_ge(sz_out[u], 16 * (NG // 2 + 1))


CT = -(-CONV // P)


def mamba_conv(nc, w, xn_ch, xbc):
    with Stage(nc, "v") as s:
        xn = s.sb("xn", [P, IMAGES, DC, L])
        wct = [s.sb(f"wct{b}", [P, DC, P]) for b in range(IMAGES)]
        taps, bias = s.sb("taps", [P, CT, 9]), s.sb("bias", [P, CT])
        pad = [s.sb(f"pad{b}", [P, SIDE + 2, SIDE + 2]) for b in range(IMAGES)]
        acc = [s.sb(f"acc{b}", [P, L]) for b in range(IMAGES)]
        out = [s.sb(f"out{b}", [P, L]) for b in range(IMAGES)]
        pi = [s.ps(f"pi{v}", [P, BANK]) for v in range(2)]
        w_in, stored = ([s.sem(f"{x}{b}") for b in range(IMAGES)] for x in ("w_in", "stored"))
        loaded, xn_in, zeroed, projected, padded, tapped, convolved, active, held, pe_held = (s.sem(x) for x in (
            "loaded xn_in zeroed projected padded tapped convolved active held pe_held".split()))
        block = s.block()

        @block.sync
        def _(sp):
            for b in range(IMAGES):
                sp.sem_inc(stored[b], 16)
            sp.dma_start(taps[:, :, :], w["conv1"]).then_inc(loaded, 16)
            sp.dma_start(bias[:, :], w["conv1_b"]).then_inc(loaded, 16)
            for b in range(IMAGES):
                sp.dma_start(wct[b][:, :, :], w["w_x"][0]).then_inc(w_in[b], 16)
                sp.dma_start(xn[:, b, :, :], xn_ch[:, :, b * L:(b + 1) * L]).then_inc(xn_in, 16)
            with sp.Fori(1, CT) as ct:
                for b in range(IMAGES):
                    turn = ct * 2 + b
                    sp.wait_ge(projected, (turn - 1) * GI + CREDIT)
                    sp.dma_start(wct[b][:, :, :], w["w_x"][ct]).then_inc(w_in[b], 16)
                    sp.wait_ge(active, turn - 2 + CREDIT + 1)
                    sp.dma_start(xbc[ct - 1, :, b * L:(b + 1) * L], out[b][:, :]).then_inc(stored[b], 16)
            for b in range(IMAGES):
                sp.wait_ge(active, ready(2 * (CT - 1) + b))
                sp.dma_start(xbc[CT - 1, :, b * L:(b + 1) * L], out[b][:, :]).then_inc(stored[b], 16)
            for b in range(IMAGES):
                sp.wait_ge(stored[b], 16 * (CT + 1))

        @block.gpsimd
        def _(pool):
            for b in range(IMAGES):
                nc.gpsimd.memset(pad[b][:, :, :], 0.0).then_inc(zeroed, 1)

        @block.tensor
        def _(pe):
            pe.sem_inc(projected, CREDIT)
            with pe.Fori(0, CT) as ct:
                for b in range(IMAGES):
                    pe.wait_ge(w_in[b], ct * 16 + 16)
                    pe.wait_ge(xn_in, 32)
                    settle(pe, pe_held)
                    with pe.Fori(0, GI // 2) as i:
                        for v in range(2):
                            q = i * 2 + v
                            pe.wait_ge(padded, free((ct * 2 + b) * GI + q))
                            for d in range(DC):
                                ins = nc.tensor.matmul(pi[v][:, 0:G], wct[b][:, d, :], xn[:, b, d, bass.ds(q * G, G)],
                                                       start=d == 0, stop=d == DC - 1)
                            ins.then_inc(projected, 1)

        @block.vector
        def _(dve):
            dve.sem_inc(convolved, CREDIT)
            dve.wait_ge(loaded, 32)
            chain = Chain(dve, tapped, 8)
            with dve.Fori(0, CT) as ct:
                for b in range(IMAGES):
                    turn = ct * 2 + b
                    chain.start(turn)
                    dve.wait_ge(padded, (turn + 1) * GI + CREDIT)
                    dve.wait_ge(active, turn + 1)
                    view = acc[b][:, :].rearrange("p (h w) -> p h w", w=SIDE)
                    for t in range(9):
                        tap = taps[:, bass.ds(ct, 1), t:t + 1].rearrange("p a b -> p (a b)")
                        rows = pad[b][:, t // 3:t // 3 + SIDE, t % 3:t % 3 + SIDE]
                        if t == 0:
                            ins = nc.vector.tensor_scalar(view, rows, tap, None, ALU.mult)
                        else:
                            ins = nc.vector.scalar_tensor_tensor(out=view, in0=rows, scalar=tap, in1=view,
                                                                 op0=ALU.mult, op1=ALU.add)
                        if t < 8:
                            chain(ins)
                    ins.then_inc(convolved, 1)

        @block.scalar
        def _(act):
            act.sem_inc(padded, CREDIT)
            act.sem_inc(active, 2)
            act.wait_ge(loaded, 32)
            act.wait_ge(zeroed, 2)

            def copies(ct, b):
                turn = ct * 2 + b
                act.wait_ge(convolved, free(turn))
                settle(act, held)
                with act.Fori(0, GI // 2) as i:
                    for v in range(2):
                        q = i * 2 + v
                        act.wait_ge(projected, ready(turn * GI + q))
                        settle(act, held)
                        nc.scalar.copy(pad[b][:, bass.ds(q * ROWS + 1, ROWS), 1:SIDE + 1],
                                       pi[v][:, 0:G].rearrange("p (h w) -> p h w", w=SIDE)).then_inc(padded, 1)

            def silu(ct, b):
                act.wait_ge(convolved, ready(ct * 2 + b))
                act.wait_ge(stored[b], ct * 16 + 16)
                settle(act, held)
                nc.scalar.activation(out[b][:, :], acc[b][:, :], ACT.Silu, bias=bias[:, bass.ds(ct, 1)]).then_inc(active, 1)

            copies(0, 0)
            copies(0, 1)
            silu(0, 0)
            with act.Fori(1, CT) as ct:
                copies(ct, 0)
                silu(ct - 1, 1)
                copies(ct, 1)
                silu(ct, 0)
            silu(CT - 1, 1)


NQ = L // P
HH = HEADS // 2
B_AT, CUM, SUF, TOT, SMALL = P, P + NS, P + NS + HEADS, P + NS + 2 * HEADS, P + NS + 3 * HEADS


def mamba_scan(nc, c, w, x, sz, dt_raw, xbc, out):
    with Stage(nc, "s") as s:
        ident, upto, beyond = s.sb("ident", [P, P]), s.sb("upto", [P, P]), s.sb("beyond", [P, P])
        ones = s.sb("ones", [P, P])
        wo = s.sb("wo", [P, SLOTS, D])
        d1, gamma, beta = s.sb("d1", [P, DIN]), s.sb("gamma", [P, DIN]), s.sb("beta", [P, DIN])
        dtb, alog, epst = s.sb("dtb", [P, HEADS]), s.sb("alog", [P, HEADS]), s.sb("eps", [P, 1])
        ln_one = s.sb("ln_one", [P, 2])
        raw, e, one_e, ln, corr = (s.sb(x, [P, NT, HEADS]) for x in ("raw", "e", "one_e", "ln", "corr"))
        da = s.sb("da", [P, NT, 2 * HEADS])

        def both(name, shape):
            return [s.sb(f"{name}{b}", shape) for b in range(IMAGES)]

        xc, bt, ctr = both("xc", [P, SLOTS, P]), both("bt", [NS, P]), both("ct", [NS, P])
        szt, xin, xo = both("szt", [P, DIN]), both("xin", [P, D]), both("xo", [P, D])
        dab, r = both("dab", [P, 2 * HEADS]), both("r", [P, HEADS, P])
        xs, xdt, xde, xd1 = both("xs", [P, DIN]), both("xdt", [P, DIN]), both("xde", [P, DIN]), both("xd1", [P, DIN])
        gs, es = both("gs", [P, SMALL]), both("es", [P, 3 * HEADS])
        y, state, yts = both("y", [P, DIN]), both("state", [NS, DIN]), both("yts", [P, SLOTS, P])
        gm, ex, m = s.sb("gm", [P, P]), s.sb("ex", [P, HEADS, P]), s.sb("m", [P, HEADS, P])
        stats = s.sb("stats", [P, 2, 6])
        mv, lnv, rstd = both("mv", [P, 2]), both("lnv", [P, 2]), both("rstd", [P, 1])
        px, psm, pd, py = (s.ps("px", [P, 2, BANK]), s.ps("psm", [P, BANK]), s.ps("pd", [P, 3, BANK]),
                           s.ps("py", [P, 2, BANK]))
        xc_in, tok_in, xo_out = ([s.sem(f"{x}{b}") for b in range(IMAGES)] for x in ("xc_in", "tok_in", "xo_out"))
        (loaded, set_up, a_exp, e_ready, one_ready, ln_ready, steps0, prepared, x_turned, x_copied, sums_ready, gs_ready,
         es_ready, d_ready, ex_ready, dab_ready, r_ready, xd_ready, xde_ready, xdt_ready, m_ready, ydiag, yoff, ds_ready,
         weighed, updated, steps, var_ready, rstd_ready, gated, yt_ready, yt_copied, out_ready, added, held, act_steps,
         pool_held, pe_held, one_set, gm_ready, gate_steps) = (s.sem(x) for x in (
             "loaded set_up a_exp e_ready one_ready ln_ready steps0 prepared x_turned x_copied sums_ready gs_ready "
             "es_ready d_ready ex_ready dab_ready r_ready xd_ready xde_ready xdt_ready m_ready ydiag yoff ds_ready "
             "weighed updated steps var_ready rstd_ready gated yt_ready yt_copied out_ready added held act_steps "
             "pool_held pe_held one_set gm_ready gate_steps").split())
        block = s.block()

        def heads(t):
            return t.rearrange("p (h a) -> p h a", a=1).to_broadcast([P, HEADS, HP])

        def by_head(t):
            return t[:, :].rearrange("p (h c) -> p h c", h=HEADS)

        def banks(t):
            return t.rearrange("p (a d) -> p a d", a=2)

        @block.sync
        def _(sp):
            for tile, src in ((raw[:, :, :], dt_raw), (dtb[:, :], w["dt1_b"]), (alog[:, :], w["a1_log"]),
                              (ident[:, :], c["ident"]), (upto[:, :], c["upto"]), (beyond[:, :], c["beyond"]),
                              (d1[:, :], w["d1"]), (gamma[:, :], w["gamma"]), (beta[:, :], w["beta"]), (wo[:, :, :], w["w_out1"])):
                sp.dma_start(tile, src).then_inc(loaded, 16)
            xt, szg, xg, og = (a.rearrange("(b q p) d -> b q p d", b=IMAGES, p=P) for a in (x, sz, x, out))
            bc_rows = xbc[SLOTS]

            def load(q, b):
                at = bass.ds(q * P + b * L, P)
                sp.wait_ge(x_turned, free(q * 2 + b))
                sp.wait_ge(yoff, q * 2 + b + CREDIT - 1)
                sp.dma_start(xc[b][:, :, :], xbc[0:SLOTS].rearrange("s p t -> p s t")[:, :, at]).then_inc(xc_in[b], 16)
                sp.dma_start(bt[b][:, :], bc_rows[0:NS, at]).then_inc(xc_in[b], 16)
                sp.dma_start(ctr[b][:, :], bc_rows[NS:2 * NS, at]).then_inc(xc_in[b], 16)

            def load_tok(q, b):
                sp.wait_ge(added, free(q * 2 + b))
                sp.dma_start(szt[b][:, :], szg[b, q]).then_inc(tok_in[b], 16)
                sp.dma_start(xin[b][:, :], xg[b, q]).then_inc(tok_in[b], 16)

            for b in range(IMAGES):
                sp.sem_inc(xo_out[b], 16)
                load(0, b)
                load_tok(0, b)
            with sp.Fori(1, NQ) as q:
                for b in range(IMAGES):
                    load(q, b)
                    load_tok(q, b)
                    sp.dma_start(og[b, q - 1], xo[b][:, :]).then_inc(xo_out[b], 16)
            for b in range(IMAGES):
                sp.wait_ge(added, free(NQ * 2 + b))
                sp.dma_start(og[b, NQ - 1], xo[b][:, :]).then_inc(xo_out[b], 16)
            for b in range(IMAGES):
                sp.wait_ge(xo_out[b], 16 * (NQ + 1))

        @block.tensor
        def _(pe):
            pe.sem_inc(x_turned, CREDIT)
            pe.sem_inc(d_ready, CREDIT)
            pe.sem_inc(yoff, CREDIT)
            pe.wait_ge(loaded, 160)
            pe.wait_ge(set_up, 4)

            def front(q, b):
                turn = q * 2 + b
                pe.wait_ge(xc_in[b], q * 48 + 48)
                pe.wait_ge(weighed, turn + 1)
                for j in range(SLOTS):
                    ins = nc.tensor.transpose(px[:, j // DC, (j % DC) * P:(j % DC + 1) * P], xc[b][:, j, :], ident[:, :])
                ins.then_inc(x_turned, 1)
                pe.wait_ge(gs_ready, turn + 1)
                pe.wait_ge(dab_ready, turn + CREDIT + 1)
                settle(pe, pe_held)
                a = dab[b][:, HEADS:2 * HEADS]
                nc.tensor.matmul(psm[:, 0:P], bt[b][:, :], ctr[b][:, :], start=True, stop=True)
                nc.tensor.transpose(psm[:, B_AT:CUM], bt[b][:, :], ident[0:NS, 0:NS])
                nc.tensor.matmul(psm[:, CUM:SUF], upto[:, :], a, start=True, stop=True)
                nc.tensor.matmul(psm[:, SUF:TOT], beyond[:, :], a, start=True, stop=True)
                nc.tensor.matmul(psm[:, TOT:SMALL], ones[:, :], a, start=True, stop=True).then_inc(sums_ready, 1)
                pe.wait_ge(r_ready, turn + 1)
                pe.wait_ge(updated, turn + 1)
                for j in range(3):
                    ins = nc.tensor.matmul(pd[:, j, :], beyond[:, :], r[b][:, 4 * j:4 * j + 4, :], start=True, stop=True)
                ins.then_inc(d_ready, 1)

            def middle(q, b):
                turn = q * 2 + b
                pe.wait_ge(m_ready, ready(turn))
                pe.wait_ge(added, free(turn))
                for h in range(HEADS):
                    at = (h % HH) * HP
                    ins = nc.tensor.matmul(py[:, h // HH, at:at + HP], m[:, h, :], xdt[b][:, h * HP:(h + 1) * HP],
                                           start=True, stop=True)
                ins.then_inc(ydiag, 1)
                for half in range(2):
                    ins = nc.tensor.matmul(px[:, half, 0:D], ctr[b][:, :], state[b][:, half * D:(half + 1) * D], start=True, stop=True)
                ins.then_inc(yoff, 1)
                pe.wait_ge(xde_ready, turn + 1)
                for half in range(2):
                    ins = nc.tensor.matmul(pd[0:NS, half, 0:D], gs[b][:, B_AT:CUM], xde[b][:, half * D:(half + 1) * D],
                                           start=True, stop=True)
                ins.then_inc(ds_ready, 1)

            def tail(q, b, ahead=2):
                turn = q * 2 + b
                last_updated = turn + 1 + ahead
                pe.wait_ge(gated, turn + 1)
                pe.wait_ge(updated, last_updated)
                for j in range(SLOTS):
                    ins = nc.tensor.transpose(py[:, j // DC, (j % DC) * P:(j % DC + 1) * P], y[b][:, j * P:(j + 1) * P], ident[:, :])
                ins.then_inc(yt_ready, 1)
                pe.wait_ge(yt_copied, turn + 1)
                for j in range(SLOTS):
                    ins = nc.tensor.matmul(py[:, 0, 0:D], yts[b][:, j, :], wo[:, j, :], start=j == 0, stop=j == SLOTS - 1)
                ins.then_inc(out_ready, 1)

            front(0, 0)
            middle(0, 0)
            front(0, 1)
            with pe.Fori(0, NQ - 1) as q:
                for b in range(IMAGES):
                    middle(q + b, 1 - b)
                    front(q + 1, b)
                    tail(q, b)
            middle(NQ - 1, 1)
            tail(NQ - 1, 0)
            tail(NQ - 1, 1, ahead=1)

        @block.scalar
        def _(act):
            nc.scalar.preload_act_table_set("natural_log_exp_and_others")
            act.sem_inc(gs_ready, 1)
            act.wait_ge(set_up, 4)
            act.wait_ge(one_set, 1)
            nc.scalar.activation(ln_one[:, 1:2], ln_one[:, 0:1], ACT.Ln)
            act.wait_ge(loaded, 160)
            nc.scalar.activation(alog[:, :], alog[:, :], ACT.Exp).then_inc(a_exp, 1)
            act.wait_ge(steps0, 2)
            nc.scalar.activation(e[:, :, :], e[:, :, :], ACT.Exp, scale=-1.0).then_inc(e_ready, 1)
            act.wait_ge(one_ready, 1)
            nc.scalar.activation(ln[:, :, :], one_e[:, :, :], ACT.Ln).then_inc(ln_ready, 1)
            chain = Chain(act, act_steps, 1)

            def turn_x(q, b):
                act.wait_ge(x_turned, ready(q * 2 + b))
                nc.scalar.copy(banks(xs[b][:, :]), px[:, :, 0:D]).then_inc(x_copied, 1)

            def root(q, b):
                turn = q * 2 + b
                act.wait_ge(var_ready, turn + 1)
                chain.start(turn)
                chain(nc.scalar.activation(lnv[b][:, 1:2], lnv[b][:, 0:1], ACT.Ln, bias=epst[:, :]))
                nc.scalar.activation(rstd[b][:, :], lnv[b][:, 1:2], ACT.Exp, scale=-0.5).then_inc(rstd_ready, 1)

            def decays(q, b, root_at=None):
                turn = q * 2 + b
                act.wait_ge(sums_ready, turn + 1)
                nc.scalar.copy(gs[b][:, :], psm[:, 0:SMALL]).then_inc(gs_ready, 1)
                act.wait_ge(gs_ready, turn + 2)
                nc.scalar.activation(es[b][:, :], gs[b][:, CUM:SMALL], ACT.Exp).then_inc(es_ready, 1)
                if root_at:
                    root(*root_at)
                act.wait_ge(d_ready, ready(turn))
                act.wait_ge(m_ready, turn + CREDIT)
                nc.scalar.activation(ex[:, :, :].rearrange("p (j h) l -> p j (h l)", j=3), pd[:, :, :], ACT.Exp).then_inc(ex_ready, 1)

            def turn_y(q, b):
                turn = q * 2 + b
                act.wait_ge(yt_ready, turn + 1)
                nc.scalar.copy(yts[b][:, :, :].rearrange("p (a j) l -> p a (j l)", a=2), py[:, :, 0:D]).then_inc(yt_copied, 1)

            turn_x(0, 0)
            decays(0, 0)
            turn_x(0, 1)
            root(0, 0)
            decays(0, 1)
            with act.Fori(0, NQ - 1) as q:
                for b in range(IMAGES):
                    turn_x(q + 1, b)
                    decays(q + 1, b, root_at=(q + b, 1 - b))
                    turn_y(q, b)
            root(NQ - 1, 1)
            turn_y(NQ - 1, 0)
            turn_y(NQ - 1, 1)

        @block.gpsimd
        def _(pool):
            nc.gpsimd.memset(ones[:, :], 1.0).then_inc(set_up, 1)
            nc.gpsimd.memset(epst[:, :], 1e-5).then_inc(set_up, 1)
            nc.gpsimd.memset(state[0][:, :], 0.0).then_inc(set_up, 1)
            nc.gpsimd.memset(state[1][:, :], 0.0).then_inc(set_up, 1)
            pool.sem_inc(dab_ready, CREDIT)
            pool.wait_ge(set_up, 4)
            pool.wait_ge(loaded, 160)
            pool.wait_ge(prepared, 2)
            with pool.Fori(0, NQ) as q:
                for b in range(IMAGES):
                    turn = q * 2 + b
                    pool.wait_ge(m_ready, free(turn))
                    pool.wait_ge(d_ready, free(turn))
                    settle(pool, pool_held)
                    nc.gpsimd.tensor_tensor(dab[b][:, :], da[:, bass.ds(b * NQ + q, 1), :].rearrange("p a h -> p (a h)"),
                                            ones[:, 0:2 * HEADS], ALU.mult).then_inc(dab_ready, 1)
                    pool.wait_ge(dab_ready, ready(turn))
                    nc.gpsimd.tensor_tensor(r[b][:, :, :],
                                            dab[b][:, HEADS:].rearrange("p (h a) -> p h a", a=1).to_broadcast([P, HEADS, P]),
                                            upto[:, :].rearrange("p (a l) -> p a l", a=1).to_broadcast([P, HEADS, P]),
                                            ALU.mult).then_inc(r_ready, 1)
                    pool.wait_ge(x_copied, turn + 1)
                    nc.gpsimd.tensor_tensor(xd1[b][:, :], xs[b][:, :], d1[:, :], ALU.mult).then_inc(xd_ready, 1)
                    pool.wait_ge(xdt_ready, turn + 1)
                    pool.wait_ge(es_ready, turn + 1)
                    nc.gpsimd.tensor_tensor(by_head(xde[b]), by_head(xdt[b]), heads(es[b][:, HEADS:2 * HEADS]),
                                            ALU.mult).then_inc(xde_ready, 1)

        @block.vector
        def _(dve):
            dve.sem_inc(weighed, 1)
            dve.sem_inc(updated, 1)
            dve.sem_inc(added, CREDIT)
            dve.sem_inc(m_ready, CREDIT)
            nc.vector.memset(ln_one[:, 0:1], 1.0).then_inc(one_set, 1)
            dve.wait_ge(loaded, 160)
            once = Chain(dve, steps0, None)

            def tiles(t):
                return t[:, :].rearrange("p (a h) -> p a h", a=1).to_broadcast([P, NT, HEADS])

            once(nc.vector.tensor_tensor(raw[:, :, :], raw[:, :, :], tiles(dtb), ALU.add))
            once(nc.vector.scalar_tensor_tensor(out=e[:, :, :], in0=raw[:, :, :], scalar=-1.0, in1=raw[:, :, :],
                                                op0=ALU.mult, op1=ALU.max))
            dve.wait_ge(e_ready, 1)
            nc.vector.tensor_scalar(one_e[:, :, :], e[:, :, :], 1.0, None, ALU.add).then_inc(one_ready, 1)
            dve.wait_ge(one_ready, 1)
            once(nc.vector.scalar_tensor_tensor(out=corr[:, :, :], in0=one_e[:, :, :], scalar=1.0, in1=e[:, :, :],
                                                op0=ALU.subtract, op1=ALU.subtract))
            dve.wait_ge(ln_ready, 1)
            once(nc.vector.scalar_tensor_tensor(out=corr[:, :, :], in0=ln[:, :, :], scalar=ln_one[:, 1:2], in1=corr[:, :, :],
                                                op0=ALU.subtract, op1=ALU.subtract))
            nc.vector.scalar_tensor_tensor(out=da[:, :, 0:HEADS], in0=raw[:, :, :], scalar=0.0, in1=corr[:, :, :],
                                           op0=ALU.max, op1=ALU.add).then_inc(prepared, 1)
            dve.wait_ge(prepared, 1)
            dve.wait_ge(a_exp, 1)
            nc.vector.scalar_tensor_tensor(out=da[:, :, HEADS:], in0=da[:, :, 0:HEADS], scalar=-1.0, in1=tiles(alog),
                                           op0=ALU.mult, op1=ALU.mult).then_inc(prepared, 1)
            chain = Chain(dve, steps, 6)
            gate_chain = Chain(dve, gate_steps, 3)

            def weights(q, b):
                turn = q * 2 + b
                dve.wait_ge(x_copied, turn + 1)
                dve.wait_ge(dab_ready, ready(turn))
                nc.vector.tensor_tensor(by_head(xdt[b]), by_head(xs[b]), heads(dab[b][:, 0:HEADS]), ALU.mult).then_inc(xdt_ready, 1)
                dve.wait_ge(gs_ready, turn + 2)
                nc.vector.tensor_tensor(gm[:, :], gs[b][:, 0:P], upto[:, :], ALU.mult).then_inc(gm_ready, 1)
                dve.wait_ge(gm_ready, turn + 1)
                dve.wait_ge(ex_ready, turn + 1)
                nc.vector.tensor_tensor(m[:, :, :], ex[:, :, :],
                                        gm[:, :].rearrange("p (a l) -> p a l", a=1).to_broadcast([P, HEADS, P]),
                                        ALU.mult).then_inc(m_ready, 1)

            def outputs(q, b):
                turn = q * 2 + b
                chain.start(turn)
                yv = banks(y[b][:, :])
                dve.wait_ge(yoff, ready(turn))
                dve.wait_ge(es_ready, turn + 1)
                nc.vector.tensor_tensor(y[b][:, :].rearrange("p (a h c) -> p a h c", a=2, h=HH),
                                        px[:, :, 0:D].rearrange("p a (h c) -> p a h c", h=HH),
                                        es[b][:, 0:HEADS].rearrange("p (a h c) -> p a h c", a=2, c=1).to_broadcast([P, 2, HH, HP]),
                                        ALU.mult).then_inc(weighed, 1)
                chain.mark(nc.vector.tensor_tensor(by_head(state[b]), by_head(state[b]),
                                                   es[b][0:NS, 2 * HEADS:].rearrange("p (h a) -> p h a", a=1).to_broadcast([NS, HEADS, HP]),
                                                   ALU.mult))
                dve.wait_ge(weighed, turn + 2)
                dve.wait_ge(ydiag, turn + 1)
                chain(nc.vector.tensor_tensor(yv, yv, py[:, :, 0:D], ALU.add))
                dve.wait_ge(ds_ready, turn + 1)
                sv = banks(state[b][:, :])
                nc.vector.tensor_tensor(sv, sv, pd[0:NS, 0:2, 0:D], ALU.add).then_inc(updated, 1)
                dve.wait_ge(xd_ready, turn + 1)
                chain(nc.vector.tensor_tensor(y[b][:, :], y[b][:, :], xd1[b][:, :], ALU.add))
                for half in range(2):
                    chain.mark(nc.vector.bn_stats(stats[:, half, :], y[b][:, half * D:(half + 1) * D]))
                chain.wait()
                settle(dve, held)
                chain(nc.vector.bn_aggr(mv[b][:, :], stats[:, :, :]))
                nc.vector.tensor_copy(lnv[b][:, 0:1], mv[b][:, 1:2]).then_inc(var_ready, 1)

            def gate(q, b):
                turn = q * 2 + b
                gate_chain.start(turn)
                dve.wait_ge(rstd_ready, turn + 1)
                gate_chain(nc.vector.tensor_scalar(y[b][:, :], y[b][:, :], mv[b][:, 0:1], rstd[b][:, :], ALU.subtract, ALU.mult))
                gate_chain(nc.vector.tensor_tensor(y[b][:, :], y[b][:, :], gamma[:, :], ALU.mult))
                gate_chain(nc.vector.tensor_tensor(y[b][:, :], y[b][:, :], beta[:, :], ALU.add))
                dve.wait_ge(tok_in[b], q * 32 + 32)
                nc.vector.tensor_tensor(y[b][:, :], y[b][:, :], szt[b][:, :], ALU.mult).then_inc(gated, 1)

            def add(q, b):
                dve.wait_ge(out_ready, q * 2 + b + 1)
                dve.wait_ge(xo_out[b], q * 16 + 16)
                nc.vector.tensor_tensor(xo[b][:, :], py[:, 0, 0:D], xin[b][:, :], ALU.add).then_inc(added, 1)

            weights(0, 0)
            outputs(0, 0)
            weights(0, 1)
            with dve.Fori(0, NQ - 1) as q:
                for b in range(IMAGES):
                    gate(q, b)
                    outputs(q + b, 1 - b)
                    weights(q + 1, b)
                    add(q, b)
            gate(NQ - 1, 0)
            outputs(NQ - 1, 1)
            add(NQ - 1, 0)
            gate(NQ - 1, 1)
            add(NQ - 1, 1)



FT = FF // P
HPAIRS = FT // 2
X_SCALE = 16.0
XBUFS = 4


def kron_ffn(nc, c, w, x, out):
    x_g, out_g = tok_groups(x), tok_groups(out)
    with Stage(nc, "f") as s:
        ident, epst = s.sb("ident", [P, P]), s.sb("eps", [P, 1])
        fc1, pj1 = s.sb("fc1", [3 * KR, FF]), s.sb("pj1", [P, FT, KR])
        ident16, fc1p = s.sb("ident16", [P, P], F16), s.sb("fc1p", [3 * KR, FF], F16)
        fc2, pj2 = s.sb("fc2", [P, KJ]), s.sb("pj2", [P, KJ])
        xin = [s.sb(f"x{u}", [P, GT, D]) for u in range(XBUFS)]
        xo = [s.sb(f"xo{u}", [P, GT, D]) for u in range(2)]
        xn, prod = s.sb("xn", [P, GT, D]), s.sb("prod", [P, GT, D])
        xr = s.sb("xr", [P, GT, KR])
        xp = [s.sb(f"xp{u}", [P, GT, 3, KR], F16) for u in range(2)]
        xpt = [s.sb(f"xpt{u}", [3 * KR, G], F16) for u in range(2)]
        ot = s.sb("ot", [KR, G])
        h = [s.sb(f"h{u}", [P, FT, G]) for u in range(2)]
        o = s.sb("o", [P, GT, KR])
        stats, mv = s.sb("stats", [P, GT, 6]), s.sb("mv", [P, GT, 2])
        std, rstd = s.sb("std", [P, 2, GT]), s.sb("rstd", [P, GT])
        pt, pot, po = s.ps("pt", [3 * KR, 2 * BANK], F16), s.ps("pot", [KR, BANK]), s.ps("po", [P, BANK])
        ph = [s.ps(f"ph{v}", [P, 2, BANK]) for v in range(2)]
        x_in, x_out = ([s.sem(f"{x}{u}") for u in range(XBUFS)] for x in ("x_in", "x_out"))
        (loaded, eps_set, var_ready, std_ready, steps, osteps, reduced, turned, copied, h_ready, gelu, o_ready, o_taken, added, held, split,
         ot_ready, ot_copied, pe_held) = (
            s.sem(x) for x in "loaded eps_set var_ready std_ready steps osteps reduced turned copied h_ready gelu o_ready "
            "o_taken added held split ot_ready ot_copied pe_held".split())
        block = s.block()

        @block.sync
        def _(sp):
            for u in range(XBUFS):
                sp.sem_inc(x_out[u], 16)
            for tile, src in ((ident[:, :], c["ident"]), (fc1[:, :], w["fc1"]), (pj1[:, :, :], w["pj1"]), (fc2[:, :], w["fc2"]),
                              (pj2[:, :], w["pj2"])):
                sp.dma_start(tile, src).then_inc(loaded, 16)
            for u in range(XBUFS):
                sp.dma_start(xin[u][:, :, :], x_g[u]).then_inc(x_in[u], 16)
            with sp.Fori(0, NG // XBUFS - 1) as i:
                for u in range(XBUFS):
                    g = i * XBUFS + u
                    sp.wait_ge(added, g + 1)
                    sp.dma_start(out_g[g], xo[u % 2][:, :, :]).then_inc(x_out[u], 16)
                    sp.dma_start(xin[u][:, :, :], x_g[g + XBUFS]).then_inc(x_in[u], 16)
            for u in range(XBUFS):
                sp.wait_ge(added, NG - XBUFS + u + 1)
                sp.dma_start(out_g[NG - XBUFS + u], xo[u % 2][:, :, :]).then_inc(x_out[u], 16)
            for u in range(XBUFS):
                sp.wait_ge(x_out[u], 16 * (NG // XBUFS + 1))

        @block.vector
        def _(dve):
            nc.vector.memset(epst[:, :], 1e-5).then_inc(eps_set, 1)
            dve.sem_inc(o_taken, 1)
            dve.wait_ge(loaded, 80)
            nc.vector.tensor_copy(ident16[:, :], ident[:, :]).then_inc(split, 1)
            nc.vector.tensor_scalar(fc1[:, :], fc1[:, :], W_SCALE, None, ALU.mult).then_inc(split, 1)
            dve.wait_ge(split, 2)
            nc.vector.tensor_copy(fc1p[:, :], fc1[:, :]).then_inc(split, 1)
            dve.wait_ge(split, 3)
            low = slice(KR, 2 * KR)
            nc.vector.tensor_tensor(fc1p[low, :], fc1[low, :], fc1p[low, :], ALU.subtract).then_inc(split, 1)
            chain = Chain(dve, steps, NORM_STEPS + 5)
            ochain = Chain(dve, osteps, 1)

            def reduce(g, i, x, u):
                chain.start(g)
                dve.wait_ge(x_in[x], i * 16 + 16)
                chain(norm_steps(dve, chain, xin[x], stats, mv, std, rstd, xn, var_ready, std_ready, g, held))
                chain(nc.vector.tensor_tensor(prod[:, :, :].rearrange("p t (i j) -> p (t i) j", j=KJ),
                                              xn[:, :, :].rearrange("p t (i j) -> p (t i) j", j=KJ),
                                              fc2[:, :].rearrange("p (a j) -> p a j", a=1).to_broadcast([P, GT * KR, KJ]), ALU.mult))
                chain(nc.vector.tensor_reduce(xr[:, :, :].rearrange("p t i -> p (t i)"),
                                              prod[:, :, :].rearrange("p t (i j) -> p (t i) j", j=KJ), AX.X, ALU.add))
                chain(nc.vector.tensor_scalar(xr[:, :, :], xr[:, :, :], X_SCALE, None, ALU.mult))
                dve.wait_ge(turned, free(g))
                for part in range(2):
                    ins = nc.vector.tensor_copy(xp[u][:, :, part, :], xr[:, :, :])
                chain(ins)
                nc.vector.tensor_tensor(xp[u][:, :, 2, :], xr[:, :, :], xp[u][:, :, 0, :], ALU.subtract).then_inc(reduced, 1)

            def spread(g, i, x, u):
                ochain.start(g)
                dve.wait_ge(o_ready, g + 1)
                nc.vector.tensor_copy(o[:, :, :].rearrange("p t i -> p (t i)"), po[:, 0:GT * KR]).then_inc(o_taken, 1)
                dve.wait_ge(o_taken, g + 2)
                dve.wait_ge(x_out[(x + 2) % XBUFS], i * 16 + (32 if x >= 2 else 16))
                view = xo[u][:, :, :].rearrange("p t (i j) -> p (t i) j", j=KJ)
                ochain(nc.vector.tensor_tensor(view,
                                               o[:, :, :].rearrange("p t (i a) -> p (t i) a", a=1).to_broadcast([P, GT * KR, KJ]),
                                               pj2[:, :].rearrange("p (a j) -> p a j", a=1).to_broadcast([P, GT * KR, KJ]), ALU.mult))
                nc.vector.tensor_tensor(xo[u][:, :, :], xo[u][:, :, :], xin[x][:, :, :], ALU.add).then_inc(added, 1)

            def step(i, x):
                g = i * XBUFS + x
                if isinstance(i, int) and g + 2 >= NG:
                    return spread(g, i, x, x % 2)
                reduce(g + 2, i + (x + 2) // XBUFS, (x + 2) % XBUFS, x % 2)
                spread(g, i, x, x % 2)

            reduce(0, 0, 0, 0)
            reduce(1, 0, 1, 1)
            with dve.Fori(0, NG // XBUFS - 1) as i:
                for x in range(XBUFS):
                    step(i, x)
            for x in range(XBUFS):
                step(NG // XBUFS - 1, x)

        @block.tensor
        def _(pe):
            pe.sem_inc(turned, CREDIT)
            pe.wait_ge(loaded, 80)
            pe.wait_ge(split, 4)

            def hidden(i, u):
                g = i * 2 + u
                pe.wait_ge(reduced, g + 1)
                for t in range(GT):
                    ins = nc.tensor.transpose(pt[:, t * P:(t + 1) * P], xp[u][:, t, :, :].rearrange("p a i -> p (a i)"), ident16[:, :])
                ins.then_inc(turned, 1)
                pe.wait_ge(copied, g + 1)
                for jj in range(HPAIRS):
                    pe.wait_ge(gelu, g * HPAIRS + jj + 1)
                    for j in range(2):
                        at = (2 * jj + j) * P
                        ins = nc.tensor.matmul(ph[jj % 2][:, j, 0:G], fc1p[:, at:at + P], xpt[u][:, :], start=True, stop=True)
                    ins.then_inc(h_ready, 1)

            def outputs(i, u):
                g = i * 2 + u
                pe.wait_ge(gelu, g * HPAIRS + HPAIRS + CREDIT)
                pe.wait_ge(o_taken, g + 1)
                for j in range(FT):
                    ins = nc.tensor.matmul(pot[:, 0:G], pj1[:, j, :], h[u][:, j, :], start=j == 0, stop=j == FT - 1)
                ins.then_inc(ot_ready, 1)
                pe.wait_ge(ot_copied, g + 1)
                settle(pe, pe_held)
                for t in range(GT):
                    ins = nc.tensor.transpose(po[:, t * KR:(t + 1) * KR], ot[:, t * P:(t + 1) * P], ident[0:KR, 0:KR])
                ins.then_inc(o_ready, 1)

            hidden(0, 0)
            with pe.Fori(0, NG // 2 - 1) as i:
                for u in range(2):
                    hidden(i + u, 1 - u)
                    outputs(i, u)
            hidden(NG // 2 - 1, 1)
            outputs(NG // 2 - 1, 0)
            outputs(NG // 2 - 1, 1)

        @block.scalar
        def _(act):
            act.sem_inc(gelu, CREDIT)
            act.wait_ge(eps_set, 1)

            def root(g):
                act.wait_ge(var_ready, g + 1)
                nc.scalar.activation(std[:, 1, :], std[:, 0, :], ACT.Sqrt, bias=epst[:, :]).then_inc(std_ready, 1)

            def gelus(g, u):
                for jj in range(HPAIRS):
                    act.wait_ge(h_ready, g * HPAIRS + jj + 1)
                    nc.scalar.activation(h[u][:, 2 * jj:2 * jj + 2, :], ph[jj % 2][:, :, 0:G], ACT.Gelu, scale=1.0 / (W_SCALE * X_SCALE)).then_inc(gelu, 1)

            def turn(g, u):
                act.wait_ge(turned, g + 1 + CREDIT)
                nc.scalar.copy(xpt[u][:, :], pt[:, 0:G]).then_inc(copied, 1)

            def turn_o(g):
                act.wait_ge(ot_ready, g + 1)
                nc.scalar.copy(ot[:, :], pot[:, 0:G]).then_inc(ot_copied, 1)

            root(0)
            root(1)
            turn(0, 0)
            gelus(0, 0)
            turn(1, 1)
            root(2)
            with act.Fori(0, NG // 2 - 2) as i:
                for u in range(2):
                    g = i * 2 + u
                    gelus(g + 1, 1 - u)
                    turn_o(g)
                    turn(g + 2, u)
                    root(g + 3)
            gelus(NG - 3, 1)
            turn_o(NG - 4)
            turn(NG - 2, 0)
            root(NG - 1)
            gelus(NG - 2, 0)
            turn_o(NG - 3)
            turn(NG - 1, 1)
            gelus(NG - 1, 1)
            turn_o(NG - 2)
            turn_o(NG - 1)


def program(nc, c, w, out):
    def dram(name, *shape, dt=F32):
        return nc.dram_tensor(name, list(shape), dt).ap()

    x = w["x"].rearrange("b h w d -> (b h w) d")
    xn, y = dram("xn", P, DC, T), dram("y", SLOTS, P, T)
    norm_transpose(nc, "n", c, x, xn, 1e-6)
    ss2d(nc, c, dict(w, xn=xn), y)
    x1, th, tl, scores = dram("x1", T, D), dram("th", P, DC, T, dt=F16), dram("tl", P, DC, T, dt=F16), dram("scores", P, NT, EX)
    ss2d_out(nc, c, w, y, x, x1, th, tl, scores)
    x2 = dram("x2", T, D)
    moe(nc, c, w, x1, th, tl, scores, x2)
    xn1, sz, dt_raw = dram("xn1", P, DC, T), dram("sz", T, DIN), dram("dt_raw", P, NT, HEADS)
    mamba_gate(nc, c, w, x2, xn1, sz, dt_raw)
    xbc, x3 = dram("xbc", CT, P, T), dram("x3", T, D)
    mamba_conv(nc, w, xn1, xbc)
    mamba_scan(nc, c, w, x2, sz, dt_raw, xbc, x3)
    kron_ffn(nc, c, w, x3, out.rearrange("b h w d -> (b h w) d"))


def constants(np, bf16):
    i = np.arange(P)
    sel = np.zeros((BROWS, 3, BC, P), bf16)
    for p in range(BROWS):
        sel[p, 0, p % BC] = 1
        sel[p, 1, p % BC, :REST] = 1
        sel[p, 2, p % BC, REST:] = 1
    return dict(ident=np.eye(P, dtype=np.float32), mean768=np.full((P, P), 1.0 / CI, np.float32),
                upto=(i[:, None] <= i[None]).astype(np.float32), beyond=(i[:, None] > i[None]).astype(np.float32), sel=sel)


def layouts(np, I):
    def zeros(*shape):
        return np.zeros(shape, np.float32)

    def rows(a):
        return a.reshape((-1, P) + a.shape[1:]).swapaxes(0, 1)

    def spread(a):
        return np.broadcast_to(a.reshape(1, -1), (P, a.size))

    w = dict(x=I["x"])
    proj = I["L0_conv_in_proj_w"].reshape(KD, DI, DC, P).transpose(0, 3, 2, 1)
    w["in_proj"] = zeros(KD, P, 3, DC, P)
    w["in_proj"][:, :, 0] = proj[..., :P]
    w["in_proj"][:, :, 1, :, :REST] = proj[..., P:]
    w["in_proj"][:, :, 2, :, REST:] = proj[..., P:]

    def tiles(a):
        a = a.reshape((KD, DI) + a.shape[1:] if a.shape[0] == CI else a.shape)
        r = zeros(KD, P, 3, *a.shape[2:])
        r[:, :, 0], r[:, :, 1] = a[:, :P], a[:, :P]
        r[:, :REST, 2], r[:, REST:, 2] = a[:, P:], a[:, P:]
        return r

    w["conv"] = tiles(I["L0_conv_conv_w"].reshape(KD, DI, 9))
    w["conv_b"], w["ds"] = tiles(I["L0_conv_conv_b"]), tiles(I["L0_conv_Ds"])
    w["a_logs"], w["dt_b"] = tiles(I["L0_conv_A_logs"]), tiles(I["L0_conv_dt_projs_bias"])
    xp = I["L0_conv_x_proj_weight"]
    xp = np.concatenate([xp[:, RANK:]] * PARTS + [xp[:, :RANK]], 1).transpose(0, 2, 1)
    w["x_proj"] = zeros(KD, P, 3, XROWS)
    w["x_proj"][:, :, 0], w["x_proj"][:, :REST, 1], w["x_proj"][:, REST:, 2] = xp[:, :P], xp[:, P:], xp[:, P:]
    dp = I["L0_conv_dt_projs_weight"].transpose(0, 2, 1)
    w["dt_proj"] = zeros(KD, XROWS, 3, P)
    w["dt_proj"][:, BROWS:, 0] = dp[:, :, :P]
    w["dt_proj"][:, BROWS:, 1, :REST], w["dt_proj"][:, BROWS:, 2, REST:] = dp[:, :, P:], dp[:, :, P:]

    def slots(a):
        a = a.reshape((KD, DI) + a.shape[1:])
        r = zeros(P, SLOTS, *a.shape[2:])
        for k in range(KD):
            r[:, k] = a[k, :P]
            r[k % 2 * REST:k % 2 * REST + REST, KD + k // 2] = a[k, P:]
        return r

    w["out_proj"] = slots(I["L0_conv_out_proj_w"].T)
    w["out_nw"], w["out_nb"] = slots(I["L0_conv_out_norm_w"]), slots(I["L0_conv_out_norm_b"])
    w["gate_w"], w["gate_b"] = rows(I["L0_ffn_gate_w"]), I["L0_ffn_gate_b"].reshape(1, EX)
    w["w1"] = I["L0_ffn_w1"].reshape(EX, DC, P, 2, HALF).transpose(0, 3, 2, 1, 4)
    w["w2"] = I["L0_ffn_w2"].reshape(EX, 2, HT, P, D).transpose(0, 1, 3, 2, 4)
    w["b1"] = I["L0_ffn_b1"].reshape(EX, HID // P, P).transpose(2, 0, 1).reshape(P, -1)
    w["b2"] = I["L0_ffn_b2"].reshape(1, -1)
    win = I["L1_conv_W_in"]
    w["w_z"], w["w_dt"] = rows(win[:, :DIN]), rows(win[:, DIN + CONV:])
    xbc, conv = zeros(D, CT * P), zeros(CT * P, 10)
    xbc[:, :CONV] = win[:, DIN:DIN + CONV]
    w["w_x"] = xbc.reshape(DC, P, CT, P).transpose(2, 1, 0, 3)
    conv[:CONV, :9], conv[:CONV, 9] = I["L1_conv_W_conv"].reshape(9, CONV).T, I["L1_conv_b_conv"]
    conv = rows(conv)
    w["conv1"], w["conv1_b"] = conv[:, :, :9], conv[:, :, 9]
    w["dt1_b"], w["a1_log"] = spread(I["L1_conv_dt_bias"]), spread(I["L1_conv_A_log"])
    w["d1"] = spread(np.repeat(I["L1_conv_D_param"], HP))
    w["gamma"], w["beta"], w["w_out1"] = spread(I["L1_conv_gamma"]), spread(I["L1_conv_beta"]), rows(I["L1_conv_W_out"])
    w["fc1"], w["fc2"] = np.tile(I["L1_ffn_c_fc_1"].T, (3, 1)), spread(I["L1_ffn_c_fc_2"])
    w["pj1"], w["pj2"] = rows(I["L1_ffn_c_proj_1"].T), spread(I["L1_ffn_c_proj_2"])
    return w


def kernel(**inputs):
    import numpy as np
    import concourse.bacc as bacc
    from concourse.bass_utils import run_bass_kernel_spmd

    nc = bacc.Bacc("TRN2", target_bir_lowering=False, num_devices=1)
    arrays, c, w = {}, {}, {}
    for into, source in ((c, constants(np, mybir.dt.np(BF16))), (w, layouts(np, {k: np.asarray(v) for k, v in inputs.items()}))):
        for name, a in source.items():
            a = np.ascontiguousarray(a)
            arrays[f"in_{name}"] = a
            into[name] = nc.dram_tensor(f"in_{name}", a.shape, mybir.dt.from_np(a.dtype), kind="ExternalInput").ap()
    out = nc.dram_tensor("out", [IMAGES, SIDE, SIDE, D], F32, kind="ExternalOutput").ap()
    program(nc, c, w, out)
    return run_bass_kernel_spmd(nc, [arrays], core_ids=[0]).results[0]["out"]
```

```python
from contextlib import ExitStack

import concourse.bass as bass
from concourse import mybir

F32 = mybir.dt.float32
F16 = mybir.dt.float16
BF16 = mybir.dt.bfloat16
ACT = mybir.ActivationFunctionType
ALU = mybir.AluOpType
AX = mybir.AxisListType

P = 128
IMAGES, SIDE, D = 2, 48, 384
L = SIDE * SIDE
T = IMAGES * L
DC = D // P
G = 384
GT = G // P
NG = T // G
GI = L // G
ROWS = G // SIDE
BANK = 512

W_SCALE = 64.0

KD, DI, NS, RANK = 4, 192, 16, 12
CI = KD * DI
AT, AT1 = 3, 4
REST = DI - P
BC = 2 * NS
EX, HID = 4, 1536
HEADS, HP = 12, 64
DIN = HEADS * HP
CONV = DIN + 2 * NS
KR, KJ, FF = 32, 12, 1536


class Chain:

    def __init__(self, eng, sem, per):
        self.eng, self.sem, self.per = eng, sem, per
        self.base, self.n = 0, 0

    def start(self, turn):
        assert self.n in (0, self.per), (self.n, self.per)
        self.base, self.n = turn * self.per, 0

    def mark(self, ins):
        ins.then_inc(self.sem, 1)
        self.n += 1

    def wait(self):
        self.eng.wait_ge(self.sem, self.base + self.n)

    def __call__(self, ins):
        self.mark(ins)
        self.wait()


def settle(eng, held):
    eng.sem_inc(held, 1)


class Stage:

    def __init__(self, nc, name):
        self.nc, self.name = nc, name

    def __enter__(self):
        self.ctx, self.sems = ExitStack(), []
        return self

    def sb(self, name, shape, dt=F32):
        return self.ctx.enter_context(self.nc.sbuf_tensor(f"{self.name}_{name}", shape, dt))

    def ps(self, name, shape, dt=F32):
        return self.ctx.enter_context(self.nc.psum_tensor(f"{self.name}_{name}", shape, dt))

    def sem(self, name):
        self.sems.append(self.nc.alloc_semaphore(f"{self.name}_{name}"))
        return self.sems[-1]

    def block(self):
        return self.ctx.enter_context(self.nc.Block())

    def __exit__(self, *a):
        self.ctx.__exit__(*a)
        if self.sems:
            self.nc.clear_and_free_semaphores(self.sems)
            self.nc.all_engine_barrier()


def tok_groups(dram):
    return dram.rearrange("(g t p) d -> g p t d", t=GT, p=P)


def norm_steps(dve, chain, x, stats, mv, std, rstd, out, var_ready, std_ready, turn, held):
    nc = dve.bass
    for t in range(GT):
        chain.mark(nc.vector.bn_stats(stats[:, t, :], x[:, t, :]))
    chain.wait()
    settle(dve, held)
    for t in range(GT):
        chain.mark(nc.vector.bn_aggr(mv[:, t, :], stats[:, t, :]))
    chain.wait()
    nc.vector.tensor_copy(std[:, 0, :], mv[:, :, 1]).then_inc(var_ready, 1)
    dve.wait_ge(std_ready, turn + 1)
    chain(nc.vector.reciprocal(rstd[:, :], std[:, 1, :]))
    for t in range(GT):
        last = nc.vector.tensor_scalar(out[:, t, :], x[:, t, :], mv[:, t, 0:1], rstd[:, t:t + 1],
                                       ALU.subtract, ALU.mult)
    return last


NORM_STEPS = 2 * GT + 1


CREDIT = 2


def free(turn):
    return turn + 1


def ready(turn):
    return turn + CREDIT + 1


def norm_transpose(nc, c, src, xh, xl, eps):
    src_g = tok_groups(src)
    with Stage(nc, "n") as s:
        ident, epst = s.sb("ident", [P, P]), s.sb("eps", [P, 1])
        x = [s.sb(f"x{u}", [P, GT, D]) for u in range(2)]
        xn = [s.sb(f"xn{u}", [P, GT, D]) for u in range(2)]
        stats, mv = s.sb("stats", [P, GT, 6]), s.sb("mv", [P, GT, 2])
        std, rstd = s.sb("std", [P, 2, GT]), s.sb("rstd", [P, GT])
        xt = [s.sb(f"xt{u}", [P, DC, G]) for u in range(2)]
        pt = [s.ps(f"pt{u}", [P, DC, BANK]) for u in range(2)]
        x_in = [s.sem("x_in0"), s.sem("x_in1")]
        consts, eps_set, var_ready, std_ready, normed, steps, turned, copied, held, act_held, high_ready, low_ready, pool_held = (s.sem(x) for x in (
            "consts eps_set var_ready std_ready normed steps turned copied held act_held high_ready low_ready pool_held".split()))
        block = s.block()

        @block.sync
        def _(sp):
            with sp.Fori(0, NG // 2) as i:
                for u in range(2):
                    g = i * 2 + u
                    sp.wait_ge(normed, free(g))
                    sp.dma_start(x[u][:, :, :], src_g[g]).then_inc(x_in[u], 16)

        @block.vector
        def _(dve):
            nc.vector.memset(epst[:, :], eps).then_inc(eps_set, 1)
            dve.sem_inc(normed, CREDIT)
            chain = Chain(dve, steps, NORM_STEPS)
            with dve.Fori(0, NG // 2) as i:
                for u in range(2):
                    g = i * 2 + u
                    chain.start(g)
                    dve.wait_ge(x_in[u], i * 16 + 16)
                    dve.wait_ge(turned, free(g))
                    norm_steps(dve, chain, x[u], stats, mv, std, rstd, xn[u], var_ready, std_ready, g,
                               held).then_inc(normed, 1)

        @block.tensor
        def _(pe):
            pe.sem_inc(turned, CREDIT)
            pe.wait_ge(consts, 16)
            with pe.Fori(0, NG // 2) as i:
                for u in range(2):
                    g = i * 2 + u
                    pe.wait_ge(normed, ready(g))
                    pe.wait_ge(copied, free(g))
                    for t in range(GT):
                        for d in range(DC):
                            ins = nc.tensor.transpose(pt[u][:, d, t * P:(t + 1) * P],
                                                      xn[u][:, t, d * P:(d + 1) * P], ident[:, :])
                    ins.then_inc(turned, 1)

        @block.gpsimd
        def _(pool):
            pool.sem_inc(low_ready, CREDIT)
            for b in range(IMAGES):
                with pool.Fori(0, GI // 2) as i:
                    for u in range(2):
                        q = i * 2 + u
                        pool.wait_ge(high_ready, q + (b * GI + 1))
                        settle(pool, pool_held)
                        part = bass.ds(q * G, G)
                        nc.gpsimd.tensor_tensor(xl[:, b, :, part], xt[u][:, :, :], xh[:, b, :, part], ALU.subtract).then_inc(low_ready, 1)

        @block.scalar
        def _(act):
            act.dma_start(ident[:, :], c["ident"]).then_inc(consts, 16)
            act.sem_inc(copied, CREDIT)
            act.wait_ge(eps_set, 1)

            def root(g):
                act.wait_ge(var_ready, g + 1)
                nc.scalar.activation(std[:, 1, :], std[:, 0, :], ACT.Sqrt, bias=epst[:, :]).then_inc(std_ready, 1)

            def copy(g, b, q, u):
                act.wait_ge(turned, ready(g))
                act.wait_ge(low_ready, free(g))
                nc.scalar.copy(xt[u][:, :, :], pt[u][:, :, 0:G]).then_inc(copied, 1)
                act.wait_ge(copied, ready(g))
                settle(act, act_held)
                nc.scalar.copy(xh[:, b, :, bass.ds(q * G, G)], xt[u][:, :, :]).then_inc(high_ready, 1)

            root(0)
            root(1)
            for b in range(IMAGES):
                last = b == IMAGES - 1
                with act.Fori(0, GI // 2 - (1 if last else 0)) as i:
                    for u in range(2):
                        q = i * 2 + u
                        root(q + (b * GI + 2))
                        copy(q + b * GI, b, q, u)
                if last:
                    for u in range(2):
                        copy(NG - 2 + u, b, GI - 2 + u, u)


SEG = 2 * G
SEGS = L // SEG
STEPS_N = 3 * SEGS
PARTS = 3
BROWS = PARTS * BC
XROWS = BROWS + RANK


def in_order(image, k):
    if k >= 2:
        image = image[:, ::-1]
    return image.rearrange("p (h w) -> p h w" if k % 2 == 0 else "p (h w) -> p w h", h=SIDE)


def ss2d_conv(nc, c, w, k, xh, xl, u, dt, y, aneg, sel, y_stored, before):
    with Stage(nc, f"a{k}") as s:
        win = s.sb("win", [P, 3, DC, P])
        wh, wl = s.sb("wh", [P, 3, DC, P], F16), s.sb("wl", [P, 3, DC, P], F16)
        taps, bias = s.sb("taps", [P, 3, 9]), s.sb("bias", [P, 3])
        alog = s.sb("alog", [P, 3, NS])
        pad = [s.sb(f"pad{v}", [P, SIDE + 2, SIDE + 2]) for v in range(2)]
        acc = [y[:, v, :].rearrange("p (h w) -> p h w", w=SIDE) for v in range(2)]
        tmp, tap_sum = dt, y[:, 2, :]
        pi = s.ps("pi", [P, GI, BANK])
        w_split = s.sem("w_split")
        multiplied, act_tapped, pool_steps = s.sem("multiplied"), s.sem("act_tapped"), s.sem("pool_steps")
        loaded, win_in, zeroed, projected, padded, tapped, convolved, active, a_ready, a_exp = (s.sem(x) for x in (
            "loaded win_in zeroed projected padded tapped convolved active a_ready a_exp".split()))
        block = s.block()

        @block.sync
        def _(sp):
            sp.dma_start(win[:, :, :, :], w["in_proj"][k]).then_inc(win_in, 16)
            sp.dma_start(taps[:, :, :], w["conv"][k]).then_inc(loaded, 16)
            sp.dma_start(bias[:, :], w["conv_b"][k]).then_inc(loaded, 16)
            sp.dma_start(alog[:, :, :], w["a_logs"][k]).then_inc(loaded, 16)
            if sel:
                sp.dma_start(sel[0][:, :, :, :], c["sel"]).then_inc(sel[1], 16)
                sp.wait_ge(sel[1], 16)

        @block.gpsimd
        def _(pool):
            for v in range(2):
                nc.gpsimd.memset(pad[v][:, :, :], 0.0).then_inc(zeroed, 1)
            chain = Chain(pool, pool_steps, None)
            for ct in range(3):
                for t in range(1, AT):
                    pool.wait_ge(multiplied, ct * AT + t + 1)
                    if t == AT - 1 and ct:
                        pool.wait_ge(convolved, ct)
                    ins = nc.gpsimd.tensor_tensor(tmp[:, 0, :] if t < AT - 1 else tap_sum, tmp[:, 0, :], tmp[:, t, :], ALU.add)
                    if t < AT - 1:
                        chain(ins)
                ins.then_inc(act_tapped, 1)

        @block.tensor
        def _(pe):
            pe.wait_ge(w_split, 3)
            for ct in range(3):
                images = ((0,), (1,), (0, 1))[ct]
                terms = [(j, b, d, wp, xp) for j, b in enumerate(images) for d in range(DC) for wp, xp in ((wh, xh), (wh, xl), (wl, xh))]
                for q in range(GI):
                    pe.wait_ge(padded, ct * GI + q + 1)
                    for n, (j, b, d, wp, xp) in enumerate(terms):
                        ins = nc.tensor.matmul(pi[:, q, 0:G], wp[:, 1 + j if ct == 2 else 0, d, :],
                                               xp[:, b, d, q * G:(q + 1) * G], start=n == 0, stop=n == len(terms) - 1)
                    ins.then_inc(projected, 1)

        @block.vector
        def _(dve):
            dve.wait_ge(win_in, 16)
            nc.vector.tensor_scalar(wh[:, :, :, :], win[:, :, :, :], W_SCALE, None, ALU.mult).then_inc(w_split, 1)
            nc.vector.tensor_scalar(win[:, :, :, :], win[:, :, :, :], W_SCALE, None, ALU.mult).then_inc(w_split, 1)
            dve.wait_ge(w_split, 2)
            nc.vector.tensor_tensor(wl[:, :, :, :], win[:, :, :, :], wh[:, :, :, :], ALU.subtract).then_inc(w_split, 1)
            dve.wait_ge(loaded, 48)
            dve.wait_ge(a_exp, 1)
            nc.vector.tensor_scalar(aneg[:, :, :], alog[:, :, :], -1.0, None, ALU.mult).then_inc(a_ready, 1)
            chain = Chain(dve, tapped, None)
            if before:
                dve.wait_ge(y_stored, 64 * before)
            for ct in range(3):
                dve.wait_ge(padded, GI * (ct + 2))
                if ct == 2:
                    dve.wait_ge(active, 1)
                image = acc[ct % 2]
                for t in range(9 - AT):
                    rows = pad[ct % 2][:, t // 3:t // 3 + SIDE, t % 3:t % 3 + SIDE]
                    tap = taps[:, ct, t:t + 1]
                    if t == 0:
                        ins = nc.vector.tensor_scalar(image, rows, tap, None, ALU.mult)
                    else:
                        ins = nc.vector.scalar_tensor_tensor(out=image, in0=rows, scalar=tap, in1=image,
                                                             op0=ALU.mult, op1=ALU.add)
                    chain(ins)
                dve.wait_ge(act_tapped, ct + 1)
                nc.vector.tensor_tensor(image, image, tap_sum.rearrange("p (h w) -> p h w", w=SIDE), ALU.add).then_inc(convolved, 1)

        @block.scalar
        def _(act):
            act.sem_inc(padded, GI)
            act.wait_ge(loaded, 48)
            nc.scalar.activation(alog[:, :, :], alog[:, :, :], ACT.Exp).then_inc(a_exp, 1)
            act.wait_ge(zeroed, 2)

            def silu(ct):
                act.wait_ge(convolved, ct + 1)
                nc.scalar.activation(in_order(u[:, ct, :], k), acc[ct % 2], ACT.Silu,
                                     bias=bias[:, ct:ct + 1]).then_inc(active, 1)

            for ct in range(3):
                if ct == 2:
                    act.wait_ge(convolved, 1)
                for q in range(GI):
                    act.wait_ge(projected, ct * GI + q + 1)
                    nc.scalar.activation(pad[ct % 2][:, q * ROWS + 1:(q + 1) * ROWS + 1, 1:SIDE + 1],
                                         pi[:, q, 0:G].rearrange("p (h w) -> p h w", w=SIDE), ACT.Copy,
                                         scale=1.0 / W_SCALE).then_inc(padded, 1)
                if ct:
                    act.wait_ge(act_tapped, ct)
                elif before:
                    act.wait_ge(y_stored, 64 * before)
                act.wait_ge(padded, GI * (ct + 2))
                for t in range(AT):
                    tap = 9 - AT + t
                    nc.scalar.activation(tmp[:, t, :].rearrange("p (h w) -> p h w", w=SIDE),
                                               pad[ct % 2][:, tap // 3:tap // 3 + SIDE, tap % 3:tap % 3 + SIDE], ACT.Copy,
                                               scale=taps[:, ct, tap:tap + 1]).then_inc(multiplied, 1)
                if ct:
                    silu(ct - 1)
            silu(2)


def ss2d_project(nc, c, w, k, u, dt, y, bc):
    with Stage(nc, f"b{k}") as s:
        wx = s.sb("wx", [P, 3, XROWS])
        wd = s.sb("wd", [XROWS, 3, P])
        dtb, ds = s.sb("dtb", [P, 3]), s.sb("ds", [P, 3])
        xd = [[s.sb(f"xd{v}{b}", [XROWS, G]) for b in range(IMAGES)] for v in range(2)]
        rest = s.sb("rest", [64, G])
        e, one_e, ln = (s.sb(x, [P, 3, G]) for x in ("e", "one_e", "ln"))
        corr = [s.sb(f"corr{v}", [P, 3, G]) for v in range(2)]
        px = [s.ps(f"px{b}", [P, BANK]) for b in range(IMAGES)]
        pd = s.ps("pd", [P, 3, BANK])
        (loaded, projected, xd_ready, split, dt_done, e_ready, one_ready, ln_ready, steps, summed, positive, dt_added, y_ready,
         act_steps, one_set, held, pool_held, done) = (s.sem(x) for x in "loaded projected xd_ready split dt_done e_ready one_ready "
                                            "ln_ready steps summed positive dt_added y_ready act_steps one_set held pool_held done".split())
        ln_one = s.sb("ln_one", [P, 2])
        block = s.block()

        def ahead(eng, first, second):
            first(0, 0)
            with eng.Fori(0, GI // 2 - 1) as i:
                for v in range(2):
                    first(i * 2 + v + 1, 1 - v)
                    second(i * 2 + v, v)
            first(GI - 1, 1)
            second(GI - 2, 0)
            second(GI - 1, 1)

        def cols(q):
            return bass.ds(q * G, G)

        @block.sync
        def _(sp):
            sp.dma_start(wx[:, :, :], w["x_proj"][k]).then_inc(loaded, 16)
            sp.dma_start(wd[:, :, :], w["dt_proj"][k]).then_inc(loaded, 16)
            sp.dma_start(dtb[:, :], w["dt_b"][k]).then_inc(loaded, 16)
            sp.dma_start(ds[:, :], w["ds"][k]).then_inc(loaded, 16)

        @block.tensor
        def _(pe):
            pe.wait_ge(loaded, 64)

            def x_proj(q, v):
                for b in range(IMAGES):
                    pe.wait_ge(xd_ready, q * 2 + b + 1)
                    nc.tensor.matmul(px[b][0:XROWS, 0:G], wx[:, 0, :], u[:, b, cols(q)], start=True, stop=False)
                    nc.tensor.matmul(px[b][0:XROWS, 0:G], wx[:, 1 + b, :], u[:, 2, cols(q)],
                                     start=False, stop=True).then_inc(projected, 1)

            def dt_proj(q, v):
                pe.wait_ge(xd_ready, q * 2 + 4)
                pe.wait_ge(positive, q + 1)
                for b in range(IMAGES):
                    nc.tensor.matmul(pd[:, b, 0:G], wd[:, 0, :], xd[v][b][:, :], start=True, stop=True)
                nc.tensor.matmul(pd[:, 2, 0:G], wd[:, 1, :], xd[v][0][:, :], start=True, stop=False)
                nc.tensor.matmul(pd[:, 2, 0:G], wd[:, 2, :], xd[v][1][:, :], start=False, stop=True).then_inc(dt_done, 1)

            ahead(pe, x_proj, dt_proj)

        @block.scalar
        def _(act):
            nc.scalar.preload_act_table_set("natural_log_exp_and_others")
            act.sem_inc(xd_ready, 2)
            act.sem_inc(positive, 1)
            act.wait_ge(one_set, 1)
            nc.scalar.activation(ln_one[:, 1:2], ln_one[:, 0:1], ACT.Ln).then_inc(one_set, 1)
            chain = Chain(act, act_steps, 1)
            act.wait_ge(loaded, 64)

            def copy(q, v):
                act.wait_ge(split, free(q))
                for b in range(IMAGES):
                    act.wait_ge(projected, q * 2 + b + 1)
                    nc.scalar.copy(xd[v][b][:, :], px[b][0:XROWS, 0:G]).then_inc(xd_ready, 1)

            def softplus(q, v):
                act.wait_ge(dt_done, q + 1)
                act.wait_ge(summed, q + 1)
                chain.start(q)
                for ct in range(3):
                    ins = nc.scalar.activation(e[:, ct, :], pd[:, ct, 0:G], ACT.Abs, bias=dtb[:, ct:ct + 1])
                chain(ins)
                nc.scalar.activation(e[:, :, :], e[:, :, :], ACT.Exp, scale=-1.0).then_inc(e_ready, 1)
                for ct in range(3):
                    ins = nc.scalar.activation(dt[:, ct, cols(q)], pd[:, ct, 0:G], ACT.Relu, bias=dtb[:, ct:ct + 1])
                ins.then_inc(positive, 1)
                for ct in range(3):
                    ins = nc.scalar.activation(y[:, ct, cols(q)], u[:, ct, cols(q)], ACT.Copy, scale=ds[:, ct:ct + 1])
                ins.then_inc(y_ready, 1)
                act.wait_ge(one_ready, q + 1)
                nc.scalar.activation(ln[:, :, :], one_e[:, :, :], ACT.Ln).then_inc(ln_ready, 1)

            ahead(act, copy, softplus)

        @block.vector
        def _(dve):
            dve.sem_inc(split, CREDIT)
            dve.sem_inc(summed, 1)
            nc.vector.memset(ln_one[:, 0:1], 1.0).then_inc(one_set, 1)
            chain = Chain(dve, steps, 6)
            corr_chain = Chain(dve, done, 1)
            dve.wait_ge(one_set, 2)

            def parts(q, v):
                chain.start(q)
                for b in range(IMAGES):
                    dve.wait_ge(xd_ready, q * 2 + 3 + b)
                    settle(dve, held)
                    chain(nc.vector.tensor_copy(bc[:, b, cols(q)], xd[v][b][0:BROWS, :]))
                    chain(nc.vector.tensor_tensor(rest[:, :], xd[v][b][0:64, :], bc[0:64, b, cols(q)], ALU.subtract))
                    settle(dve, held)
                    chain(nc.vector.tensor_copy(bc[0:64, b, cols(q)], rest[:, :]))
                    last = nc.vector.tensor_tensor(bc[0:32, b, cols(q)], rest[0:32, :], bc[0:32, b, cols(q)], ALU.subtract)
                last.then_inc(split, 1)

            def log1p(q, v):
                corr_chain.start(q)
                dve.wait_ge(e_ready, q + 1)
                nc.vector.tensor_scalar(one_e[:, :, :], e[:, :, :], 1.0, None, ALU.add).then_inc(one_ready, 1)
                dve.wait_ge(one_ready, q + 1)
                dve.wait_ge(dt_added, free(q))
                corr_chain(nc.vector.scalar_tensor_tensor(out=corr[v][:, :, :], in0=one_e[:, :, :], scalar=1.0, in1=e[:, :, :],
                                                          op0=ALU.subtract, op1=ALU.subtract))
                dve.wait_ge(ln_ready, q + 1)
                nc.vector.scalar_tensor_tensor(out=corr[v][:, :, :], in0=ln[:, :, :], scalar=ln_one[:, 1:2], in1=corr[v][:, :, :],
                                               op0=ALU.subtract, op1=ALU.subtract).then_inc(summed, 1)

            ahead(dve, parts, log1p)

        @block.gpsimd
        def _(pool):
            pool.sem_inc(dt_added, CREDIT)
            with pool.Fori(0, GI // 2) as i:
                for v in range(2):
                    q = i * 2 + v
                    pool.wait_ge(positive, q + 2)
                    pool.wait_ge(summed, q + 2)
                    settle(pool, pool_held)
                    nc.gpsimd.tensor_tensor(dt[:, :, cols(q)], corr[v][:, :, :], dt[:, :, cols(q)], ALU.add).then_inc(dt_added, 1)
                    pool.wait_ge(dt_added, ready(q))
                    pool.wait_ge(y_ready, q + 1)
                    settle(pool, pool_held)
                    nc.gpsimd.tensor_tensor(u[:, :, cols(q)], dt[:, :, cols(q)], u[:, :, cols(q)], ALU.mult)


def ss2d_scan(nc, c, w, k, du, dt, y, bc, aneg, sel, out, stored, last):
    with Stage(nc, f"c{k}") as s:
        a, h, hc = ([s.sb(f"{x}{v}", [P, SEG]) for v in range(2)] for x in ("a", "h", "hc"))
        b_copy, fed_pool = s.sb("b_copy", [P, SEG]), [s.sb(f"fed_pool{v}", [P, SEG]) for v in range(2)]
        pb, pcc = ([s.ps(f"{x}{v}", [P, 2 * BANK]) for v in range(2)] for x in ("pb", "pc"))
        b_ready, c_ready, a_ready = s.sem("b_ready"), s.sem("c_ready"), s.sem("a_ready")
        fed, scanned, weighed, added = s.sem("fed"), s.sem("scanned"), s.sem("weighed"), s.sem("added")
        ordered, ordered_act, held = s.sem("ordered"), s.sem("ordered_act"), s.sem("held")
        b_copied, pool_fed = s.sem("b_copied"), s.sem("pool_fed")
        block = s.block()
        ITER = 2 * STEPS_N

        by_pool = list(range(1, ITER - 1, 2))
        by_dve = [m for m in range(ITER) if m not in by_pool]
        PF, DF = len(by_pool), len(by_dve)

        def place(m):
            return (m % STEPS_N) // SEGS, m % SEGS, m % 2, m // STEPS_N

        def cols(t, ct, seg):
            return t[:, ct, seg * SEG:(seg + 1) * SEG]

        @block.tensor
        def _(pe):
            with pe.Fori(0, NS // 2) as i:
                def spread(m, first, tiles, gone, signal):
                    ct, seg, v, half = place(m)
                    if tiles is pb and m - 2 in by_pool:
                        pe.wait_ge(b_copied, i * PF + by_pool.index(m - 2) + 1)
                    else:
                        pe.wait_ge(gone, free(i * ITER + m))
                    terms = (((0, 0),), ((1, 0),), ((0, 1), (1, 2)))[ct]
                    for j, width in ((0, BANK), (BANK, SEG - BANK)):
                        at = seg * SEG + j
                        for b, kind in terms:
                            ins = nc.tensor.matmul(tiles[v][:, j:j + width], sel[:, kind, i * 2 + (half + first), :],
                                                   bc[:, b, at:at + width], start=(b, kind) == terms[0],
                                                   stop=(b, kind) == terms[-1])
                    ins.then_inc(signal, 1)

                spread(0, 0, pb, scanned, b_ready)
                for m in range(ITER):
                    if m + 1 < ITER:
                        spread(m + 1, 0, pb, scanned, b_ready)
                    spread(m, NS, pcc, weighed, c_ready)

        @block.scalar
        def _(act):
            with act.Fori(0, NS // 2) as i:
                for m in range(ITER):
                    ct, seg, v, half = place(m)
                    act.wait_ge(scanned, free(i * ITER + m))
                    settle(act, held)
                    nc.scalar.activation(a[v][:, :], dt[:, ct, seg * SEG:(seg + 1) * SEG], ACT.Exp,
                                         scale=aneg[:, ct, bass.ds(i * 2 + half, 1)]).then_inc(a_ready, 1)
                    if m + 1 in by_pool:
                        act.wait_ge(b_ready, i * ITER + m + 2)
                        act.wait_ge(pool_fed, i * PF + by_pool.index(m + 1) + 1)
                        nc.scalar.copy(b_copy[:, :], pb[(m + 1) % 2][:, 0:SEG]).then_inc(b_copied, 1)
            if k:
                act.wait_ge(added, NS * STEPS_N + STEPS_N)
                nc.scalar.copy(in_order(dt[:, 1, :], k), y[:, 1, :].rearrange("p (h w) -> p h w", w=SIDE)).then_inc(ordered_act, 1)

        @block.vector
        def _(dve):
            dve.sem_inc(scanned, CREDIT)
            dve.sem_inc(weighed, CREDIT)
            with dve.Fori(0, NS // 2) as i:
                def feed(m):
                    ct, seg, v, _ = place(m)
                    dve.wait_ge(b_ready, i * ITER + m + 1)
                    nc.vector.tensor_tensor(pb[v][:, 0:SEG], pb[v][:, 0:SEG], cols(du, ct, seg), ALU.mult).then_inc(fed, 1)

                def scan(m):
                    ct, seg, v, _ = place(m)
                    if m in by_pool:
                        source = fed_pool[by_pool.index(m) % 2][:, :]
                        dve.wait_ge(pool_fed, i * PF + by_pool.index(m) + 2)
                    else:
                        source = pb[v][:, 0:SEG]
                        dve.wait_ge(fed, i * DF + by_dve.index(m) + 1)
                    dve.wait_ge(a_ready, i * ITER + m + 1)
                    dve.wait_ge(weighed, free(i * ITER + m))
                    if seg:
                        dve.wait_ge(scanned, i * ITER + m + CREDIT)
                    nc.vector.tensor_tensor_scan(h[v][:, :], a[v][:, :], source, h[1 - v][:, SEG - 1:SEG] if seg else 0.0,
                                                 ALU.mult, ALU.add).then_inc(scanned, 1)

                def weigh(m):
                    ct, seg, v, _ = place(m)
                    dve.wait_ge(scanned, i * ITER + m + 1 + CREDIT)
                    dve.wait_ge(c_ready, i * ITER + m + 1)
                    dve.wait_ge(added, i * ITER + (m - 1 + STEPS_N))
                    nc.vector.tensor_tensor(hc[v][:, :], h[v][:, :], pcc[v][:, 0:SEG], ALU.mult).then_inc(weighed, 1)

                feed(0)
                for m in range(ITER):
                    if m + 1 in by_dve:
                        feed(m + 1)
                    scan(m)
                    if m:
                        weigh(m - 1)
                weigh(ITER - 1)
            if k:
                for ct in (0, 2):
                    dve.wait_ge(added, NS * STEPS_N + STEPS_N)
                    nc.vector.tensor_copy(in_order(dt[:, ct, :], k), y[:, ct, :].rearrange("p (h w) -> p h w", w=SIDE)).then_inc(ordered, 1)

        @block.gpsimd
        def _(pool):
            pool.sem_inc(added, STEPS_N)
            pool.sem_inc(pool_fed, 1)
            with pool.Fori(0, NS // 2) as i:
                for m in range(ITER):
                    ct, seg, v, half = place(m)
                    for f in ([1] if m == 0 else []) + [m + 3]:
                        if f not in by_pool:
                            continue
                        n = by_pool.index(f)
                        ct1, seg1, _, _ = place(f)
                        pool.wait_ge(b_copied, i * PF + n + 1)
                        nc.gpsimd.tensor_tensor(fed_pool[n % 2][:, :], b_copy[:, :], cols(du, ct1, seg1), ALU.mult).then_inc(pool_fed, 1)
                    pool.wait_ge(weighed, ready(i * ITER + m))
                    pool.wait_ge(added, i * ITER + m + 1)
                    part = y[:, ct, seg * SEG:(seg + 1) * SEG]
                    nc.gpsimd.tensor_tensor(part, part, hc[v][:, :], ALU.add).then_inc(added, 1)

        @block.sync
        def _(sp):
            sp.wait_ge(added, NS * STEPS_N + STEPS_N)
            src = dt if k else y
            slot, row = 4 + k // 2, (k % 2) * REST
            if k:
                sp.wait_ge(ordered, 1)
            sp.dma_start(out[k, :, 0:L], src[:, 0, :]).then_inc(stored, 16)
            if k:
                sp.wait_ge(ordered_act, 1)
            sp.dma_start(out[k, :, L:T], src[:, 1, :]).then_inc(stored, 16)
            if k:
                sp.wait_ge(ordered, 2)
            sp.dma_start(out[slot, row:row + REST, 0:L], src[0:REST, 2, :]).then_inc(stored, 16)
            sp.dma_start(out[slot, row:row + REST, L:T], src[REST:P, 2, :]).then_inc(stored, 16)
            if last is not None:
                sp.wait_ge(stored, 64 * (last + 1))


def ss2d(nc, c, w, x, out, directions=range(KD)):
    with Stage(nc, "ss2d") as s:
        u = s.sb("u", [P, 3, L])
        bc = s.sb("bc", [BROWS, IMAGES, L], BF16)
        aneg = s.sb("aneg", [P, 3, NS])
        sel = s.sb("sel", [BROWS, 3, BC, P], BF16)
        sel_in = s.sem("sel_in")
        xh, xl = s.sb("xh", [P, IMAGES, DC, L], F16), s.sb("xl", [P, IMAGES, DC, L], F16)
        dt, y = s.sb("dt", [P, 3, L]), s.sb("y", [P, 3, L])
        stored = s.sem("y_stored")
        norm_transpose(nc, c, x, xh, xl, 1e-6)
        for n, k in enumerate(directions):
            ss2d_conv(nc, c, w, k, xh, xl, u, dt, y, aneg, (sel, sel_in) if n == 0 else None, stored, n)
            ss2d_project(nc, c, w, k, u, dt, y, bc)
            ss2d_scan(nc, c, w, k, u, dt, y, bc, aneg, sel, out, stored, n if k == directions[-1] else None)


SLOTS = CI // P
NT = T // P


def ss2d_out(nc, c, w, y, x, x1, th, tl, sc):
    xg = tok_groups(x)
    with Stage(nc, "o") as s:
        ident, mean_w = s.sb("ident", [P, P]), s.sb("mean_w", [P, P])
        wo, nw, nb = s.sb("wo", [P, SLOTS, D]), s.sb("nw", [P, SLOTS]), s.sb("nb", [P, SLOTS])
        nbb, bias = s.sb("nbb", [P, SLOTS, P]), s.sb("bias", [P, D])
        gw, gb, ones = s.sb("gw", [P, DC, EX]), s.sb("gb", [1, EX]), s.sb("ones", [P, P])
        epst = s.sb("eps", [P, 1])
        yt = [s.sb(f"yt{u}", [P, SLOTS, G]) for u in range(2)]
        sq = s.sb("sq", [P, SLOTS, G])
        xin = [s.sb(f"xin{u}", [P, GT, D]) for u in range(2)]
        xo = [s.sb(f"xo{u}", [P, GT, D]) for u in range(2)]
        xn = [s.sb(f"xn{u}", [P, GT, D]) for u in range(2)]
        xt = s.sb("xt", [P, DC, G])
        stats, mv = s.sb("stats", [P, GT, 6]), s.sb("mv", [P, GT, 2])
        std, rstd = s.sb("std", [P, 2, GT]), s.sb("rstd", [P, GT])
        var_row = s.sb("var_row", [1, G])
        ystd, yrstd = s.sb("ystd", [P, GT]), s.sb("yrstd", [P, GT])
        pm, po, pt, pg = (s.ps("pm", [P, BANK]), s.ps("po", [P, GT, BANK]), s.ps("pt", [P, DC, BANK]),
                          s.ps("pg", [P, BANK]))
        loaded, y_in, x_in = s.sem("loaded"), [s.sem(f"y_in{u}") for u in range(2)], [s.sem(f"x_in{u}") for u in range(2)]
        (eps_set, setup, bias_sum, mean_ready, centred, squared, var_ready, rooted, projected, x1_ready, nvar_ready, nstd_ready,
         normed, turned, copied, scored, taken, hi_ready, lo_ready, steps, held, x1_steps, row_ready, row_copied, pe_held, act_held, pool_held,
         x1_copied) = (s.sem(x) for x in (
             "eps_set setup bias_sum mean_ready centred squared var_ready rooted projected x1_ready nvar_ready nstd_ready "
             "normed turned copied scored taken hi_ready lo_ready steps held x1_steps row_ready row_copied pe_held act_held pool_held x1_copied").split())
        block = s.block()

        @block.sync
        def _(sp):
            for tile, src in ((ident[:, :], c["ident"]), (mean_w[:, :], c["mean768"]), (wo[:, :, :], w["out_proj"]),
                              (nw[:, :], w["out_nw"]), (nb[:, :], w["out_nb"]), (gw[:, :, :], w["gate_w"]), (gb[:, :], w["gate_b"])):
                sp.dma_start(tile, src).then_inc(loaded, 16)
            with sp.Fori(0, NG // 2) as i:
                for v in range(2):
                    g = i * 2 + v
                    sp.wait_ge(projected, free(g))
                    sp.wait_ge(squared, free(g))
                    sp.dma_start(yt[v][:, :, :], y.rearrange("s p t -> p s t")[:, :, bass.ds(g * G, G)]).then_inc(y_in[v], 16)
                    sp.wait_ge(x1_ready, free(g))
                    sp.dma_start(xin[v][:, :, :], xg[g]).then_inc(x_in[v], 16)

        @block.vector
        def _(dve):
            nc.vector.memset(ones[:, :], 1.0).then_inc(eps_set, 1)
            nc.vector.memset(epst[:, :], 1e-5).then_inc(eps_set, 1)
            dve.sem_inc(x1_ready, CREDIT)
            dve.sem_inc(taken, 1)
            dve.wait_ge(loaded, 112)
            dve.wait_ge(eps_set, 2)
            for j in range(SLOTS):
                ins = nc.vector.tensor_scalar(nbb[:, j, :], ones[:, :], nb[:, j:j + 1], None, ALU.mult)
            ins.then_inc(setup, 1)
            dve.wait_ge(bias_sum, 1)
            nc.vector.tensor_copy(bias[:, :], pm[:, 0:D])
            for j in range(SLOTS):
                ins = nc.vector.tensor_scalar(wo[:, j, :], wo[:, j, :], nw[:, j:j + 1], None, ALU.mult)
            ins.then_inc(setup, 1)
            dve.wait_ge(setup, 2)
            x1_chain, chain = Chain(dve, x1_steps, 2), Chain(dve, steps, NORM_STEPS)

            def centre(g, v):
                dve.wait_ge(mean_ready, g + 1)
                nc.vector.tensor_tensor(yt[v][:, :, :], yt[v][:, :, :],
                                        pm[:, 0:G].rearrange("p (a g) -> p a g", a=1).to_broadcast([P, SLOTS, G]),
                                        ALU.subtract).then_inc(centred, 1)

            def residual(g, i, v):
                x1_chain.start(g)
                dve.wait_ge(rooted, g + 2)
                x1_chain(nc.vector.reciprocal(yrstd[:, :], ystd[:, :]))
                dve.wait_ge(projected, ready(g))
                dve.wait_ge(x_in[v], i * 16 + 16)
                dve.wait_ge(x1_copied, free(g))
                for t in range(GT):
                    ins = nc.vector.scalar_tensor_tensor(out=xo[v][:, t, :], in0=po[:, t, 0:D], scalar=yrstd[:, t:t + 1],
                                                         in1=xin[v][:, t, :], op0=ALU.mult, op1=ALU.add)
                x1_chain(ins)
                nc.vector.tensor_tensor(xo[v][:, :, :], xo[v][:, :, :],
                                        bias[:, :].rearrange("p (a g) -> p a g", a=1).to_broadcast([P, GT, D]),
                                        ALU.add).then_inc(x1_ready, 1)

            def norm(g, v):
                chain.start(g)
                dve.wait_ge(x1_ready, ready(g))
                dve.wait_ge(turned, free(g))
                norm_steps(dve, chain, xo[v], stats, mv, std, rstd, xn[v], nvar_ready, nstd_ready, g, held).then_inc(normed, 1)

            def take(g):
                dve.wait_ge(scored, g + 2)
                settle(dve, held)
                nc.vector.tensor_copy(sc[:, bass.ds(g * GT, GT), :],
                                      pg[:, 0:GT * EX].rearrange("p (t e) -> p t e", e=EX)).then_inc(taken, 1)

            centre(0, 0)
            residual(0, 0, 0)
            centre(1, 1)
            norm(0, 0)
            with dve.Fori(0, NG // 2 - 1) as i:
                for v in range(2):
                    g = i * 2 + v
                    residual(g + 1, i + v, 1 - v)
                    centre(g + 2, v)
                    norm(g + 1, 1 - v)
                    take(g)
            residual(NG - 1, NG // 2 - 1, 1)
            norm(NG - 1, 1)
            take(NG - 2)
            take(NG - 1)

        @block.gpsimd
        def _(pool):
            pool.sem_inc(lo_ready, 1)
            with pool.Fori(0, NG // 2) as i:
                for v in range(2):
                    g = i * 2 + v
                    pool.wait_ge(hi_ready, g + 1)
                    settle(pool, pool_held)
                    at = bass.ds(g * G, G)
                    nc.gpsimd.tensor_tensor(tl[:, :, at], xt[:, :, :], th[:, :, at], ALU.subtract).then_inc(lo_ready, 1)

        @block.tensor
        def _(pe):
            pe.sem_inc(projected, CREDIT)
            pe.sem_inc(turned, CREDIT)
            pe.sem_inc(scored, 1)
            pe.wait_ge(loaded, 112)
            pe.wait_ge(setup, 1)
            for j in range(SLOTS):
                ins = nc.tensor.matmul(pm[:, 0:D], nbb[:, j, :], wo[:, j, :], start=j == 0, stop=j == SLOTS - 1)
            ins.then_inc(bias_sum, 1)
            pe.wait_ge(setup, 2)

            def mean(g, i, v):
                pe.wait_ge(y_in[v], i * 16 + 16)
                pe.wait_ge(rooted, g + 1)
                for j in range(SLOTS):
                    ins = nc.tensor.matmul(pm[:, 0:G], mean_w[:, :], yt[v][:, j, :], start=j == 0, stop=j == SLOTS - 1)
                ins.then_inc(mean_ready, 1)

            def project(g, v):
                pe.wait_ge(centred, g + 1)
                pe.wait_ge(x1_ready, g + CREDIT)
                for t in range(GT):
                    for j in range(SLOTS):
                        ins = nc.tensor.matmul(po[:, t, 0:D], yt[v][:, j, t * P:(t + 1) * P], wo[:, j, :],
                                               start=j == 0, stop=j == SLOTS - 1)
                ins.then_inc(projected, 1)
                pe.wait_ge(squared, ready(g))
                for j in range(SLOTS):
                    ins = nc.tensor.matmul(pm[0:1, 0:G], mean_w[:, 0:1], sq[:, j, :], start=j == 0, stop=j == SLOTS - 1)
                ins.then_inc(row_ready, 1)

            def turn_variance(g):
                pe.wait_ge(row_copied, g + 1)
                settle(pe, pe_held)
                for t in range(GT):
                    ins = nc.tensor.matmul(pm[:, G + t:G + t + 1], var_row[:, t * P:(t + 1) * P], ones[0:1, 0:1], start=True, stop=True)
                ins.then_inc(var_ready, 1)

            def turn(g, v):
                pe.wait_ge(normed, g + 1)
                pe.wait_ge(copied, g + 1)
                for t in range(GT):
                    for d in range(DC):
                        ins = nc.tensor.transpose(pt[:, d, t * P:(t + 1) * P], xn[v][:, t, d * P:(d + 1) * P], ident[:, :])
                ins.then_inc(turned, 1)

            def score(g):
                pe.wait_ge(copied, g + 2)
                pe.wait_ge(taken, g + 1)
                for t in range(GT):
                    out = pg[:, t * EX:(t + 1) * EX]
                    for d in range(DC):
                        nc.tensor.matmul(out, xt[:, d, t * P:(t + 1) * P], gw[:, d, :], start=d == 0, stop=False)
                    ins = nc.tensor.matmul(out, ones[0:1, :], gb[:, :], start=False, stop=True)
                ins.then_inc(scored, 1)

            for g in range(2):
                mean(g, 0, g)
                project(g, g)
                turn_variance(g)
            with pe.Fori(0, NG // 2 - 1) as i:
                for v in range(2):
                    g = i * 2 + v
                    mean(g + 2, i + 1, v)
                    turn(g, v)
                    project(g + 2, v)
                    score(g)
                    turn_variance(g + 2)
            for g in range(NG - 2, NG):
                turn(g, g % 2)
                score(g)

        @block.scalar
        def _(act):
            act.sem_inc(copied, 1)
            act.sem_inc(rooted, 1)
            act.sem_inc(squared, CREDIT)
            act.sem_inc(x1_copied, CREDIT)
            act.wait_ge(eps_set, 2)

            def square(g, v):
                act.wait_ge(centred, g + 1)
                nc.scalar.activation(sq[:, :, :], yt[v][:, :, :], ACT.Square).then_inc(squared, 1)

            def root_y(g, v):
                act.wait_ge(row_ready, g + 1)
                nc.scalar.copy(var_row[:, :], pm[0:1, 0:G]).then_inc(row_copied, 1)
                act.wait_ge(var_ready, g + 1)
                nc.scalar.activation(ystd[:, :], pm[:, G:G + GT], ACT.Sqrt, bias=epst[:, :]).then_inc(rooted, 1)

            def store_x1(g, v):
                act.wait_ge(x1_ready, ready(g))
                settle(act, act_held)
                nc.scalar.copy(x1[:, bass.ds(g * GT, GT), :], xo[v][:, :, :]).then_inc(x1_copied, 1)

            def root(g):
                act.wait_ge(nvar_ready, g + 1)
                nc.scalar.activation(std[:, 1, :], std[:, 0, :], ACT.Sqrt, bias=epst[:, :]).then_inc(nstd_ready, 1)

            def store_t(g):
                act.wait_ge(turned, ready(g))
                act.wait_ge(lo_ready, g + 1)
                act.wait_ge(scored, g + 1)
                nc.scalar.copy(xt[:, :, :], pt[:, :, 0:G]).then_inc(copied, 1)
                act.wait_ge(copied, g + 2)
                settle(act, act_held)
                nc.scalar.copy(th[:, :, bass.ds(g * G, G)], xt[:, :, :]).then_inc(hi_ready, 1)

            for g in range(2):
                square(g, g)
                if g:
                    root(0)
                root_y(g, g)
                store_x1(g, g)
            with act.Fori(0, NG // 2 - 1) as i:
                for v in range(2):
                    g = i * 2 + v
                    square(g + 2, v)
                    root(g + 1)
                    store_t(g)
                    root_y(g + 2, v)
                    store_x1(g + 2, v)
            root(NG - 1)
            for g in range(NG - 2, NG):
                store_t(g)


HALF = HID // 2
HT = HALF // P
PAIRS = HT // 2


def moe(nc, c, w, acc, xh, xl, sc, x2):
    with Stage(nc, "m") as s:
        w1s, w2s = s.sb("w1s", [P, DC, HALF]), s.sb("w2s", [P, HT, D])
        w1h, w1l, w2h, w2l = ([s.sb(f"{x}{v}", shape, F16) for v in range(2)] for x, shape in (
            ("w1h", [P, DC, HALF]), ("w1l", [P, DC, HALF]), ("w2h", [P, HT, D]), ("w2l", [P, HT, D])))
        b1, b2, ones = s.sb("b1", [P, EX * 2 * HT]), s.sb("b2", [1, EX * D]), s.sb("ones", [1, P])
        act_out = [s.sb(f"act_out{v}", [P, 2, G]) for v in range(2)]
        hh, hl = ([s.sb(f"{x}{v}", [P, HT, G], F16) for v in range(2)] for x in ("hh", "hl"))
        gate, rank = s.sb("gate", [P, NT, EX]), s.sb("rank", [P, NT, EX])
        row, above = s.sb("row", [P, NT]), s.sb("above", [P, NT])
        ph = [s.ps(f"ph{v}", [P, 2, BANK]) for v in range(2)]
        py = s.ps("py", [P, GT, BANK])
        (loaded, w_in, split, h_ready, gelu, parted, y_ready, added, stored, steps, shifted, expd, ones_set,
         held, parts, high, pe_held, pool_held, w1_in, first_steps, first_split) = (s.sem(x) for x in "loaded w_in split h_ready gelu parted y_ready added stored steps shifted "
                   "expd ones_set held parts high pe_held pool_held w1_in first_steps first_split".split())
        block = s.block()
        UNIT = NG * GT
        Y_CREDIT = 2 * UNIT

        @block.sync
        def _(sp):
            sp.dma_start(w1s[:, :, :], w["w1"][0, 0]).then_inc(w1_in, 16)
            sp.dma_start(w2s[:, :, :], w["w2"][0, 0]).then_inc(w_in, 16)
            for tile, src in ((b1[:, :], w["b1"]), (b2[:, :], w["b2"])):
                sp.dma_start(tile, src).then_inc(loaded, 16)
            sp.wait_ge(split, 1)
            sp.wait_ge(first_split, 1)
            sp.dma_start(w1s[:, :, :], w["w1"][0, 1]).then_inc(w_in, 16)
            sp.dma_start(w2s[:, :, :], w["w2"][0, 1]).then_inc(w_in, 16)
            with sp.Fori(1, EX) as e:
                for v in range(2):
                    sp.wait_ge(split, e * 2 + v)
                    sp.dma_start(w1s[:, :, :], w["w1"][e, v]).then_inc(w_in, 16)
                    sp.dma_start(w2s[:, :, :], w["w2"][e, v]).then_inc(w_in, 16)
            with sp.Fori(0, NG) as g:
                sp.wait_ge(added, g * GT + ((EX * 2 - 1) * UNIT + 2 * GT))
                sp.dma_start(tok_groups(x2)[g], acc[:, bass.ds(g * GT, GT), :]).then_inc(stored, 16)
            sp.wait_ge(stored, 16 * NG)

        @block.gpsimd
        def _(pool):
            def parts_of(e, v, pairs):
                unit = e * 2 + v
                pool.wait_ge(w_in, unit * 32 + 16)
                pool.wait_ge(y_ready, unit * UNIT + UNIT)
                settle(pool, pool_held)
                for high_part, whole, _ in pairs:
                    nc.gpsimd.tensor_scalar(high_part[v][:, :, :], whole[:, :, :], W_SCALE, 1.0, ALU.mult, ALU.mult)
                    ins = nc.gpsimd.tensor_scalar(whole[:, :, :], whole[:, :, :], W_SCALE, 1.0, ALU.mult, ALU.mult)
                ins.then_inc(parts, 1)
                pool.wait_ge(parts, unit + 1)
                for high_part, whole, low_part in pairs:
                    ins = nc.gpsimd.tensor_tensor(low_part[v][:, :, :], whole[:, :, :], high_part[v][:, :, :], ALU.subtract)
                ins.then_inc(split, 1)

            both = ((w1h, w1s, w1l), (w2h, w2s, w2l))
            parts_of(0, 0, both[1:])
            pool.wait_ge(first_split, 1)
            parts_of(0, 1, both)
            with pool.Fori(1, EX) as e:
                for v in range(2):
                    parts_of(e, v, both)

        @block.tensor
        def _(pe):
            pe.sem_inc(y_ready, Y_CREDIT)
            pe.wait_ge(first_split, 1)
            pe.wait_ge(loaded, 32)
            pe.wait_ge(ones_set, 2)
            with pe.Fori(0, EX) as e:
                for half in range(2):
                    pe.wait_ge(split, e * 2 + half + 1)
                    settle(pe, pe_held)
                    with pe.Fori(0, NG // 2) as i:
                        turn0 = (e * 2 + half) * NG + i * 2

                        def hidden(v):
                            cols = bass.ds((i * 2 + v) * G, G)
                            for jj in range(PAIRS):
                                pe.wait_ge(gelu, (turn0 + v) * PAIRS + jj + 1)
                                for j in (2 * jj, 2 * jj + 1):
                                    terms = [(a, b, d) for a, b in ((w1h, xh), (w1h, xl), (w1l, xh)) for d in range(DC)]
                                    for n, (a, b, d) in enumerate(terms):
                                        ins = nc.tensor.matmul(ph[(v * PAIRS + jj) % 2][:, j % 2, 0:G],
                                                               a[half][:, d, j * P:(j + 1) * P], b[:, d, cols],
                                                               start=n == 0, stop=n == len(terms) - 1)
                                ins.then_inc(h_ready, 1)

                        def outputs(v):
                            pe.wait_ge(parted, (turn0 + v) * PAIRS + PAIRS + CREDIT)
                            for t in range(GT):
                                pe.wait_ge(added, (turn0 + v) * GT + t + 1)
                                if half == 0:
                                    settle(pe, pe_held)
                                    nc.tensor.matmul(py[:, t, 0:D], ones[:, :], b2[:, bass.ds(e * D, D)], start=True, stop=False)
                                terms = [(a, b, j) for a, b in ((hh, w2h), (hl, w2h), (hh, w2l)) for j in range(HT)]
                                for n, (a, b, j) in enumerate(terms):
                                    ins = nc.tensor.matmul(py[:, t, 0:D], a[v][:, j, t * P:(t + 1) * P], b[half][:, j, :],
                                                           start=n == 0 and half == 1, stop=n == len(terms) - 1)
                                ins.then_inc(y_ready, 1)

                        hidden(0)
                        hidden(1)
                        outputs(0)
                        outputs(1)

        @block.scalar
        def _(act):
            act.sem_inc(gelu, CREDIT)
            act.wait_ge(loaded, 32)
            act.wait_ge(shifted, 1)
            nc.scalar.activation(sc[:, :, :], sc[:, :, :], ACT.Exp).then_inc(expd, 1)
            with act.Fori(0, EX) as e:
                for half in range(2):
                    with act.Fori(0, NG // 2) as i:
                        for v in range(2):
                            for jj in range(PAIRS):
                                n = ((e * 2 + half) * NG + i * 2 + v) * PAIRS + jj
                                b = (v * PAIRS + jj) % 2
                                act.wait_ge(parted, n + 1)
                                act.wait_ge(h_ready, n + 1)
                                settle(act, held)
                                for j in range(2):
                                    ins = nc.scalar.activation(act_out[b][:, j, :], ph[b][:, j, 0:G], ACT.Gelu, scale=1.0 / W_SCALE,
                                                               bias=b1[:, bass.ds(e * (2 * HT) + (half * HT + 2 * jj + j), 1)])
                                ins.then_inc(gelu, 1)

        @block.vector
        def _(dve):
            dve.sem_inc(parted, CREDIT)
            dve.sem_inc(added, GT)
            dve.wait_ge(loaded, 32)
            nc.vector.memset(ones[:, :], 1.0).then_inc(ones_set, 1)
            dve.wait_ge(w1_in, 16)
            first = Chain(dve, first_steps, None)
            nc.vector.tensor_scalar(w1h[0][:, :, :], w1s[:, :, :], W_SCALE, None, ALU.mult)
            first(nc.vector.tensor_scalar(w1s[:, :, :], w1s[:, :, :], W_SCALE, None, ALU.mult))
            nc.vector.tensor_tensor(w1l[0][:, :, :], w1s[:, :, :], w1h[0][:, :, :], ALU.subtract).then_inc(first_split, 1)
            nc.vector.tensor_scalar(b2[:, :], b2[:, :], W_SCALE, None, ALU.mult).then_inc(ones_set, 1)
            chain = Chain(dve, steps, None)
            chain(nc.vector.tensor_reduce(row[:, :], sc[:, :, :], AX.X, ALU.max))

            def by_expert(t):
                return t[:, :].rearrange("p (n a) -> p n a", a=1).to_broadcast([P, NT, EX])

            nc.vector.tensor_tensor(sc[:, :, :], sc[:, :, :], by_expert(row), ALU.subtract).then_inc(shifted, 1)
            dve.wait_ge(expd, 1)
            chain(nc.vector.tensor_reduce(row[:, :], sc[:, :, :], AX.X, ALU.add))
            chain(nc.vector.reciprocal(row[:, :], row[:, :]))
            chain(nc.vector.tensor_tensor(sc[:, :, :], sc[:, :, :], by_expert(row), ALU.mult))
            for j in range(EX):
                ins = nc.vector.memset(rank[:, :, j], float(j))
            chain(ins)
            for i in range(EX):
                for j in range(i + 1, EX):
                    chain(nc.vector.tensor_tensor(above[:, :], sc[:, :, j], sc[:, :, i], ALU.is_gt))
                    chain(nc.vector.tensor_tensor(rank[:, :, i], rank[:, :, i], above[:, :], ALU.add))
                    chain(nc.vector.tensor_tensor(rank[:, :, j], rank[:, :, j], above[:, :], ALU.subtract))
            chain(nc.vector.tensor_scalar(rank[:, :, :], rank[:, :, :], 2.0, None, ALU.is_lt))
            chain(nc.vector.tensor_tensor(sc[:, :, :], sc[:, :, :], rank[:, :, :], ALU.mult))
            chain(nc.vector.tensor_reduce(row[:, :], sc[:, :, :], AX.X, ALU.add))
            chain(nc.vector.tensor_scalar(row[:, :], row[:, :], 1e-9, None, ALU.add))
            chain(nc.vector.reciprocal(row[:, :], row[:, :]))
            chain(nc.vector.tensor_tensor(gate[:, :, :], sc[:, :, :], by_expert(row), ALU.mult))
            chain(nc.vector.tensor_scalar(gate[:, :, :], gate[:, :, :], 1.0 / W_SCALE, None, ALU.mult))
            with dve.Fori(0, EX) as e:
                for half in range(2):
                    with dve.Fori(0, NG // 2) as i:
                        turn0 = (e * 2 + half) * NG + i * 2

                        def part(v):
                            dve.wait_ge(y_ready, (turn0 + v) * GT + (Y_CREDIT - GT))
                            for jj in range(PAIRS):
                                n, b = (turn0 + v) * PAIRS + jj, (v * PAIRS + jj) % 2
                                at = slice(2 * jj, 2 * jj + 2)
                                dve.wait_ge(gelu, n + 1 + CREDIT)
                                nc.vector.tensor_copy(hh[v][:, at, :], act_out[b][:, :, :]).then_inc(high, 1)
                                dve.wait_ge(high, n + 1)
                                nc.vector.tensor_tensor(hl[v][:, at, :], act_out[b][:, :, :], hh[v][:, at, :],
                                                        ALU.subtract).then_inc(parted, 1)

                        def add(v):
                            for t in range(GT):
                                n = (turn0 + v) * GT + t
                                tile = (i * 2 + v) * GT + t
                                dve.wait_ge(y_ready, n + 1 + Y_CREDIT)
                                into = acc[:, bass.ds(tile, 1), :].rearrange("p a d -> p (a d)")
                                nc.vector.scalar_tensor_tensor(out=into, in0=py[:, t, 0:D],
                                                               scalar=gate[:, bass.ds(tile, 1), bass.ds(e, 1)].rearrange("p a b -> p (a b)"), in1=into,
                                                               op0=ALU.mult, op1=ALU.add).then_inc(added, 1)

                        part(0)
                        part(1)
                        add(0)
                        add(1)


ZD = DIN + HEADS


def mamba_gate(nc, c, w, x, xn_ch, sz, dt_raw):
    src_g, sz_g = tok_groups(x), tok_groups(sz)
    with Stage(nc, "g") as s:
        ident, epst = s.sb("ident", [P, P]), s.sb("eps", [P, 1])
        wz = s.sb("wz", [P, DC, ZD])
        wh, wl = s.sb("wh", [P, DC, ZD], F16), s.sb("wl", [P, DC, ZD], F16)
        xin = [s.sb(f"x{u}", [P, GT, D]) for u in range(2)]
        xn = [s.sb(f"xn{u}", [P, GT, D]) for u in range(2)]
        xt = [s.sb(f"xt{u}", [P, DC, G]) for u in range(2)]
        xh, xl = ([s.sb(f"{x}{u}", [P, DC, G], F16) for u in range(2)] for x in ("xh", "xl"))
        szt = [s.sb(f"szt{u}", [P, GT, DIN]) for u in range(2)]
        raw = s.sb("raw", [P, NT, HEADS])
        stats, mv = s.sb("stats", [P, GT, 6]), s.sb("mv", [P, GT, 2])
        std, rstd = s.sb("std", [P, 2, GT]), s.sb("rstd", [P, GT])
        pt = s.ps("pt", [P, DC, BANK])
        pz = [s.ps(f"pz{v}", [P, 2, BANK]) for v in range(2)]
        x_in, sz_out = ([s.sem(f"{x}{u}") for u in range(2)] for x in ("x_in", "sz_out"))
        (loaded, eps_set, var_ready, std_ready, normed, steps, turned, copied, z_ready, gated, high_ready, low_ready, w_split, held, kept, act_held,
         dt_out) = (s.sem(x) for x in "loaded eps_set var_ready std_ready normed steps turned copied z_ready gated high_ready "
                    "low_ready w_split held kept act_held dt_out".split())
        block = s.block()

        @block.sync
        def _(sp):
            for tile, src in ((ident[:, :], c["ident"]), (wz[:, :, :], w["w_z"])):
                sp.dma_start(tile, src).then_inc(loaded, 16)
            with sp.Fori(0, NG // 2) as i:
                for u in range(2):
                    g = i * 2 + u
                    sp.wait_ge(normed, free(g))
                    sp.dma_start(xin[u][:, :, :], src_g[g]).then_inc(x_in[u], 16)
            sp.wait_ge(gated, NG * GT + CREDIT)
            sp.dma_start(dt_raw, raw[:, :, :]).then_inc(dt_out, 16)
            sp.wait_ge(dt_out, 16)

        @block.vector
        def _(dve):
            nc.vector.memset(epst[:, :], 1e-6).then_inc(eps_set, 1)
            dve.sem_inc(normed, CREDIT)
            dve.wait_ge(loaded, 32)
            nc.vector.tensor_scalar(wh[:, :, :], wz[:, :, :], W_SCALE, None, ALU.mult).then_inc(w_split, 1)
            nc.vector.tensor_scalar(wz[:, :, :], wz[:, :, :], W_SCALE, None, ALU.mult).then_inc(w_split, 1)
            dve.wait_ge(w_split, 2)
            nc.vector.tensor_tensor(wl[:, :, :], wz[:, :, :], wh[:, :, :], ALU.subtract).then_inc(w_split, 1)
            chain = Chain(dve, steps, NORM_STEPS)

            def norm(g, i, u):
                chain.start(g)
                dve.wait_ge(x_in[u], i * 16 + 16)
                dve.wait_ge(turned, free(g))
                norm_steps(dve, chain, xin[u], stats, mv, std, rstd, xn[u], var_ready, std_ready, g,
                           held).then_inc(normed, 1)

            norm(0, 0, 0)
            norm(1, 0, 1)
            with dve.Fori(0, NG // 2 - 1) as i:
                for u in range(2):
                    norm(i * 2 + u + 2, i + 1, u)

        @block.tensor
        def _(pe):
            pe.sem_inc(turned, CREDIT)
            pe.wait_ge(loaded, 32)
            pe.wait_ge(w_split, 3)

            def turn(g, u):
                pe.wait_ge(normed, ready(g))
                pe.wait_ge(copied, g + CREDIT)
                for t in range(GT):
                    for d in range(DC):
                        ins = nc.tensor.transpose(pt[:, d, t * P:(t + 1) * P], xn[u][:, t, d * P:(d + 1) * P],
                                                  ident[:, :])
                ins.then_inc(turned, 1)

            def products(g, u):
                pe.wait_ge(low_ready, ready(g))
                for t in range(GT):
                    v = (u * GT + t) % 2
                    pe.wait_ge(gated, free(g * GT + t))
                    for half, width in ((0, D), (1, D + HEADS)):
                        terms = [(a, b, d) for a, b in ((xh, wh), (xl, wh), (xh, wl)) for d in range(DC)]
                        for n, (a, b, d) in enumerate(terms):
                            ins = nc.tensor.matmul(pz[v][:, half, 0:width], a[u][:, d, t * P:(t + 1) * P],
                                                   b[:, d, half * D:half * D + width], start=n == 0, stop=n == len(terms) - 1)
                    ins.then_inc(z_ready, 1)

            turn(0, 0)
            turn(1, 1)
            with pe.Fori(0, NG // 2 - 1) as i:
                for u in range(2):
                    products(i * 2 + u, u)
                    turn(i * 2 + u + 2, u)
            products(NG - 2, 0)
            products(NG - 1, 1)

        @block.gpsimd
        def _(pool):
            pool.sem_inc(low_ready, CREDIT)
            with pool.Fori(0, NG // 2) as i:
                for u in range(2):
                    g = i * 2 + u
                    pool.wait_ge(high_ready, g + 1)
                    nc.gpsimd.tensor_tensor(xl[u][:, :, :], xt[u][:, :, :], xh[u][:, :, :], ALU.subtract).then_inc(low_ready, 1)

        @block.scalar
        def _(act):
            act.sem_inc(copied, CREDIT)
            act.sem_inc(kept, CREDIT)
            act.sem_inc(gated, CREDIT)
            for u in range(2):
                act.sem_inc(sz_out[u], 16)
            act.wait_ge(eps_set, 1)

            def root(g):
                act.wait_ge(var_ready, g + 1)
                nc.scalar.activation(std[:, 1, :], std[:, 0, :], ACT.Sqrt, bias=epst[:, :]).then_inc(std_ready, 1)

            def copy(g, i, u):
                act.wait_ge(turned, ready(g))
                act.wait_ge(low_ready, free(g))
                act.wait_ge(kept, free(g))
                nc.scalar.copy(xt[u][:, :, :], pt[:, :, 0:G]).then_inc(copied, 1)
                act.wait_ge(copied, ready(g))
                nc.scalar.copy(xh[u][:, :, :], xt[u][:, :, :]).then_inc(high_ready, 1)
                settle(act, act_held)
                nc.scalar.copy(xn_ch[:, :, bass.ds(g * G, G)], xt[u][:, :, :]).then_inc(kept, 1)

            def gates(g, i, u):
                act.wait_ge(sz_out[u], i * 16 + 16)
                for t in range(GT):
                    v = (u * GT + t) % 2
                    act.wait_ge(z_ready, g * GT + t + 1)
                    nc.scalar.activation(szt[u][:, t, :].rearrange("p (a d) -> p a d", a=2), pz[v][:, :, 0:D],
                                         ACT.Silu, scale=1.0 / W_SCALE)
                    nc.scalar.activation(raw[:, bass.ds(g * GT + t, 1), :].rearrange("p a h -> p (a h)"),
                                         pz[v][:, 1, D:D + HEADS], ACT.Copy, scale=1.0 / W_SCALE).then_inc(gated, 1)

            def store(g, u):
                act.wait_ge(gated, g * GT + GT + CREDIT)
                act.dma_start(sz_g[g], szt[u][:, :, :]).then_inc(sz_out[u], 16)

            for u in range(2):
                root(u)
                copy(u, 0, u)
            with act.Fori(0, NG // 2 - 1) as i:
                for u in range(2):
                    g = i * 2 + u
                    root(g + 2)
                    gates(g, i, u)
                    copy(g + 2, i + 1, u)
                    store(g, u)
            for u in range(2):
                gates(NG - 2 + u, NG // 2 - 1, u)
                store(NG - 2 + u, u)
            for u in range(2):
                act.wait_ge(sz_out[u], 16 * (NG // 2 + 1))


CT = -(-CONV // P)


def mamba_conv(nc, w, xn, xbc):
    with Stage(nc, "v") as s:
        wct = [s.sb(f"wct{b}", [P, DC, P]) for b in range(IMAGES)]
        taps, bias = s.sb("taps", [P, CT, 9]), s.sb("bias", [P, CT])
        pad = [s.sb(f"pad{b}", [P, SIDE + 2, SIDE + 2]) for b in range(IMAGES)]
        acc = [s.sb(f"acc{b}", [P, L]) for b in range(IMAGES)]
        out = [s.sb(f"out{b}", [P, L]) for b in range(IMAGES)]
        tmp = [s.sb(f"tmp{b}", [P, AT1, L]) for b in range(IMAGES)]
        pi = s.ps("pi", [P, GI, BANK])
        w_in, stored = ([s.sem(f"{x}{b}") for b in range(IMAGES)] for x in ("w_in", "stored"))
        multiplied, act_tapped, pool_steps = s.sem("multiplied"), s.sem("act_tapped"), s.sem("pool_steps")
        loaded, zeroed, projected, padded, tapped, convolved, active, held = (s.sem(x) for x in (
            "loaded zeroed projected padded tapped convolved active held".split()))
        block = s.block()

        @block.sync
        def _(sp):
            for b in range(IMAGES):
                sp.sem_inc(stored[b], 16)
            for b in range(IMAGES):
                sp.dma_start(wct[b][:, :, :], w["w_x"][0]).then_inc(w_in[b], 16)
            sp.dma_start(taps[:, :, :], w["conv1"]).then_inc(loaded, 16)
            sp.dma_start(bias[:, :], w["conv1_b"]).then_inc(loaded, 16)
            with sp.Fori(1, CT) as ct:
                for b in range(IMAGES):
                    turn = ct * 2 + b
                    sp.wait_ge(projected, (turn - 1) * GI + CREDIT)
                    sp.dma_start(wct[b][:, :, :], w["w_x"][ct]).then_inc(w_in[b], 16)
                    sp.wait_ge(active, turn - 2 + CREDIT + 1)
                    sp.dma_start(xbc[ct - 1, :, b * L:(b + 1) * L], out[b][:, :]).then_inc(stored[b], 16)
            for b in range(IMAGES):
                sp.wait_ge(active, ready(2 * (CT - 1) + b))
                sp.dma_start(xbc[CT - 1, :, b * L:(b + 1) * L], out[b][:, :]).then_inc(stored[b], 16)
            for b in range(IMAGES):
                sp.wait_ge(stored[b], 16 * (CT + 1))

        @block.gpsimd
        def _(pool):
            for b in range(IMAGES):
                nc.gpsimd.memset(pad[b][:, :, :], 0.0).then_inc(zeroed, 1)
            chain = Chain(pool, pool_steps, AT1 - 2)
            with pool.Fori(0, CT) as ct:
                for b in range(IMAGES):
                    turn = ct * 2 + b
                    chain.start(turn)
                    for t in range(1, AT1):
                        pool.wait_ge(multiplied, turn * AT1 + t + 1)
                        ins = nc.gpsimd.tensor_tensor(tmp[b][:, 0, :], tmp[b][:, 0, :], tmp[b][:, t, :], ALU.add)
                        if t < AT1 - 1:
                            chain(ins)
                    ins.then_inc(act_tapped, 1)

        @block.tensor
        def _(pe):
            pe.sem_inc(projected, CREDIT)
            with pe.Fori(0, CT) as ct:
                for b in range(IMAGES):
                    pe.wait_ge(w_in[b], ct * 16 + 16)
                    for q in range(GI):
                        pe.wait_ge(padded, (ct * 2 + b) * GI + q + 1)
                        for d in range(DC):
                            ins = nc.tensor.matmul(pi[:, q, 0:G], wct[b][:, d, :], xn[:, d, b * L + q * G:b * L + (q + 1) * G],
                                                   start=d == 0, stop=d == DC - 1)
                        ins.then_inc(projected, 1)

        @block.vector
        def _(dve):
            dve.sem_inc(convolved, CREDIT)
            dve.wait_ge(loaded, 32)
            chain = Chain(dve, tapped, 9 - AT1)
            with dve.Fori(0, CT) as ct:
                for b in range(IMAGES):
                    turn = ct * 2 + b
                    chain.start(turn)
                    dve.wait_ge(padded, (turn + 2) * GI)
                    dve.wait_ge(active, turn + 1)
                    view = acc[b][:, :].rearrange("p (h w) -> p h w", w=SIDE)
                    for t in range(9 - AT1):
                        tap = taps[:, bass.ds(ct, 1), t:t + 1].rearrange("p a b -> p (a b)")
                        rows = pad[b][:, t // 3:t // 3 + SIDE, t % 3:t % 3 + SIDE]
                        if t == 0:
                            ins = nc.vector.tensor_scalar(view, rows, tap, None, ALU.mult)
                        else:
                            ins = nc.vector.scalar_tensor_tensor(out=view, in0=rows, scalar=tap, in1=view,
                                                                 op0=ALU.mult, op1=ALU.add)
                        chain(ins)
                    dve.wait_ge(act_tapped, turn + 1)
                    nc.vector.tensor_tensor(acc[b][:, :], acc[b][:, :], tmp[b][:, 0, :], ALU.add).then_inc(convolved, 1)

        @block.scalar
        def _(act):
            act.sem_inc(padded, GI)
            act.sem_inc(active, 2)
            act.wait_ge(loaded, 32)
            act.wait_ge(zeroed, 2)

            def copies(ct, b):
                turn = ct * 2 + b
                act.wait_ge(convolved, free(turn))
                for q in range(GI):
                    act.wait_ge(projected, turn * GI + q + 1 + CREDIT)
                    nc.scalar.copy(pad[b][:, q * ROWS + 1:(q + 1) * ROWS + 1, 1:SIDE + 1],
                                   pi[:, q, 0:G].rearrange("p (h w) -> p h w", w=SIDE)).then_inc(padded, 1)
                act.wait_ge(padded, (turn + 2) * GI)
                settle(act, held)
                for t in range(AT1):
                    tap = 9 - AT1 + t
                    nc.scalar.activation(tmp[b][:, t, :].rearrange("p (h w) -> p h w", w=SIDE),
                                               pad[b][:, tap // 3:tap // 3 + SIDE, tap % 3:tap % 3 + SIDE], ACT.Copy,
                                               scale=taps[:, bass.ds(ct, 1), tap:tap + 1].rearrange("p a b -> p (a b)")).then_inc(multiplied, 1)

            def silu(ct, b):
                act.wait_ge(convolved, ready(ct * 2 + b))
                act.wait_ge(stored[b], ct * 16 + 16)
                settle(act, held)
                nc.scalar.activation(out[b][:, :], acc[b][:, :], ACT.Silu, bias=bias[:, bass.ds(ct, 1)]).then_inc(active, 1)

            copies(0, 0)
            copies(0, 1)
            silu(0, 0)
            with act.Fori(1, CT) as ct:
                copies(ct, 0)
                silu(ct - 1, 1)
                copies(ct, 1)
                silu(ct, 0)
            silu(CT - 1, 1)


NQ = L // P
HH = HEADS // 2
B_AT, CUM, SUF, TOT, SMALL = P, P + NS, P + NS + HEADS, P + NS + 2 * HEADS, P + NS + 3 * HEADS


def mamba_scan(nc, c, w, x, sz, dt_raw, xbc, out):
    with Stage(nc, "s") as s:
        ident, upto, beyond = s.sb("ident", [P, P]), s.sb("upto", [P, P]), s.sb("beyond", [P, P])
        ones = s.sb("ones", [P, P])
        wo = s.sb("wo", [P, SLOTS, D])
        d1, gamma, beta = s.sb("d1", [P, DIN]), s.sb("gamma", [P, DIN]), s.sb("beta", [P, DIN])
        dtb, alog, epst = s.sb("dtb", [P, HEADS]), s.sb("alog", [P, HEADS]), s.sb("eps", [P, 1])
        ln_one = s.sb("ln_one", [P, 2])
        raw, e, one_e, ln, corr = (s.sb(x, [P, NT, HEADS]) for x in ("raw", "e", "one_e", "ln", "corr"))
        da = s.sb("da", [P, NT, 2 * HEADS])

        def both(name, shape):
            return [s.sb(f"{name}{b}", shape) for b in range(IMAGES)]

        xc, bt, ctr = both("xc", [P, SLOTS, P]), both("bt", [NS, P]), both("ct", [NS, P])
        szt, xin, xo = both("szt", [P, DIN]), both("xin", [P, D]), both("xo", [P, D])
        dab, r = both("dab", [P, 2 * HEADS]), both("r", [P, HEADS, P])
        xs, xdt, xde, xd1 = both("xs", [P, DIN]), both("xdt", [P, DIN]), both("xde", [P, DIN]), both("xd1", [P, DIN])
        gs, es = both("gs", [P, SMALL]), both("es", [P, 3 * HEADS])
        y, state, yts = both("y", [P, DIN]), both("state", [NS, DIN]), both("yts", [P, SLOTS, P])
        gm, ex, m = s.sb("gm", [P, P]), s.sb("ex", [P, HEADS, P]), s.sb("m", [P, HEADS, P])
        stats = s.sb("stats", [P, 2, 6])
        mv, lnv, rstd = both("mv", [P, 2]), both("lnv", [P, 2]), both("rstd", [P, 1])
        px, psm, pd, py = (s.ps("px", [P, 2, BANK]), s.ps("psm", [P, BANK]), s.ps("pd", [P, 3, BANK]),
                           s.ps("py", [P, 2, BANK]))
        xc_in, tok_in, xo_out = ([s.sem(f"{x}{b}") for b in range(IMAGES)] for x in ("xc_in", "tok_in", "xo_out"))
        (loaded, set_up, a_exp, e_ready, one_ready, ln_ready, steps0, prepared, x_turned, x_copied, sums_ready, gs_ready,
         es_ready, d_ready, ex_ready, dab_ready, r_ready, xd_ready, xde_ready, xdt_ready, m_ready, ydiag, yoff, ds_ready,
         weighed, updated, combined, steps, var_ready, rstd_ready, gated, yt_ready, yt_copied, out_ready, added, held, act_steps,
         pool_held, pe_held, one_set, gm_ready, gate_steps) = (s.sem(x) for x in (
             "loaded set_up a_exp e_ready one_ready ln_ready steps0 prepared x_turned x_copied sums_ready gs_ready "
             "es_ready d_ready ex_ready dab_ready r_ready xd_ready xde_ready xdt_ready m_ready ydiag yoff ds_ready "
             "weighed updated combined steps var_ready rstd_ready gated yt_ready yt_copied out_ready added held act_steps "
             "pool_held pe_held one_set gm_ready gate_steps").split())
        block = s.block()

        def heads(t):
            return t.rearrange("p (h a) -> p h a", a=1).to_broadcast([P, HEADS, HP])

        def by_head(t):
            return t[:, :].rearrange("p (h c) -> p h c", h=HEADS)

        def banks(t):
            return t.rearrange("p (a d) -> p a d", a=2)

        @block.sync
        def _(sp):
            for tile, src in ((raw[:, :, :], dt_raw), (dtb[:, :], w["dt1_b"]), (alog[:, :], w["a1_log"]),
                              (ident[:, :], c["ident"]), (upto[:, :], c["upto"]), (beyond[:, :], c["beyond"]),
                              (d1[:, :], w["d1"]), (gamma[:, :], w["gamma"]), (beta[:, :], w["beta"]), (wo[:, :, :], w["w_out1"])):
                sp.dma_start(tile, src).then_inc(loaded, 16)
            xt, szg, xg, og = (a.rearrange("(b q p) d -> b q p d", b=IMAGES, p=P) for a in (x, sz, x, out))
            bc_rows = xbc[SLOTS]

            def load(q, b):
                at = bass.ds(q * P + b * L, P)
                sp.wait_ge(x_turned, free(q * 2 + b))
                sp.wait_ge(yoff, q * 2 + b + CREDIT - 1)
                sp.dma_start(xc[b][:, :, :], xbc[0:SLOTS].rearrange("s p t -> p s t")[:, :, at]).then_inc(xc_in[b], 16)
                sp.dma_start(bt[b][:, :], bc_rows[0:NS, at]).then_inc(xc_in[b], 16)
                sp.dma_start(ctr[b][:, :], bc_rows[NS:2 * NS, at]).then_inc(xc_in[b], 16)

            def load_tok(q, b):
                sp.wait_ge(added, free(q * 2 + b))
                sp.dma_start(szt[b][:, :], szg[b, q]).then_inc(tok_in[b], 16)
                sp.dma_start(xin[b][:, :], xg[b, q]).then_inc(tok_in[b], 16)

            for b in range(IMAGES):
                sp.sem_inc(xo_out[b], 16)
                load(0, b)
                load_tok(0, b)
            with sp.Fori(1, NQ) as q:
                for b in range(IMAGES):
                    load(q, b)
                    load_tok(q, b)
                    sp.dma_start(og[b, q - 1], xo[b][:, :]).then_inc(xo_out[b], 16)
            for b in range(IMAGES):
                sp.wait_ge(added, free(NQ * 2 + b))
                sp.dma_start(og[b, NQ - 1], xo[b][:, :]).then_inc(xo_out[b], 16)
            for b in range(IMAGES):
                sp.wait_ge(xo_out[b], 16 * (NQ + 1))

        @block.tensor
        def _(pe):
            pe.sem_inc(x_turned, CREDIT)
            pe.sem_inc(d_ready, CREDIT)
            pe.sem_inc(yoff, CREDIT)
            pe.wait_ge(loaded, 160)
            pe.wait_ge(set_up, 4)

            def front(q, b):
                turn = q * 2 + b
                pe.wait_ge(xc_in[b], q * 48 + 48)
                pe.wait_ge(weighed, turn + 1)
                for j in range(SLOTS):
                    ins = nc.tensor.transpose(px[:, j // DC, (j % DC) * P:(j % DC + 1) * P], xc[b][:, j, :], ident[:, :])
                ins.then_inc(x_turned, 1)
                pe.wait_ge(gs_ready, turn + 1)
                pe.wait_ge(dab_ready, turn + CREDIT + 1)
                settle(pe, pe_held)
                a = dab[b][:, HEADS:2 * HEADS]
                nc.tensor.matmul(psm[:, 0:P], bt[b][:, :], ctr[b][:, :], start=True, stop=True)
                nc.tensor.transpose(psm[:, B_AT:CUM], bt[b][:, :], ident[0:NS, 0:NS])
                nc.tensor.matmul(psm[:, CUM:SUF], upto[:, :], a, start=True, stop=True)
                nc.tensor.matmul(psm[:, SUF:TOT], beyond[:, :], a, start=True, stop=True)
                nc.tensor.matmul(psm[:, TOT:SMALL], ones[:, :], a, start=True, stop=True).then_inc(sums_ready, 1)

            def decay(q, b):
                turn = q * 2 + b
                pe.wait_ge(r_ready, turn + 1)
                pe.wait_ge(updated, turn + 1)
                for j in range(3):
                    ins = nc.tensor.matmul(pd[:, j, :], beyond[:, :], r[b][:, 4 * j:4 * j + 4, :], start=True, stop=True)
                ins.then_inc(d_ready, 1)

            def middle(q, b):
                turn = q * 2 + b
                pe.wait_ge(x_copied, turn + 1)
                pe.wait_ge(updated, turn + 1)
                for half in range(2):
                    ins = nc.tensor.matmul(px[:, half, 0:D], ctr[b][:, :], state[b][:, half * D:(half + 1) * D], start=True, stop=True)
                ins.then_inc(yoff, 1)
                pe.wait_ge(m_ready, ready(turn))
                pe.wait_ge(added, free(turn))
                for h in range(HEADS):
                    at = (h % HH) * HP
                    ins = nc.tensor.matmul(py[:, h // HH, at:at + HP], m[:, h, :], xdt[b][:, h * HP:(h + 1) * HP],
                                           start=True, stop=True)
                ins.then_inc(ydiag, 1)
                pe.wait_ge(xde_ready, turn + 1)
                for half in range(2):
                    ins = nc.tensor.matmul(pd[0:NS, half, 0:D], gs[b][:, B_AT:CUM], xde[b][:, half * D:(half + 1) * D],
                                           start=True, stop=True)
                ins.then_inc(ds_ready, 1)

            def turn_y(q, b, last_y):
                pe.wait_ge(gated, q * 2 + b + 1)
                pe.wait_ge(combined, last_y + 1)
                for j in range(SLOTS):
                    ins = nc.tensor.transpose(py[:, j // DC, (j % DC) * P:(j % DC + 1) * P], y[b][:, j * P:(j + 1) * P], ident[:, :])
                ins.then_inc(yt_ready, 1)

            def product(q, b):
                pe.wait_ge(yt_copied, q * 2 + b + 1)
                for j in range(SLOTS):
                    ins = nc.tensor.matmul(py[:, 0, 0:D], yts[b][:, j, :], wo[:, j, :], start=j == 0, stop=j == SLOTS - 1)
                ins.then_inc(out_ready, 1)

            front(0, 0)
            decay(0, 0)
            middle(0, 0)
            front(0, 1)
            decay(0, 1)
            with pe.Fori(0, NQ - 1) as q:
                for b in range(IMAGES):
                    middle(q + b, 1 - b)
                    front(q + 1, b)
                    turn_y(q, b, q * 2 + b + 1)
                    decay(q + 1, b)
                    product(q, b)
            middle(NQ - 1, 1)
            turn_y(NQ - 1, 0, 2 * NQ - 1)
            product(NQ - 1, 0)
            pe.wait_ge(added, free(2 * NQ))
            turn_y(NQ - 1, 1, 2 * NQ - 1)
            product(NQ - 1, 1)

        @block.scalar
        def _(act):
            nc.scalar.preload_act_table_set("natural_log_exp_and_others")
            act.sem_inc(gs_ready, 1)
            act.wait_ge(set_up, 4)
            act.wait_ge(one_set, 1)
            nc.scalar.activation(ln_one[:, 1:2], ln_one[:, 0:1], ACT.Ln)
            act.wait_ge(loaded, 160)
            nc.scalar.activation(alog[:, :], alog[:, :], ACT.Exp).then_inc(a_exp, 1)
            act.wait_ge(steps0, 2)
            nc.scalar.activation(e[:, :, :], e[:, :, :], ACT.Exp, scale=-1.0).then_inc(e_ready, 1)
            act.wait_ge(one_ready, 1)
            nc.scalar.activation(ln[:, :, :], one_e[:, :, :], ACT.Ln).then_inc(ln_ready, 1)
            chain = Chain(act, act_steps, 1)

            def turn_x(q, b):
                act.wait_ge(x_turned, ready(q * 2 + b))
                nc.scalar.copy(banks(xs[b][:, :]), px[:, :, 0:D]).then_inc(x_copied, 1)

            def root(q, b):
                turn = q * 2 + b
                act.wait_ge(var_ready, turn + 1)
                chain.start(turn)
                chain(nc.scalar.activation(lnv[b][:, 1:2], lnv[b][:, 0:1], ACT.Ln, bias=epst[:, :]))
                nc.scalar.activation(rstd[b][:, :], lnv[b][:, 1:2], ACT.Exp, scale=-0.5).then_inc(rstd_ready, 1)

            def decays(q, b, between=None):
                turn = q * 2 + b
                act.wait_ge(sums_ready, turn + 1)
                nc.scalar.copy(gs[b][:, :], psm[:, 0:SMALL]).then_inc(gs_ready, 1)
                act.wait_ge(gs_ready, turn + 2)
                nc.scalar.activation(es[b][:, :], gs[b][:, CUM:SMALL], ACT.Exp).then_inc(es_ready, 1)
                if between:
                    between()
                act.wait_ge(d_ready, ready(turn))
                act.wait_ge(m_ready, turn + CREDIT)
                nc.scalar.activation(ex[:, :, :].rearrange("p (j h) l -> p j (h l)", j=3), pd[:, :, :], ACT.Exp).then_inc(ex_ready, 1)

            def turn_y(q, b):
                turn = q * 2 + b
                act.wait_ge(yt_ready, turn + 1)
                nc.scalar.copy(yts[b][:, :, :].rearrange("p (a j) l -> p a (j l)", a=2), py[:, :, 0:D]).then_inc(yt_copied, 1)

            turn_x(0, 0)
            decays(0, 0)
            turn_x(0, 1)
            root(0, 0)
            decays(0, 1)
            with act.Fori(0, NQ - 1) as q:
                for b in range(IMAGES):
                    turn_x(q + 1, b)
                    decays(q + 1, b, between=lambda: (turn_y(q, b), root(q + b, 1 - b)))
            root(NQ - 1, 1)
            turn_y(NQ - 1, 0)
            turn_y(NQ - 1, 1)

        @block.gpsimd
        def _(pool):
            nc.gpsimd.memset(ones[:, :], 1.0).then_inc(set_up, 1)
            nc.gpsimd.memset(epst[:, :], 1e-5).then_inc(set_up, 1)
            nc.gpsimd.memset(state[0][:, :], 0.0).then_inc(set_up, 1)
            nc.gpsimd.memset(state[1][:, :], 0.0).then_inc(set_up, 1)
            pool.sem_inc(dab_ready, CREDIT)
            pool.wait_ge(set_up, 4)
            pool.wait_ge(loaded, 160)
            pool.wait_ge(prepared, 2)
            with pool.Fori(0, NQ) as q:
                for b in range(IMAGES):
                    turn = q * 2 + b
                    pool.wait_ge(m_ready, free(turn))
                    pool.wait_ge(d_ready, free(turn))
                    settle(pool, pool_held)
                    nc.gpsimd.tensor_tensor(dab[b][:, :], da[:, bass.ds(b * NQ + q, 1), :].rearrange("p a h -> p (a h)"),
                                            ones[:, 0:2 * HEADS], ALU.mult).then_inc(dab_ready, 1)
                    pool.wait_ge(dab_ready, ready(turn))
                    nc.gpsimd.tensor_tensor(r[b][:, :, :],
                                            dab[b][:, HEADS:].rearrange("p (h a) -> p h a", a=1).to_broadcast([P, HEADS, P]),
                                            upto[:, :].rearrange("p (a l) -> p a l", a=1).to_broadcast([P, HEADS, P]),
                                            ALU.mult).then_inc(r_ready, 1)
                    pool.wait_ge(x_copied, turn + 1)
                    nc.gpsimd.tensor_tensor(xd1[b][:, :], xs[b][:, :], d1[:, :], ALU.mult).then_inc(xd_ready, 1)
                    pool.wait_ge(xdt_ready, turn + 1)
                    pool.wait_ge(es_ready, turn + 1)
                    nc.gpsimd.tensor_tensor(by_head(xde[b]), by_head(xdt[b]), heads(es[b][:, HEADS:2 * HEADS]),
                                            ALU.mult).then_inc(xde_ready, 1)

        @block.vector
        def _(dve):
            dve.sem_inc(weighed, 1)
            dve.sem_inc(updated, 1)
            dve.sem_inc(added, CREDIT)
            dve.sem_inc(m_ready, CREDIT)
            nc.vector.memset(ln_one[:, 0:1], 1.0).then_inc(one_set, 1)
            dve.wait_ge(loaded, 160)
            once = Chain(dve, steps0, None)

            def tiles(t):
                return t[:, :].rearrange("p (a h) -> p a h", a=1).to_broadcast([P, NT, HEADS])

            once(nc.vector.tensor_tensor(raw[:, :, :], raw[:, :, :], tiles(dtb), ALU.add))
            once(nc.vector.scalar_tensor_tensor(out=e[:, :, :], in0=raw[:, :, :], scalar=-1.0, in1=raw[:, :, :],
                                                op0=ALU.mult, op1=ALU.max))
            dve.wait_ge(e_ready, 1)
            nc.vector.tensor_scalar(one_e[:, :, :], e[:, :, :], 1.0, None, ALU.add).then_inc(one_ready, 1)
            dve.wait_ge(one_ready, 1)
            once(nc.vector.scalar_tensor_tensor(out=corr[:, :, :], in0=one_e[:, :, :], scalar=1.0, in1=e[:, :, :],
                                                op0=ALU.subtract, op1=ALU.subtract))
            dve.wait_ge(ln_ready, 1)
            once(nc.vector.scalar_tensor_tensor(out=corr[:, :, :], in0=ln[:, :, :], scalar=ln_one[:, 1:2], in1=corr[:, :, :],
                                                op0=ALU.subtract, op1=ALU.subtract))
            nc.vector.scalar_tensor_tensor(out=da[:, :, 0:HEADS], in0=raw[:, :, :], scalar=0.0, in1=corr[:, :, :],
                                           op0=ALU.max, op1=ALU.add).then_inc(prepared, 1)
            dve.wait_ge(prepared, 1)
            dve.wait_ge(a_exp, 1)
            nc.vector.scalar_tensor_tensor(out=da[:, :, HEADS:], in0=da[:, :, 0:HEADS], scalar=-1.0, in1=tiles(alog),
                                           op0=ALU.mult, op1=ALU.mult).then_inc(prepared, 1)
            chain = Chain(dve, steps, 5)
            gate_chain = Chain(dve, gate_steps, 3)

            def weights(q, b):
                turn = q * 2 + b
                dve.wait_ge(x_copied, turn + 1)
                dve.wait_ge(dab_ready, ready(turn))
                nc.vector.tensor_tensor(by_head(xdt[b]), by_head(xs[b]), heads(dab[b][:, 0:HEADS]), ALU.mult).then_inc(xdt_ready, 1)
                dve.wait_ge(gs_ready, turn + 2)
                nc.vector.tensor_tensor(gm[:, :], gs[b][:, 0:P], upto[:, :], ALU.mult).then_inc(gm_ready, 1)
                dve.wait_ge(gm_ready, turn + 1)
                dve.wait_ge(ex_ready, turn + 1)
                nc.vector.tensor_tensor(m[:, :, :], ex[:, :, :],
                                        gm[:, :].rearrange("p (a l) -> p a l", a=1).to_broadcast([P, HEADS, P]),
                                        ALU.mult).then_inc(m_ready, 1)

            def outputs(q, b):
                turn = q * 2 + b
                chain.start(turn)
                yv = banks(y[b][:, :])
                dve.wait_ge(yoff, ready(turn))
                dve.wait_ge(es_ready, turn + 1)
                nc.vector.tensor_tensor(y[b][:, :].rearrange("p (a h c) -> p a h c", a=2, h=HH),
                                        px[:, :, 0:D].rearrange("p a (h c) -> p a h c", h=HH),
                                        es[b][:, 0:HEADS].rearrange("p (a h c) -> p a h c", a=2, c=1).to_broadcast([P, 2, HH, HP]),
                                        ALU.mult).then_inc(weighed, 1)
                chain.mark(nc.vector.tensor_tensor(by_head(state[b]), by_head(state[b]),
                                                   es[b][0:NS, 2 * HEADS:].rearrange("p (h a) -> p h a", a=1).to_broadcast([NS, HEADS, HP]),
                                                   ALU.mult))
                dve.wait_ge(weighed, turn + 2)
                dve.wait_ge(ydiag, turn + 1)
                nc.vector.tensor_tensor(yv, yv, py[:, :, 0:D], ALU.add).then_inc(combined, 1)
                chain.wait()
                dve.wait_ge(ds_ready, turn + 1)
                sv = banks(state[b][:, :])
                nc.vector.tensor_tensor(sv, sv, pd[0:NS, 0:2, 0:D], ALU.add).then_inc(updated, 1)
                dve.wait_ge(xd_ready, turn + 1)
                dve.wait_ge(combined, turn + 1)
                chain(nc.vector.tensor_tensor(y[b][:, :], y[b][:, :], xd1[b][:, :], ALU.add))
                for half in range(2):
                    chain.mark(nc.vector.bn_stats(stats[:, half, :], y[b][:, half * D:(half + 1) * D]))
                chain.wait()
                settle(dve, held)
                chain(nc.vector.bn_aggr(mv[b][:, :], stats[:, :, :]))
                nc.vector.tensor_copy(lnv[b][:, 0:1], mv[b][:, 1:2]).then_inc(var_ready, 1)

            def gate(q, b):
                turn = q * 2 + b
                gate_chain.start(turn)
                dve.wait_ge(rstd_ready, turn + 1)
                gate_chain(nc.vector.tensor_scalar(y[b][:, :], y[b][:, :], mv[b][:, 0:1], rstd[b][:, :], ALU.subtract, ALU.mult))
                gate_chain(nc.vector.tensor_tensor(y[b][:, :], y[b][:, :], gamma[:, :], ALU.mult))
                gate_chain(nc.vector.tensor_tensor(y[b][:, :], y[b][:, :], beta[:, :], ALU.add))
                dve.wait_ge(tok_in[b], q * 32 + 32)
                nc.vector.tensor_tensor(y[b][:, :], y[b][:, :], szt[b][:, :], ALU.mult).then_inc(gated, 1)

            def add(q, b):
                dve.wait_ge(out_ready, q * 2 + b + 1)
                dve.wait_ge(xo_out[b], q * 16 + 16)
                nc.vector.tensor_tensor(xo[b][:, :], py[:, 0, 0:D], xin[b][:, :], ALU.add).then_inc(added, 1)

            weights(0, 0)
            outputs(0, 0)
            weights(0, 1)
            with dve.Fori(0, NQ - 1) as q:
                for b in range(IMAGES):
                    gate(q, b)
                    outputs(q + b, 1 - b)
                    weights(q + 1, b)
                    add(q, b)
            gate(NQ - 1, 0)
            outputs(NQ - 1, 1)
            add(NQ - 1, 0)
            gate(NQ - 1, 1)
            add(NQ - 1, 1)



FT = FF // P
HPAIRS = FT // 2
X_SCALE = 16.0
XBUFS = 6


def kron_ffn(nc, c, w, x, out):
    x_g, out_g = tok_groups(x), tok_groups(out)
    with Stage(nc, "f") as s:
        ident, epst = s.sb("ident", [P, P]), s.sb("eps", [P, 1])
        fc1, pj1 = s.sb("fc1", [3 * KR, FF]), s.sb("pj1", [P, FT, KR])
        ident16, fc1p = s.sb("ident16", [P, P], F16), s.sb("fc1p", [3 * KR, FF], F16)
        fc2, pj2 = s.sb("fc2", [P, KJ]), s.sb("pj2", [P, KJ])
        xin = [s.sb(f"x{u}", [P, GT, D]) for u in range(XBUFS)]
        xo = [s.sb(f"xo{u}", [P, GT, D]) for u in range(2)]
        xn, prod = s.sb("xn", [P, GT, D]), s.sb("prod", [P, GT, D])
        xr = s.sb("xr", [P, GT, KR])
        xp = [s.sb(f"xp{u}", [P, GT, 3, KR], F16) for u in range(2)]
        xpt = [s.sb(f"xpt{u}", [3 * KR, G], F16) for u in range(2)]
        ot = s.sb("ot", [KR, G])
        h = [s.sb(f"h{u}", [P, FT, G]) for u in range(2)]
        o = s.sb("o", [P, GT, KR])
        stats = s.sb("stats", [P, GT, 6])
        mv, std, rstd = ([s.sb(f"{x}{u}", shape) for u in range(2)] for x, shape in (
            ("mv", [P, GT, 2]), ("std", [P, 2, GT]), ("rstd", [P, GT])))
        pt, pot, po = s.ps("pt", [3 * KR, 2 * BANK], F16), s.ps("pot", [KR, BANK]), s.ps("po", [P, BANK])
        ph = [s.ps(f"ph{v}", [P, 2, BANK]) for v in range(2)]
        x_in, x_out = ([s.sem(f"{x}{u}") for u in range(XBUFS)] for x in ("x_in", "x_out"))
        (loaded, eps_set, var_ready, std_ready, steps, osteps, reduced, turned, copied, h_ready, gelu, o_ready, o_taken, added, held, split,
         ot_ready, ot_copied, pe_held, stat_steps) = (
            s.sem(x) for x in "loaded eps_set var_ready std_ready steps osteps reduced turned copied h_ready gelu o_ready "
            "o_taken added held split ot_ready ot_copied pe_held stat_steps".split())
        block = s.block()

        @block.sync
        def _(sp):
            for u in range(XBUFS):
                sp.sem_inc(x_out[u], 16)
            for tile, src in ((ident[:, :], c["ident"]), (fc1[:, :], w["fc1"]), (pj1[:, :, :], w["pj1"]), (fc2[:, :], w["fc2"]),
                              (pj2[:, :], w["pj2"])):
                sp.dma_start(tile, src).then_inc(loaded, 16)
            for u in range(XBUFS):
                sp.dma_start(xin[u][:, :, :], x_g[u]).then_inc(x_in[u], 16)
            with sp.Fori(0, NG // XBUFS - 1) as i:
                for u in range(XBUFS):
                    g = i * XBUFS + u
                    sp.wait_ge(added, g + 1)
                    sp.dma_start(out_g[g], xo[u % 2][:, :, :]).then_inc(x_out[u], 16)
                    sp.dma_start(xin[u][:, :, :], x_g[g + XBUFS]).then_inc(x_in[u], 16)
            for u in range(XBUFS):
                sp.wait_ge(added, NG - XBUFS + u + 1)
                sp.dma_start(out_g[NG - XBUFS + u], xo[u % 2][:, :, :]).then_inc(x_out[u], 16)
            for u in range(XBUFS):
                sp.wait_ge(x_out[u], 16 * (NG // XBUFS + 1))

        @block.vector
        def _(dve):
            nc.vector.memset(epst[:, :], 1e-5).then_inc(eps_set, 1)
            dve.sem_inc(o_taken, 1)
            dve.wait_ge(loaded, 80)
            nc.vector.tensor_copy(ident16[:, :], ident[:, :]).then_inc(split, 1)
            nc.vector.tensor_scalar(fc1[:, :], fc1[:, :], W_SCALE, None, ALU.mult).then_inc(split, 1)
            dve.wait_ge(split, 2)
            nc.vector.tensor_copy(fc1p[:, :], fc1[:, :]).then_inc(split, 1)
            dve.wait_ge(split, 3)
            low = slice(KR, 2 * KR)
            nc.vector.tensor_tensor(fc1p[low, :], fc1[low, :], fc1p[low, :], ALU.subtract).then_inc(split, 1)
            stat_chain, chain = Chain(dve, stat_steps, 2 * GT), Chain(dve, steps, 6)
            ochain = Chain(dve, osteps, 1)

            def statistics(g, i, x, u):
                stat_chain.start(g)
                dve.wait_ge(x_in[x], i * 16 + 16)
                for t in range(GT):
                    stat_chain.mark(nc.vector.bn_stats(stats[:, t, :], xin[x][:, t, :]))
                stat_chain.wait()
                settle(dve, held)
                for t in range(GT):
                    stat_chain.mark(nc.vector.bn_aggr(mv[u][:, t, :], stats[:, t, :]))
                stat_chain.wait()
                nc.vector.tensor_copy(std[u][:, 0, :], mv[u][:, :, 1]).then_inc(var_ready, 1)

            def reduce(g, x, u):
                chain.start(g)
                dve.wait_ge(std_ready, g + 1)
                chain(nc.vector.reciprocal(rstd[u][:, :], std[u][:, 1, :]))
                for t in range(GT):
                    ins = nc.vector.tensor_scalar(xn[:, t, :], xin[x][:, t, :], mv[u][:, t, 0:1], rstd[u][:, t:t + 1],
                                                  ALU.subtract, ALU.mult)
                chain(ins)
                chain(nc.vector.tensor_tensor(prod[:, :, :].rearrange("p t (i j) -> p (t i) j", j=KJ),
                                              xn[:, :, :].rearrange("p t (i j) -> p (t i) j", j=KJ),
                                              fc2[:, :].rearrange("p (a j) -> p a j", a=1).to_broadcast([P, GT * KR, KJ]), ALU.mult))
                chain(nc.vector.tensor_reduce(xr[:, :, :].rearrange("p t i -> p (t i)"),
                                              prod[:, :, :].rearrange("p t (i j) -> p (t i) j", j=KJ), AX.X, ALU.add))
                chain(nc.vector.tensor_scalar(xr[:, :, :], xr[:, :, :], X_SCALE, None, ALU.mult))
                dve.wait_ge(turned, free(g))
                for part in range(2):
                    ins = nc.vector.tensor_copy(xp[u][:, :, part, :], xr[:, :, :])
                chain(ins)
                nc.vector.tensor_tensor(xp[u][:, :, 2, :], xr[:, :, :], xp[u][:, :, 0, :], ALU.subtract).then_inc(reduced, 1)

            def spread(g, i, x, u):
                ochain.start(g)
                dve.wait_ge(o_ready, g + 1)
                nc.vector.tensor_copy(o[:, :, :].rearrange("p t i -> p (t i)"), po[:, 0:GT * KR]).then_inc(o_taken, 1)
                dve.wait_ge(o_taken, g + 2)
                dve.wait_ge(x_out[(x - 2) % XBUFS], i * 16 + (32 if x >= 2 else 16))
                view = xo[u][:, :, :].rearrange("p t (i j) -> p (t i) j", j=KJ)
                ochain(nc.vector.tensor_tensor(view,
                                               o[:, :, :].rearrange("p t (i a) -> p (t i) a", a=1).to_broadcast([P, GT * KR, KJ]),
                                               pj2[:, :].rearrange("p (a j) -> p a j", a=1).to_broadcast([P, GT * KR, KJ]), ALU.mult))
                nc.vector.tensor_tensor(xo[u][:, :, :], xo[u][:, :, :], xin[x][:, :, :], ALU.add).then_inc(added, 1)

            def step(i, x):
                g = i * XBUFS + x
                if not isinstance(i, int) or g + 3 < NG:
                    statistics(g + 3, i + (x + 3) // XBUFS, (x + 3) % XBUFS, (x + 3) % 2)
                if not isinstance(i, int) or g + 2 < NG:
                    reduce(g + 2, (x + 2) % XBUFS, x % 2)
                spread(g, i, x, x % 2)

            statistics(0, 0, 0, 0)
            statistics(1, 0, 1, 1)
            reduce(0, 0, 0)
            statistics(2, 0, 2, 0)
            reduce(1, 1, 1)
            with dve.Fori(0, NG // XBUFS - 1) as i:
                for x in range(XBUFS):
                    step(i, x)
            for x in range(XBUFS):
                step(NG // XBUFS - 1, x)

        @block.tensor
        def _(pe):
            pe.sem_inc(turned, CREDIT)
            pe.wait_ge(loaded, 80)
            pe.wait_ge(split, 4)

            def hidden(g, u, between=None):
                pe.wait_ge(reduced, g + 1)
                for t in range(GT):
                    ins = nc.tensor.transpose(pt[:, t * P:(t + 1) * P], xp[u][:, t, :, :].rearrange("p a i -> p (a i)"), ident16[:, :])
                ins.then_inc(turned, 1)
                pe.wait_ge(copied, g + 1)
                for jj in range(HPAIRS):
                    pe.wait_ge(gelu, g * HPAIRS + jj + 1)
                    for j in range(2):
                        at = (2 * jj + j) * P
                        ins = nc.tensor.matmul(ph[jj % 2][:, j, 0:G], fc1p[:, at:at + P], xpt[u][:, :], start=True, stop=True)
                    ins.then_inc(h_ready, 1)
                    if between:
                        between(jj)

            def outputs(g, u, jj):
                if jj == 0:
                    pe.wait_ge(gelu, g * HPAIRS + HPAIRS + CREDIT)
                    pe.wait_ge(o_taken, g + 1)
                for j in (2 * jj, 2 * jj + 1):
                    ins = nc.tensor.matmul(pot[:, 0:G], pj1[:, j, :], h[u][:, j, :], start=j == 0, stop=j == FT - 1)
                if jj == HPAIRS - 1:
                    ins.then_inc(ot_ready, 1)

            def turn_o(g):
                pe.wait_ge(ot_copied, g + 1)
                settle(pe, pe_held)
                for t in range(GT):
                    ins = nc.tensor.transpose(po[:, t * KR:(t + 1) * KR], ot[:, t * P:(t + 1) * P], ident[0:KR, 0:KR])
                ins.then_inc(o_ready, 1)

            hidden(0, 0)
            with pe.Fori(0, NG // 2 - 1) as i:
                for u in range(2):
                    g = i * 2 + u
                    hidden(g + 1, 1 - u, lambda jj: outputs(g, u, jj))
                    turn_o(g)
            hidden(NG - 1, 1, lambda jj: outputs(NG - 2, 0, jj))
            turn_o(NG - 2)
            for jj in range(HPAIRS):
                outputs(NG - 1, 1, jj)
            turn_o(NG - 1)

        @block.scalar
        def _(act):
            act.sem_inc(gelu, CREDIT)
            act.wait_ge(eps_set, 1)

            def root(g, u):
                act.wait_ge(var_ready, g + 1)
                nc.scalar.activation(std[u][:, 1, :], std[u][:, 0, :], ACT.Sqrt, bias=epst[:, :]).then_inc(std_ready, 1)

            def gelus(g, u):
                for jj in range(HPAIRS):
                    act.wait_ge(h_ready, g * HPAIRS + jj + 1)
                    nc.scalar.activation(h[u][:, 2 * jj:2 * jj + 2, :], ph[jj % 2][:, :, 0:G], ACT.Gelu, scale=1.0 / (W_SCALE * X_SCALE)).then_inc(gelu, 1)

            def turn(g, u):
                act.wait_ge(turned, g + 1 + CREDIT)
                nc.scalar.copy(xpt[u][:, :], pt[:, 0:G]).then_inc(copied, 1)

            def turn_o(g):
                act.wait_ge(ot_ready, g + 1)
                nc.scalar.copy(ot[:, :], pot[:, 0:G]).then_inc(ot_copied, 1)

            def step(g, u):
                gelus(g + 1, 1 - u)
                turn_o(g)
                if not isinstance(g, int) or g + 2 < NG:
                    turn(g + 2, u)
                if not isinstance(g, int) or g + 3 < NG:
                    root(g + 3, 1 - u)

            for g in range(3):
                root(g, g % 2)
            turn(0, 0)
            gelus(0, 0)
            turn(1, 1)
            with act.Fori(0, NG // 2 - 2) as i:
                for u in range(2):
                    step(i * 2 + u, u)
            for g in range(NG - 4, NG - 1):
                step(g, g % 2)
            turn_o(NG - 1)


def program(nc, c, w, out):
    def dram(name, *shape):
        return nc.dram_tensor(name, list(shape), F32).ap()

    x = w["x"].rearrange("b h w d -> (b h w) d")
    y = dram("y", SLOTS, P, T)
    ss2d(nc, c, w, x, y)
    x2 = dram("x2", T, D)
    with Stage(nc, "l0") as s:
        x1, th, tl, scores = s.sb("x1", [P, NT, D]), s.sb("th", [P, DC, T], F16), s.sb("tl", [P, DC, T], F16), s.sb("scores", [P, NT, EX])
        ss2d_out(nc, c, w, y, x, x1, th, tl, scores)
        moe(nc, c, w, x1, th, tl, scores, x2)
    sz, dt_raw, xbc, x3 = dram("sz", T, DIN), dram("dt_raw", P, NT, HEADS), dram("xbc", CT, P, T), dram("x3", T, D)
    with Stage(nc, "l1") as s:
        xn = s.sb("xn", [P, DC, T])
        mamba_gate(nc, c, w, x2, xn, sz, dt_raw)
        mamba_conv(nc, w, xn, xbc)
    mamba_scan(nc, c, w, x2, sz, dt_raw, xbc, x3)
    kron_ffn(nc, c, w, x3, out.rearrange("b h w d -> (b h w) d"))


def constants(np, bf16):
    i = np.arange(P)
    sel = np.zeros((BROWS, 3, BC, P), bf16)
    for p in range(BROWS):
        sel[p, 0, p % BC] = 1
        sel[p, 1, p % BC, :REST] = 1
        sel[p, 2, p % BC, REST:] = 1
    return dict(ident=np.eye(P, dtype=np.float32), mean768=np.full((P, P), 1.0 / CI, np.float32),
                upto=(i[:, None] <= i[None]).astype(np.float32), beyond=(i[:, None] > i[None]).astype(np.float32), sel=sel)


def layouts(np, I):
    def zeros(*shape):
        return np.zeros(shape, np.float32)

    def rows(a):
        return a.reshape((-1, P) + a.shape[1:]).swapaxes(0, 1)

    def spread(a):
        return np.broadcast_to(a.reshape(1, -1), (P, a.size))

    w = dict(x=I["x"])
    proj = I["L0_conv_in_proj_w"].reshape(KD, DI, DC, P).transpose(0, 3, 2, 1)
    w["in_proj"] = zeros(KD, P, 3, DC, P)
    w["in_proj"][:, :, 0] = proj[..., :P]
    w["in_proj"][:, :, 1, :, :REST] = proj[..., P:]
    w["in_proj"][:, :, 2, :, REST:] = proj[..., P:]

    def tiles(a):
        a = a.reshape((KD, DI) + a.shape[1:] if a.shape[0] == CI else a.shape)
        r = zeros(KD, P, 3, *a.shape[2:])
        r[:, :, 0], r[:, :, 1] = a[:, :P], a[:, :P]
        r[:, :REST, 2], r[:, REST:, 2] = a[:, P:], a[:, P:]
        return r

    w["conv"] = tiles(I["L0_conv_conv_w"].reshape(KD, DI, 9))
    w["conv_b"], w["ds"] = tiles(I["L0_conv_conv_b"]), tiles(I["L0_conv_Ds"])
    w["a_logs"], w["dt_b"] = tiles(I["L0_conv_A_logs"]), tiles(I["L0_conv_dt_projs_bias"])
    xp = I["L0_conv_x_proj_weight"]
    xp = np.concatenate([xp[:, RANK:]] * PARTS + [xp[:, :RANK]], 1).transpose(0, 2, 1)
    w["x_proj"] = zeros(KD, P, 3, XROWS)
    w["x_proj"][:, :, 0], w["x_proj"][:, :REST, 1], w["x_proj"][:, REST:, 2] = xp[:, :P], xp[:, P:], xp[:, P:]
    dp = I["L0_conv_dt_projs_weight"].transpose(0, 2, 1)
    w["dt_proj"] = zeros(KD, XROWS, 3, P)
    w["dt_proj"][:, BROWS:, 0] = dp[:, :, :P]
    w["dt_proj"][:, BROWS:, 1, :REST], w["dt_proj"][:, BROWS:, 2, REST:] = dp[:, :, P:], dp[:, :, P:]

    def slots(a):
        a = a.reshape((KD, DI) + a.shape[1:])
        r = zeros(P, SLOTS, *a.shape[2:])
        for k in range(KD):
            r[:, k] = a[k, :P]
            r[k % 2 * REST:k % 2 * REST + REST, KD + k // 2] = a[k, P:]
        return r

    w["out_proj"] = slots(I["L0_conv_out_proj_w"].T)
    w["out_nw"], w["out_nb"] = slots(I["L0_conv_out_norm_w"]), slots(I["L0_conv_out_norm_b"])
    w["gate_w"], w["gate_b"] = rows(I["L0_ffn_gate_w"]), I["L0_ffn_gate_b"].reshape(1, EX)
    w["w1"] = I["L0_ffn_w1"].reshape(EX, DC, P, 2, HALF).transpose(0, 3, 2, 1, 4)
    w["w2"] = I["L0_ffn_w2"].reshape(EX, 2, HT, P, D).transpose(0, 1, 3, 2, 4)
    w["b1"] = I["L0_ffn_b1"].reshape(EX, HID // P, P).transpose(2, 0, 1).reshape(P, -1)
    w["b2"] = I["L0_ffn_b2"].reshape(1, -1)
    win = I["L1_conv_W_in"]
    w["w_z"] = rows(np.concatenate([win[:, :DIN], win[:, DIN + CONV:]], 1))
    xbc, conv = zeros(D, CT * P), zeros(CT * P, 10)
    xbc[:, :CONV] = win[:, DIN:DIN + CONV]
    w["w_x"] = xbc.reshape(DC, P, CT, P).transpose(2, 1, 0, 3)
    conv[:CONV, :9], conv[:CONV, 9] = I["L1_conv_W_conv"].reshape(9, CONV).T, I["L1_conv_b_conv"]
    conv = rows(conv)
    w["conv1"], w["conv1_b"] = conv[:, :, :9], conv[:, :, 9]
    w["dt1_b"], w["a1_log"] = spread(I["L1_conv_dt_bias"]), spread(I["L1_conv_A_log"])
    w["d1"] = spread(np.repeat(I["L1_conv_D_param"], HP))
    w["gamma"], w["beta"], w["w_out1"] = spread(I["L1_conv_gamma"]), spread(I["L1_conv_beta"]), rows(I["L1_conv_W_out"])
    w["fc1"], w["fc2"] = np.tile(I["L1_ffn_c_fc_1"].T, (3, 1)), spread(I["L1_ffn_c_fc_2"])
    w["pj1"], w["pj2"] = rows(I["L1_ffn_c_proj_1"].T), spread(I["L1_ffn_c_proj_2"])
    return w


def kernel(**inputs):
    import numpy as np
    import concourse.bacc as bacc
    from concourse.bass_utils import run_bass_kernel_spmd

    nc = bacc.Bacc("TRN2", target_bir_lowering=False, num_devices=1)
    arrays, c, w = {}, {}, {}
    for into, source in ((c, constants(np, mybir.dt.np(BF16))), (w, layouts(np, {k: np.asarray(v) for k, v in inputs.items()}))):
        for name, a in source.items():
            a = np.ascontiguousarray(a)
            arrays[f"in_{name}"] = a
            into[name] = nc.dram_tensor(f"in_{name}", a.shape, mybir.dt.from_np(a.dtype), kind="ExternalInput").ap()
    out = nc.dram_tensor("out", [IMAGES, SIDE, SIDE, D], F32, kind="ExternalOutput").ap()
    program(nc, c, w, out)
    return run_bass_kernel_spmd(nc, [arrays], core_ids=[0]).results[0]["out"]
```
